# Optimizing a Trainium2 kernel written in Bass

```python
import numpy as np
import jax
import jax.numpy as jnp

def _softmax(x, axis=-1):
    return jax.nn.softmax(x, axis=axis)

def _gelu(x):
    return jax.nn.gelu(x, approximate=True)

def _silu(x):
    return jax.nn.silu(x)

def _sigmoid(x):
    return jax.nn.sigmoid(x)

def _layernorm(x, axis=-1, eps=1e-05):
    m = jnp.mean(x, axis=axis, keepdims=True)
    v = jnp.var(x, axis=axis, keepdims=True)
    return (x - m) / jnp.sqrt(v + eps)

def _scatter_add(tgt, idx, src, axis=0):
    return tgt.at[idx].add(src)

def _segment_sum(src, seg, n):
    return jax.ops.segment_sum(src, seg, n)
kernel_name = 'mk_perceiver_d2_seqx_r4_5e7d02'

def setup_inputs(seed: int=0):
    np.random.seed(seed)
    _w = jnp.asarray

    def _rec_inputs():
        import jax
        import jax.numpy as jnp
        _rk = jax.random.key(seed)
        x = 7.22e-05 + 1 * jax.random.normal(jax.random.fold_in(_rk, 1), (2, 256, 256), jnp.float32)
        _lenS = 256 - jax.random.randint(jax.random.fold_in(_rk, 7), (2,), 0, max(1, 256 // 4) + 1, jnp.int32)
        _lenS2 = 4096 - jax.random.randint(jax.random.fold_in(_rk, 8), (2,), 0, max(1, 4096 // 4) + 1, jnp.int32)
        _ctx_1024P = jax.random.normal(jax.random.fold_in(_rk, 11), (2, 16, 256), jnp.float32)
        _ctx_1024c = jax.random.dirichlet(jax.random.fold_in(_rk, 511), 0.3 * jnp.ones((16,), jnp.float32), (2, 4096))
        _ctx_1024t = jnp.einsum('bsk,bkd->bsd', _ctx_1024c, _ctx_1024P)
        _ctx_1024t = _ctx_1024t * jax.lax.rsqrt(jnp.mean(jnp.square(_ctx_1024t)) + 1e-12) * 0.953939
        ctx_1024 = 4.13588e-05 + 0.999923 * (_ctx_1024t + 0.3 * jax.random.normal(jax.random.fold_in(_rk, 611), (2, 4096, 256), jnp.float32))
        _validS = jnp.arange(256)[None, :] < _lenS[:, None]
        _validS2 = jnp.arange(4096)[None, :] < _lenS2[:, None]
        _causal = jnp.tril(jnp.ones((256, 256), dtype=bool))
        mask_BxSxS2_ik1 = jnp.where(jnp.broadcast_to(_validS2[:, None, :], (2, 256, 4096)), 1, 0).astype(jnp.int32)
        return (x, ctx_1024, mask_BxSxS2_ik1)
    x, ctx_1024, mask_BxSxS2_ik1 = _rec_inputs()

    def _L0_xattn_setup():
        import jax, jax.numpy as jnp
        import numpy as np
        N_HEADS = 16
        D_MODEL = 256
        D_K = D_MODEL // N_HEADS
        B, S = (4, 512)
        NEG_INF = -1000000000.0

        def _proj(x, W, b):
            y = jnp.einsum('bsd,ed->bse', x, W) + b
            Bx, Sx, _ = y.shape
            return y.reshape(Bx, Sx, N_HEADS, D_K).transpose(0, 2, 1, 3)
        key = jax.random.key(seed)
        ks = jax.random.split(key, 12)
        scale = 1.0 / np.sqrt(D_MODEL)
        inp = {'query': jax.random.normal(ks[0], (B, S, D_MODEL), jnp.float32), 'key': jax.random.normal(ks[1], (B, S, D_MODEL), jnp.float32), 'value': jax.random.normal(ks[2], (B, S, D_MODEL), jnp.float32), 'mask': jax.random.randint(ks[3], (B, S, S), 0, 2, jnp.int32), 'Wq': jax.random.normal(ks[4], (D_MODEL, D_MODEL), jnp.float32) * scale, 'bq': jnp.zeros((D_MODEL,), jnp.float32), 'Wk': jax.random.normal(ks[5], (D_MODEL, D_MODEL), jnp.float32) * scale, 'bk': jnp.zeros((D_MODEL,), jnp.float32), 'Wv': jax.random.normal(ks[6], (D_MODEL, D_MODEL), jnp.float32) * scale, 'bv': jnp.zeros((D_MODEL,), jnp.float32), 'Wo': jax.random.normal(ks[7], (D_MODEL, D_MODEL), jnp.float32) * scale, 'bo': jnp.zeros((D_MODEL,), jnp.float32)}
        return inp
    _L0_xattn_all = _L0_xattn_setup()
    _L0_xattn_in = {k: v for k, v in _L0_xattn_all.items() if k in ('Wq', 'bq', 'Wk', 'bk', 'Wv', 'bv', 'Wo', 'bo')}
    del _L0_xattn_all

    def _L0_attn_setup():
        import jax, jax.numpy as jnp
        import numpy as np
        LN_EPS = 1e-05
        key = jax.random.key(seed)
        ks = jax.random.split(key, 7)
        B, L, D, N = (8, 512, 256, 16)
        x = jax.random.normal(ks[0], (B, L, D), jnp.float32)
        A = jax.random.normal(ks[1], (D, N, N), jnp.float32) * (0.2 / np.sqrt(N))
        Bp = jax.random.normal(ks[2], (D, N), jnp.float32)
        Cp = jax.random.normal(ks[3], (D, N), jnp.float32)
        Dp = jax.random.normal(ks[4], (D,), jnp.float32)
        Wg = jax.random.normal(ks[5], (D, D), jnp.float32) / np.sqrt(D)
        bg = jnp.zeros((D,), jnp.float32)
        gamma = jnp.ones((D,), jnp.float32)
        beta = jnp.zeros((D,), jnp.float32)
        return dict(x=x, A=A, Bp=Bp, Cp=Cp, Dp=Dp, Wg=Wg, bg=bg, gamma=gamma, beta=beta)
    _L0_attn_all = _L0_attn_setup()
    _L0_attn_in = {k: v for k, v in _L0_attn_all.items() if k in ('A', 'Bp', 'Cp', 'Dp', 'Wg', 'bg', 'gamma', 'beta')}
    del _L0_attn_all

    def _L0_ffn_setup():
        import jax, jax.numpy as jnp
        import numpy as np
        B, S, D, O, E, K = (4, 512, 256, 256, 8, 2)
        key = jax.random.key(seed)
        ks = jax.random.split(key, 5)
        scale_in = 1.0 / np.sqrt(D)
        x = jax.random.normal(ks[0], (B, S, D), dtype=jnp.float32)
        gate_w = jax.random.uniform(ks[1], (E, D), jnp.float32, -scale_in, scale_in)
        gate_b = jax.random.uniform(ks[2], (E,), jnp.float32, -scale_in, scale_in)
        expert_w = jax.random.uniform(ks[3], (E, D, O), jnp.float32, -scale_in, scale_in)
        expert_b = jax.random.uniform(ks[4], (E, O), jnp.float32, -scale_in, scale_in)
        return {'x': x, 'gate_w': gate_w, 'gate_b': gate_b, 'expert_w': expert_w, 'expert_b': expert_b}
    _L0_ffn_all = _L0_ffn_setup()
    _L0_ffn_in = {k: v for k, v in _L0_ffn_all.items() if k in ('gate_w', 'gate_b', 'expert_w', 'expert_b')}
    del _L0_ffn_all

    def _L1_xattn_setup():
        import jax, jax.numpy as jnp
        import numpy as np
        DIM = 256
        DIM_HEAD = 64
        HEADS = 16
        INNER = DIM_HEAD * HEADS
        EPS = 1e-05

        def layer_norm(x, g, b):
            m = jnp.mean(x, axis=-1, keepdims=True)
            v = jnp.mean(jnp.square(x - m), axis=-1, keepdims=True)
            return (x - m) * jax.lax.rsqrt(v + EPS) * g + b
        key = jax.random.key(seed)
        ks = jax.random.split(key, 8)
        B, N_IMG, N_LAT = (4, 1024, 128)
        std = 1.0 / np.sqrt(DIM)
        return {'image_embeds': jax.random.normal(ks[0], (B, N_IMG, DIM), dtype=jnp.float32), 'latents': jax.random.normal(ks[1], (B, N_LAT, DIM), dtype=jnp.float32), 'ln1_g': jnp.ones((DIM,), jnp.float32), 'ln1_b': jnp.zeros((DIM,), jnp.float32), 'ln2_g': jnp.ones((DIM,), jnp.float32), 'ln2_b': jnp.zeros((DIM,), jnp.float32), 'Wq': jax.random.normal(ks[2], (DIM, INNER), dtype=jnp.float32) * std, 'Wkv': jax.random.normal(ks[3], (DIM, 2 * INNER), dtype=jnp.float32) * std, 'Wo': jax.random.normal(ks[4], (INNER, DIM), dtype=jnp.float32) * std}
    _L1_xattn_all = _L1_xattn_setup()
    _L1_xattn_in = {k: v for k, v in _L1_xattn_all.items() if k in ('ln1_g', 'ln1_b', 'ln2_g', 'ln2_b', 'Wq', 'Wkv', 'Wo')}
    del _L1_xattn_all

    def _L1_attn_setup():
        import jax, jax.numpy as jnp
        import numpy as np
        D_MODEL = 256
        N_HEADS = 16
        N_GROUPS = 4
        CONTEXT_LEN = 128
        D_H = D_MODEL // N_HEADS
        GROUP_SIZE = N_HEADS // N_GROUPS
        B, S = (4, 512)
        key = jax.random.key(seed)
        ks = jax.random.split(key, 9)
        s = 0.02
        return {'x': jax.random.normal(ks[0], (B, S, D_MODEL), dtype=jnp.float32), 'Wq': jax.random.normal(ks[1], (D_MODEL, D_MODEL), dtype=jnp.float32) * s, 'bq': jax.random.normal(ks[2], (D_MODEL,), dtype=jnp.float32) * s, 'Wk': jax.random.normal(ks[3], (D_MODEL, N_GROUPS * D_H), dtype=jnp.float32) * s, 'bk': jax.random.normal(ks[4], (N_GROUPS * D_H,), dtype=jnp.float32) * s, 'Wv': jax.random.normal(ks[5], (D_MODEL, N_GROUPS * D_H), dtype=jnp.float32) * s, 'bv': jax.random.normal(ks[6], (N_GROUPS * D_H,), dtype=jnp.float32) * s, 'Wo': jax.random.normal(ks[7], (D_MODEL, D_MODEL), dtype=jnp.float32) * s, 'bo': jax.random.normal(ks[8], (D_MODEL,), dtype=jnp.float32) * s}
    _L1_attn_all = _L1_attn_setup()
    _L1_attn_in = {k: v for k, v in _L1_attn_all.items() if k in ('Wq', 'bq', 'Wk', 'bk', 'Wv', 'bv', 'Wo', 'bo')}
    del _L1_attn_all

    def _L1_ffn_setup():
        import jax, jax.numpy as jnp
        import numpy as np
        H = 256
        I = 256
        E = 8
        key = jax.random.key(seed)
        ks = jax.random.split(key, 8)
        s = 0.02
        x = jax.random.normal(ks[0], (4, 512, H), dtype=jnp.float32)
        Wg = jax.random.normal(ks[1], (H, E), dtype=jnp.float32) * s
        bg = jnp.zeros((E,), dtype=jnp.float32)
        W1 = jax.random.normal(ks[2], (E, H, I), dtype=jnp.float32) * s
        b1 = jnp.zeros((E, I), dtype=jnp.float32)
        W2 = jax.random.normal(ks[3], (E, I, H), dtype=jnp.float32) * s
        b2 = jnp.zeros((E, H), dtype=jnp.float32)
        return {'x': x, 'Wg': Wg, 'bg': bg, 'W1': W1, 'b1': b1, 'W2': W2, 'b2': b2}
    _L1_ffn_all = _L1_ffn_setup()
    _L1_ffn_in = {k: v for k, v in _L1_ffn_all.items() if k in ('Wg', 'bg', 'W1', 'b1', 'W2', 'b2')}
    del _L1_ffn_all
    return {'x': x, 'ctx_1024': ctx_1024, 'mask_BxSxS2_ik1': mask_BxSxS2_ik1, 'L0_xattn_Wq': _L0_xattn_in['Wq'], 'L0_xattn_bq': _L0_xattn_in['bq'], 'L0_xattn_Wk': _L0_xattn_in['Wk'], 'L0_xattn_bk': _L0_xattn_in['bk'], 'L0_xattn_Wv': _L0_xattn_in['Wv'], 'L0_xattn_bv': _L0_xattn_in['bv'], 'L0_xattn_Wo': _L0_xattn_in['Wo'], 'L0_xattn_bo': _L0_xattn_in['bo'], 'L0_attn_A': _L0_attn_in['A'], 'L0_attn_Bp': _L0_attn_in['Bp'], 'L0_attn_Cp': _L0_attn_in['Cp'], 'L0_attn_Dp': _L0_attn_in['Dp'], 'L0_attn_Wg': _L0_attn_in['Wg'], 'L0_attn_bg': _L0_attn_in['bg'], 'L0_attn_gamma': _L0_attn_in['gamma'], 'L0_attn_beta': _L0_attn_in['beta'], 'L0_ffn_gate_w': _L0_ffn_in['gate_w'], 'L0_ffn_gate_b': _L0_ffn_in['gate_b'], 'L0_ffn_expert_w': _L0_ffn_in['expert_w'], 'L0_ffn_expert_b': _L0_ffn_in['expert_b'], 'L1_xattn_ln1_g': _L1_xattn_in['ln1_g'], 'L1_xattn_ln1_b': _L1_xattn_in['ln1_b'], 'L1_xattn_ln2_g': _L1_xattn_in['ln2_g'], 'L1_xattn_ln2_b': _L1_xattn_in['ln2_b'], 'L1_xattn_Wq': _L1_xattn_in['Wq'], 'L1_xattn_Wkv': _L1_xattn_in['Wkv'], 'L1_xattn_Wo': _L1_xattn_in['Wo'], 'L1_attn_Wq': _L1_attn_in['Wq'], 'L1_attn_bq': _L1_attn_in['bq'], 'L1_attn_Wk': _L1_attn_in['Wk'], 'L1_attn_bk': _L1_attn_in['bk'], 'L1_attn_Wv': _L1_attn_in['Wv'], 'L1_attn_bv': _L1_attn_in['bv'], 'L1_attn_Wo': _L1_attn_in['Wo'], 'L1_attn_bo': _L1_attn_in['bo'], 'L1_ffn_Wg': _L1_ffn_in['Wg'], 'L1_ffn_bg': _L1_ffn_in['bg'], 'L1_ffn_W1': _L1_ffn_in['W1'], 'L1_ffn_b1': _L1_ffn_in['b1'], 'L1_ffn_W2': _L1_ffn_in['W2'], 'L1_ffn_b2': _L1_ffn_in['b2']}

def reference(x, ctx_1024, mask_BxSxS2_ik1, L0_xattn_Wq, L0_xattn_bq, L0_xattn_Wk, L0_xattn_bk, L0_xattn_Wv, L0_xattn_bv, L0_xattn_Wo, L0_xattn_bo, L0_attn_A, L0_attn_Bp, L0_attn_Cp, L0_attn_Dp, L0_attn_Wg, L0_attn_bg, L0_attn_gamma, L0_attn_beta, L0_ffn_gate_w, L0_ffn_gate_b, L0_ffn_expert_w, L0_ffn_expert_b, L1_xattn_ln1_g, L1_xattn_ln1_b, L1_xattn_ln2_g, L1_xattn_ln2_b, L1_xattn_Wq, L1_xattn_Wkv, L1_xattn_Wo, L1_attn_Wq, L1_attn_bq, L1_attn_Wk, L1_attn_bk, L1_attn_Wv, L1_attn_bv, L1_attn_Wo, L1_attn_bo, L1_ffn_Wg, L1_ffn_bg, L1_ffn_W1, L1_ffn_b1, L1_ffn_W2, L1_ffn_b2):
    import jax
    import jax.numpy as jnp

    def _L0_xattn_ref(query, key, value, mask, Wq, bq, Wk, bk, Wv, bv, Wo, bo):
        import jax, jax.numpy as jnp
        import numpy as np
        N_HEADS = 16
        D_MODEL = 256
        D_K = D_MODEL // N_HEADS
        B, S = (4, 512)
        NEG_INF = -1000000000.0

        def _proj(x, W, b):
            y = jnp.einsum('bsd,ed->bse', x, W) + b
            Bx, Sx, _ = y.shape
            return y.reshape(Bx, Sx, N_HEADS, D_K).transpose(0, 2, 1, 3)
        q = _proj(query, Wq, bq)
        k = _proj(key, Wk, bk)
        v = _proj(value, Wv, bv)
        scores = jnp.einsum('bhqd,bhkd->bhqk', q, k) / jnp.sqrt(jnp.float32(D_K))
        m = mask[:, None, :, :]
        scores = jnp.where(m == 0, jnp.float32(NEG_INF), scores)
        p_attn = jax.nn.softmax(scores, axis=-1)
        x = jnp.einsum('bhqk,bhkd->bhqd', p_attn, v)
        x = x.transpose(0, 2, 1, 3).reshape(query.shape[0], -1, D_MODEL)
        return jnp.einsum('bsd,ed->bse', x, Wo) + bo

    def _L0_attn_ref(x, A, Bp, Cp, Dp, Wg, bg, gamma, beta):
        import jax, jax.numpy as jnp
        import numpy as np
        LN_EPS = 1e-05
        gate = jax.nn.sigmoid(jnp.einsum('bld,ed->ble', x, Wg) + bg)
        xg = x * gate
        Bsz, L, D = xg.shape
        N = A.shape[-1]

        def step(s, xt):
            s = jnp.einsum('bdn,dnm->bdm', s, A) + xt[..., None] * Bp
            y = jnp.einsum('bdn,dn->bd', s, Cp) + Dp * xt
            return (s, y)
        s0 = jnp.zeros((Bsz, D, N), xg.dtype)
        _, ys = jax.lax.scan(step, s0, jnp.moveaxis(xg, 1, 0))
        y = jnp.moveaxis(ys, 0, 1) + xg
        mu = jnp.mean(y, axis=-1, keepdims=True)
        var = jnp.var(y, axis=-1, keepdims=True)
        return (y - mu) * jax.lax.rsqrt(var + LN_EPS) * gamma + beta

    def _L0_ffn_ref(x, gate_w, gate_b, expert_w, expert_b):
        import jax, jax.numpy as jnp
        import numpy as np
        B, S, D, O, E, K = (4, 512, 256, 256, 8, 2)
        logits = jnp.einsum('bsd,ed->bse', x, gate_w) + gate_b
        if K < E:
            topv, topi = jax.lax.top_k(logits, K)
            keep = jax.nn.one_hot(topi, E, dtype=jnp.float32).sum(axis=-2)
            logits = jnp.where(keep > 0, logits, -jnp.inf)
        gate_score = jax.nn.softmax(logits, axis=-1)
        expert_out = jnp.einsum('bsd,edo->bseo', x, expert_w) + expert_b
        out = jnp.einsum('bseo,bse->bso', expert_out, gate_score)
        return out

    def _L1_xattn_ref(image_embeds, latents, ln1_g, ln1_b, ln2_g, ln2_b, Wq, Wkv, Wo):
        import jax, jax.numpy as jnp
        import numpy as np
        DIM = 256
        DIM_HEAD = 64
        HEADS = 16
        INNER = DIM_HEAD * HEADS
        EPS = 1e-05

        def layer_norm(x, g, b):
            m = jnp.mean(x, axis=-1, keepdims=True)
            v = jnp.mean(jnp.square(x - m), axis=-1, keepdims=True)
            return (x - m) * jax.lax.rsqrt(v + EPS) * g + b
        B, S_lat, _ = latents.shape
        x = layer_norm(image_embeds, ln1_g, ln1_b)
        l = layer_norm(latents, ln2_g, ln2_b)
        q = l @ Wq
        kv_in = jnp.concatenate([x, l], axis=1)
        kv = kv_in @ Wkv
        k, v = jnp.split(kv, 2, axis=-1)

        def to_heads(t):
            return t.reshape(t.shape[0], t.shape[1], HEADS, DIM_HEAD).transpose(0, 2, 1, 3)
        q, k, v = (to_heads(q), to_heads(k), to_heads(v))
        scale = 1.0 / np.sqrt(np.sqrt(DIM_HEAD))
        w = jnp.einsum('bhqd,bhkd->bhqk', q * scale, k * scale)
        w = jax.nn.softmax(w.astype(jnp.float32), axis=-1).astype(q.dtype)
        out = jnp.einsum('bhqk,bhkd->bhqd', w, v)
        out = out.transpose(0, 2, 1, 3).reshape(B, S_lat, INNER)
        return out @ Wo

    def _L1_attn_ref(x, Wq, bq, Wk, bk, Wv, bv, Wo, bo):
        import jax, jax.numpy as jnp
        import numpy as np
        D_MODEL = 256
        N_HEADS = 16
        N_GROUPS = 4
        CONTEXT_LEN = 128
        D_H = D_MODEL // N_HEADS
        GROUP_SIZE = N_HEADS // N_GROUPS
        B, S = (4, 512)
        b, s = (x.shape[0], x.shape[1])
        q = (x @ Wq + bq).reshape(b, s, N_GROUPS, GROUP_SIZE, D_H)
        q = jnp.transpose(q, (0, 2, 3, 1, 4))
        k = jnp.transpose((x @ Wk + bk).reshape(b, s, N_GROUPS, D_H), (0, 2, 1, 3))
        v = jnp.transpose((x @ Wv + bv).reshape(b, s, N_GROUPS, D_H), (0, 2, 1, 3))
        scores = jnp.einsum('bghqd,bgkd->bghqk', q, k) / jnp.sqrt(jnp.float32(D_H))
        i = jnp.arange(s)
        j = jnp.arange(s)
        upper = (i - CONTEXT_LEN)[:, None] >= j[None, :]
        lower = i[:, None] < j[None, :]
        mask = upper | lower
        scores = jnp.where(mask, jnp.float32(-1000000000.0), scores)
        att = jax.nn.softmax(scores, axis=-1)
        out = jnp.einsum('bghqk,bgkd->bghqd', att, v)
        out = jnp.transpose(out, (0, 3, 1, 2, 4)).reshape(b, s, D_MODEL)
        return out @ Wo + bo

    def _L1_ffn_ref(x, Wg, bg, W1, b1, W2, b2):
        import jax, jax.numpy as jnp
        import numpy as np
        H = 256
        I = 256
        E = 8
        B, S, Hd = x.shape
        xf = x.reshape(-1, Hd)
        logits = xf @ Wg + bg
        gates = jax.nn.softmax(logits, axis=-1)
        idx = jnp.argmax(gates, axis=-1)
        h = jax.nn.gelu(jnp.einsum('th,ehi->tei', xf, W1) + b1, approximate=False)
        y = jnp.einsum('tei,eih->teh', h, W2) + b2
        out = jnp.take_along_axis(y, idx[:, None, None], axis=1)[:, 0, :]
        return out.reshape(B, S, Hd)
    x = x + _L0_xattn_ref(_layernorm(x, axis=-1), ctx_1024, ctx_1024, mask_BxSxS2_ik1, L0_xattn_Wq, L0_xattn_bq, L0_xattn_Wk, L0_xattn_bk, L0_xattn_Wv, L0_xattn_bv, L0_xattn_Wo, L0_xattn_bo)
    x = x + _L0_attn_ref(_layernorm(x, axis=-1), L0_attn_A, L0_attn_Bp, L0_attn_Cp, L0_attn_Dp, L0_attn_Wg, L0_attn_bg, L0_attn_gamma, L0_attn_beta)
    x = x + _L0_ffn_ref(_layernorm(x, axis=-1), L0_ffn_gate_w, L0_ffn_gate_b, L0_ffn_expert_w, L0_ffn_expert_b)
    x = x + _L1_xattn_ref(ctx_1024, _layernorm(x, axis=-1), L1_xattn_ln1_g, L1_xattn_ln1_b, L1_xattn_ln2_g, L1_xattn_ln2_b, L1_xattn_Wq, L1_xattn_Wkv, L1_xattn_Wo)
    x = x + _L1_attn_ref(_layernorm(x, axis=-1), L1_attn_Wq, L1_attn_bq, L1_attn_Wk, L1_attn_bk, L1_attn_Wv, L1_attn_bv, L1_attn_Wo, L1_attn_bo)
    x = x + _L1_ffn_ref(_layernorm(x, axis=-1), L1_ffn_Wg, L1_ffn_bg, L1_ffn_W1, L1_ffn_b1, L1_ffn_W2, L1_ffn_b2)
    return x

_drawn_inputs = setup_inputs


def setup_inputs(seed=0):
    import zlib

    import numpy as np

    out = dict(_drawn_inputs(seed))
    spreads = {'L0_xattn_bq': (0.0, 0.1),
     'L0_xattn_bk': (0.0, 2.0),
     'L0_xattn_bv': (0.0, 0.1),
     'L0_xattn_bo': (0.0, 0.1),
     'L0_attn_bg': (0.0, 0.1),
     'L0_attn_gamma': (1.0, 0.2),
     'L0_attn_beta': (0.0, 0.1),
     'L1_xattn_ln1_g': (1.0, 0.2),
     'L1_xattn_ln1_b': (0.0, 0.1),
     'L1_xattn_ln2_g': (1.0, 0.2),
     'L1_xattn_ln2_b': (0.0, 0.337),
     'L1_ffn_bg': (0.0, 0.1),
     'L1_ffn_b1': (0.0, 0.8),
     'L1_ffn_b2': (0.0, 0.1)}
    factors = {'L0_ffn_expert_b': 3.868,
     'L1_attn_Wq': 8.0,
     'L1_attn_bq': 62.925,
     'L1_attn_Wk': 8.0,
     'L1_attn_bk': 64.0,
     'L1_attn_bv': 8.0,
     'L1_attn_bo': 5.226}
    for name, (base, spread) in spreads.items():
        noise = np.random.default_rng([zlib.crc32(name.encode()), seed]).standard_normal(out[name].shape)
        drawn = base * np.exp(spread * noise) if base else spread * noise
        out[name] = jnp.asarray(drawn.astype(out[name].dtype))
    for name, factor in factors.items():
        out[name] = (out[name] * factor).astype(out[name].dtype)
    return out
```

```python
from contextlib import ExitStack

import concourse.bass as bass
from concourse import mybir
from concourse.alu_op_type import AluOpType as ALU

ACT = mybir.ActivationFunctionType
AX = mybir.AxisListType
F32 = mybir.dt.float32
BF16 = mybir.dt.bfloat16
I32 = mybir.dt.int32

P = 128
B = 2
S = 256
QT = S // P
NT4 = B * QT
D = 256
DC = D // P
S2 = 4096
H = 16
NEG = -3.0e38
EPS = 1e-5
E8 = 8
RING = 4
NPJ = 32
NKT = 9
NPC = NKT + 1 + 9
SCL = 64 ** -0.25
KB = 32
CONV_DONE = 4 + 2 * S + DC
TAPS_DONE = 82
ONE = 1
MG_NEG = 15
TAU = 16
NST = 16


class Attention:

    def __init__(self, sem, name, keys, width, ct):
        self.tiles = [min(512, keys - k) for k in range(0, keys, 512)]
        self.keys = keys
        self.width = width
        self.ct = ct
        self.chunks = keys // P
        self.ns = QT * len(self.tiles)
        self.nt = self.chunks // 2
        self.na = (self.nt + 1) // 2
        self.nd = self.nt // 2
        self.q_ready = sem(name + "_q_ready")
        self.scored = sem(name + "_scored")
        self.score_out = sem(name + "_score_out")
        self.max_ready = sem(name + "_max_ready")
        self.exp_done = sem(name + "_exp_done")
        self.turned = sem(name + "_turned")
        self.turned_act = sem(name + "_turned_act")
        self.turned_dve = sem(name + "_turned_dve")
        self.weighed = sem(name + "_weighed")
        self.out_taken = sem(name + "_out_taken")


def program(nc, a, out):
    with ExitStack() as ctx:
        def sb(name, shape, dt=F32):
            return ctx.enter_context(nc.sbuf_tensor(name, shape, dt))

        def sem(name):
            return ctx.enter_context(nc.semaphore(name))

        RX = sb("RX", [P, 8192])
        RK = sb("RK", [P, 8192])
        RV = sb("RV", [P, 8192])
        RS = sb("RS", [P, 2 * 2 * 4352])
        PT = sb("PT", [P, 4, 512])
        OA = sb("OA", [P, H, S])
        X = sb("X", [P, NT4, D])
        QTR = sb("QTR", [P, DC, B * S])
        WA = sb("WA", [P, 3, DC, D])
        QP = sb("QP", [P, 2, S])
        ident = sb("ident", [P, P])
        ones = sb("ones", [1, P])
        sel16 = sb("sel16", [P, H])
        sel64 = sb("sel64", [P, 2])
        mpart = sb("mpart", [P, 2, QT, 9])
        nmax = sb("nmax", [P, 2, QT])
        den = sb("den", [P, QT, H])
        rden = sb("rden", [P, QT, H])
        cols = sb("cols", [P, 32])
        mv = sb("mv", [P, NT4, 2])
        std = sb("std", [P, NT4])
        rstd = sb("rstd", [P, NT4])
        stats = sb("stats", [P, NT4, 6])

        def bank(name):
            return ctx.enter_context(nc.psum_tensor(name, [P, 512], F32))

        SP_ = [bank(f"score_bank{i}") for i in range(3)]
        TP = [bank(f"turn_bank{i}") for i in range(2)]
        OP = bank("out_bank")
        PJ = [bank(f"proj_bank{i}") for i in range(2)]

        XN = OA[:, 0:4, :]
        XT = OA[:, 4:8, :].rearrange("p (c u) s -> p c (u s)", c=DC)
        ctxT = RX[:, :].rearrange("p (c k) -> p c k", c=DC)
        keyT = RK[:, :].rearrange("p (m k) -> p m k", m=DC)
        val = RV[:, :].rearrange("p (k d) -> p k d", d=D)
        maskb = RX[:, 0:4096].bitcast(BF16).rearrange("p (t k) -> p t k", t=QT)
        VH = RX[:, 4096:6144].rearrange("p (u k d) -> p u k d", u=2, d=32)
        selA = RX[:, 6144:7168].rearrange("p (j c) -> p j c", j=8)
        hselA = RX[0:H, 7168:7424].rearrange("p (m c) -> p m c", m=2)
        scoreA = RS[:, 0:16384].rearrange("p (u t k) -> p u t k", u=2, t=QT)
        maskw = RS[:, 8192:16384].bitcast(I32).rearrange("p (t k) -> p t k", t=QT)
        scoreC = RS[:, :].rearrange("p (u t k) -> p u t k", u=2, t=QT)
        KC = RS[:, 16384:16896].rearrange("p (m k) -> p m k", m=DC)
        BOR = RS[0:1, 16896:17152]
        RB = [PJ[0], PJ[1], TP[0], TP[1]]
        recT = PT[0:H, 0, 0:S]
        ON = RS[:, 0:2048].rearrange("p (j k) -> p j k", j=8)
        OC = RS[:, 2048:4096].rearrange("p (j k) -> p j k", j=8)
        ctile = RS[:, 0:1024].rearrange("p (t d) -> p t d", t=4)
        cnorm = RS[:, 1024:2048].rearrange("p (t d) -> p t d", t=4)
        xlT = RX[:, :].rearrange("p (c k) -> p c k", c=DC)
        keyC = RK[:, 0:4352]
        latT = RK[:, 4352:4864].rearrange("p (c k) -> p c k", c=DC)
        wq = RK[:, 4864:5120].rearrange("p (c n) -> p c n", c=DC)
        wk = RK[:, 5120:5376].rearrange("p (c n) -> p c n", c=DC)
        wv = RK[:, 5376:5632].rearrange("p (c n) -> p c n", c=DC)
        qC = RK[:, 5632:5888]
        latAll = RK[:, 5888:6912].rearrange("p (c k) -> p c k", c=DC)
        valC = RV[:, 0:4352].rearrange("p (k d) -> p k d", d=P)
        woC = RV[:, 4352:6400].rearrange("p (j n) -> p j n", n=D)
        selC = RV[:, 6400:6656].rearrange("p (u c) -> p u c", u=2)
        hselC = RV[0:H, 6656:7680].rearrange("p (j c) -> p j c", j=8)

        block = ctx.enter_context(nc.Block())

        A = Attention(sem, "a", S2, 32, 4)
        C = Attention(sem, "c", S2 + S, 64, 2)

        x_in, wqa_in, wa_in, cols_in = sem("x_in"), sem("wqa_in"), sem("wa_in"), sem("cols_in")
        scan_in = sem("scan_in")
        consts = sem("consts")
        ctx_in, mask_in, sela_in = sem("ctx_in"), sem("mask_in"), sem("sela_in")
        ln_stat, ln_aggr, ln_std, ln_rstd = sem("ln_stat"), sem("ln_aggr"), sem("ln_std"), sem("ln_rstd")
        ln_norm, ln_turn, ln_out = sem("ln_norm"), sem("ln_turn"), sem("ln_out")
        qa_mm, qa_out = sem("qa_mm"), sem("qa_out")
        pja_mm, pja_out = sem("pja_mm"), sem("pja_out")
        mask_ready = sem("mask_ready")
        vh_zero, vh_ready = sem("vh_zero"), sem("vh_ready")
        pa_rden, pa_rt, pa_rtc, pa_sum, pa_oc, pa_on, pa_y, pa_x = [sem("post_" + n) for n in (
            "recip", "recip_turned", "recip_in_sbuf", "summed", "sum_in_sbuf", "normed", "projected", "added")]
        taps = sem("taps")
        gate_w_in, gate_mm, gate_act, gated = sem("gate_w_in"), sem("gate_mm"), sem("gate_act"), sem("gated")
        conv, y_turn, y_norm, scan_done = sem("conv"), sem("y_turn"), sem("y_norm"), sem("scan_done")
        pad_zero = sem("pad_zero")
        moe_w_in, moe_lg, moe_g, moe_mm, moe_acc = (
            sem("moe_w_in"), sem("moe_logits"), sem("moe_gate"), sem("moe_mm"), sem("moe_acc"))
        lat_done = sem("lat_done")
        cw_in, cpost_in = sem("cw_in"), sem("cpost_in")
        tile_in, tile_norm, tile_turn, tile_out, tile_st = (
            sem("tile_in"), sem("tile_norm"), sem("tile_turn"), sem("tile_out"), sem("tile_stat"))
        tile_ag, tile_sq, tile_rs = sem("tile_aggr"), sem("tile_std"), sem("tile_rstd")
        lat_copy = sem("lat_copy")
        wqc_in, wkc_in, wvc_in = sem("wqc_in"), sem("wkc_in"), sem("wvc_in")
        pjc_mm, pjc_out = sem("pjc_mm"), sem("pjc_out")
        sw_in, sq_mm, sq_out, skv_mm, skv_out = [sem("self_" + n) for n in ("w_in", "q_mm", "q_out", "kv_mm", "kv_out")]
        s_q, s_mm, s_ev, s_nm, s_ex, s_t, s_tc, s_pv, s_on, s_rd, s_ot, s_oc, s_y, s_x = [
            sem("self_" + n) for n in ("q", "scored", "score_out", "max", "exp", "turned", "turned_out", "weighed",
                                       "normed", "recip", "out_turned", "out_in_sbuf", "projected", "added")]
        fw_in, f_lg, f_g, f_h, f_ge, f_y, f_acc = [sem("ffn_" + n) for n in (
            "w_in", "logits", "gate", "hidden", "gelu", "mm", "acc")]
        stored = sem("stored")
        waited = sem("waited")

        C_BQ, C_BK, C_BV, C_BG, C_DP, C_G1, C_B1, C_G2, C_B2 = range(0, 18, 2)
        C_SQ, C_SK = 18, 20

        wgT = RX[:, 0:512].rearrange("p (c n) -> p c n", c=DC)
        gamma_r, beta_r = RX[:, 512:768], RX[:, 768:1024]
        GT = RX[:, 1024:2048].rearrange("p (m k) -> p m k", m=DC)
        XG = RK[:, 0:2048].rearrange("p (m b k) -> p m b k", m=DC, b=B)
        Y = RK[:, 2048:4096].rearrange("p (a m b k) -> p a m b k", a=2, m=DC, b=B)
        YT = RX[:, 2048:3072].rearrange("p (t d) -> p t d", t=NT4)
        ew = RV[:, 0:4096].rearrange("p (c n) -> p c n", c=DC)
        ebr = RK[0:1, 4096:6144]
        gw = RX[:, 4096:4112].rearrange("p (c n) -> p c n", c=DC)
        gbr = RX[0:1, 4112:4120]
        iot = RX[:, 4120:4128]
        G = RX[:, 4128:4640].rearrange("p (n t e) -> p n t e", n=16, t=NT4)
        swq = RX[:, 0:512].rearrange("p (c n) -> p c n", c=DC)
        swk = RX[:, 512:768].rearrange("p (c n) -> p c n", c=DC)
        swv = RX[:, 768:896].rearrange("p (c n) -> p c n", c=DC)
        swo = RX[:, 896:1408].rearrange("p (c n) -> p c n", c=DC)
        sbv = RX[0:1, 1408:1472]
        sbo = RX[0:1, 1472:1728]
        smask = RX[:, 1728:2240].rearrange("p (t k) -> p t k", t=QT)
        sK = RX[:, 2240:2752]
        sV = RX[:, 2752:3008].rearrange("p (t d) -> p t d", t=NT4)
        sQ = RK[:, 0:8192].rearrange("p (h k) -> p h k", h=H)
        sS = RS[:, 0:16384].rearrange("p (t h k) -> p t h k", t=NT4, h=H)
        sPT = RV[:, 0:1024].rearrange("p (n k) -> p n k", n=4)
        sO = RV[:, 1024:2048].rearrange("p (t d) -> p t d", t=NT4)
        sOT = RV[:, 2048:3072].rearrange("p (c k) -> p c k", c=DC)
        smx = RV[:, 3072:3136].rearrange("p (t h) -> p t h", t=NT4)
        sden = RV[:, 3136:3200].rearrange("p (t h) -> p t h", t=NT4)
        srd = RV[:, 3200:3264].rearrange("p (t h) -> p t h", t=NT4)
        w1 = RV[:, 4096:8192].rearrange("p (c n) -> p c n", c=DC)
        w2 = RX[:, 4096:8192].rearrange("p (e c n) -> p e c n", e=E8, c=DC)
        b2r = PT[0:1, :, :].rearrange("p a b -> p (a b)")
        fgw = RX[:, 3008:3024].rearrange("p (c n) -> p c n", c=DC)
        fbg = RX[0:1, 3024:3032]
        fb1 = RX[:, 3040:3056]
        iot2 = RX[:, 3056:3064]
        G2 = RX[:, 3072:3584].rearrange("p (n t e) -> p n t e", n=16, t=NT4)
        hT = RK[:, 0:8192].rearrange("p (e c k) -> p e c k", e=E8, c=DC)

        kA = RS[:, 0:512].rearrange("p (h n m) -> p h n m", h=2, n=NST)
        kP = RS[:, 512:1536].rearrange("p (s h n m) -> p s h n m", s=2, h=2, n=NST)
        kB = RS[:, 1536:1568].rearrange("p (h n) -> p h n", h=2)
        kC = RS[:, 1568:1600].rearrange("p (h n) -> p h n", h=2)
        kW = RS[:, 2048:2560].rearrange("p (j h n) -> p j h n", j=TAU, h=2)
        kV = RS[:, 2560:3072].rearrange("p (j h n) -> p j h n", j=TAU, h=2)
        kT = RS[:, 4096:8192]

        def ctx_views(b):
            return a["ctxT"][bass.ds(b, 1), :, :].rearrange("b (c p) k -> p (b c) k", p=P)

        def groups(second):
            return 8 if second else 2

        def normed_before(b, second):
            return b * 8 + 4 * B if second else b * 4

        def post_pe(pe, b, second):
            k = b + B * second
            at = C if second else A
            pe.wait_ge(at.out_taken, b * H + H + ONE)
            if second:
                pe.wait_ge(cpost_in, 48)
            else:
                pe.wait_ge(sela_in, 32 * b + 32)
            pe.wait_ge(pa_rden, k + 1)
            for t in range(QT):
                mm = pe.transpose(TP[0][0:H, t * P:(t + 1) * P], rden[:, t, :], ident[:, :])
            mm.then_inc(pa_rt, 1)
            pe.wait_ge(pa_rtc, k + 1)
            for j in range(groups(second)):
                if j >= 2:
                    pe.wait_ge(pa_on, normed_before(b, second) + j - 1)
                pe.matmul(PJ[j % 2][:, 0:S], (hselC if second else hselA)[:, j, :], recT, start=True, stop=True)
                n = 2 if second else 8
                for u in range(n):
                    mm = pe.matmul(SP_[j % 2][:, 0:S], (selC if second else selA)[:, u, :], OA[:, n * j + u, :],
                                   start=(u == 0), stop=(u == n - 1))
                mm.then_inc(pa_sum, 1)
            pe.wait_ge(pa_on, normed_before(b, second) + (8 if second else 4))
            for t in range(QT):
                for j in range(groups(second)):
                    mm = pe.matmul(TP[t][:, 0:D], ON[:, j, t * P:(t + 1) * P], woC[:, j, :] if second else WA[:, 2, j, :],
                                   start=(j == 0), stop=bool(second and j == 7))
                if not second:
                    mm = pe.matmul(TP[t][:, 0:D], ones[0:1, :], BOR, start=False, stop=True)
                mm.then_inc(pa_y, 1)
            pe.wait_ge(pa_x, QT * k + QT)

        def post_act(act, b, second):
            k = b + B * second
            act.wait_ge(pa_rt, k + 1)
            act.activation(recT, TP[0][0:H, 0:S], ACT.Copy).then_inc(pa_rtc, 1)
            before = b * 8 + 2 * B if second else b * 2
            for j in range(groups(second)):
                act.wait_ge(pa_sum, before + j + 1)
                act.activation(OC[:, j, :], SP_[j % 2][:, 0:S], ACT.Copy).then_inc(pa_oc, 1)

        def post_dve(dve, b, second):
            k = b + B * second
            dve.reciprocal(rden[:, :, :], den[:, :, :]).then_inc(pa_rden, 1)
            before = b * 8 + 2 * B if second else b * 2
            for j in range(groups(second)):
                dve.wait_ge(pa_oc, before + j + 1)
                dve.tensor_tensor(ON[:, j, :], OC[:, j, :], PJ[j % 2][:, 0:S], ALU.mult).then_inc(pa_on, 1)
                if not second:
                    dve.wait_ge(pa_on, b * 4 + 2 * j + 1)
                    dve.tensor_scalar(ON[:, j, :], ON[:, j, :], cols[:, C_BV + j:C_BV + j + 1], None, ALU.add)\
                        .then_inc(pa_on, 1)
            for t in range(QT):
                dve.wait_ge(pa_y, QT * k + t + 1)
                x = X[:, bass.ds(b * QT + t, 1), :].rearrange("p a d -> p (a d)")
                dve.tensor_tensor(x, x, TP[t][:, 0:D], ALU.add).then_inc(pa_x, 1)
            dve.wait_ge(pa_x, QT * k + QT)

        def self_weigh(pe, n):
            t, h = divmod(n, H)
            nb = t % QT + 1
            pe.wait_ge(s_tc, n + 1)
            if h == 0 and t >= 2:
                pe.wait_ge(s_on, t - 1)
            for k in range(nb):
                mm = pe.matmul([OP, PJ[0]][t % 2][:, h * 16:h * 16 + 16], sPT[:, n % 4, k * P:(k + 1) * P],
                               sV[:, t // QT * QT + k, (h // 4) * 16:(h // 4) * 16 + 16], start=(k == 0), stop=(k == nb - 1))
            mm.then_inc(s_pv, 1)

        def self_norm(dve, t):
            dve.wait_ge(s_pv, (t + 1) * H)
            dve.reciprocal(srd[:, t, :], sden[:, t, :]).then_inc(s_rd, 1)
            dve.wait_ge(s_rd, t + 1)
            dve.tensor_tensor(sO[:, t, :].rearrange("p (h d) -> p h d", h=H),
                              [OP, PJ[0]][t % 2][:, 0:D].rearrange("p (h d) -> p h d", h=H),
                              srd[:, t, :].unsqueeze(2).broadcast_to([P, H, 16]), ALU.mult).then_inc(s_on, 1)

        @block.sync
        def _(sp):
            def load(dst, name, s_):
                return sp.dma_start(dst, a[name]).then_inc(s_, 16)

            sp.dma_start(X[:, :, :], a["x"].rearrange("b (t p) d -> p (b t) d", p=P)).then_inc(x_in, 16)
            load(kA, "A", scan_in)
            load(kB, "Bp", scan_in)
            load(kC, "Cp", scan_in)
            load(RV[:, 0:512].rearrange("p (c n) -> p c n", c=DC), "WqT", wqa_in)
            load(WA[:, 0, :, :], "WkT", wa_in)
            load(WA[:, 1, :, :], "WvT", wa_in)
            load(WA[:, 2, :, :], "WoT", wa_in)
            load(cols[:, 0:22], "cols", cols_in)
            load(sel16[:, :], "sel16", cols_in)
            load(sel64[:, :], "sel64", cols_in)
            load(BOR, "bo", cols_in)
            with sp.Fori(0, B) as b:
                sp.wait_ge(A.out_taken, b * H + ONE)
                for c in range(DC):
                    for k in range(2):
                        sp.dma_start(ctxT[:, c, 2048 * k:2048 * k + 2048],
                                     ctx_views(b)[:, c, 2048 * k:2048 * k + 2048]).then_inc(ctx_in, 16)
                for t in range(QT):
                    sp.dma_start(maskw[:, t, :], a["mask"][bass.ds(b, 1), t * P:(t + 1) * P, :]
                                 .rearrange("b p k -> p (b k)")).then_inc(mask_in, 16)
                sp.wait_ge(pja_out, b * NPJ + RING + NPJ)
                sp.dma_start(selA, a["selA"]).then_inc(sela_in, 16)
                sp.dma_start(hselA, a["hselA"]).then_inc(sela_in, 16)
                sp.wait_ge(pa_x, QT * b + QT)
                sp.sem_inc(waited, 1)

            load(wgT, "WgT", gate_w_in)
            load(gamma_r, "gamma", gate_w_in)
            load(beta_r, "beta", gate_w_in)
            load(ew, "ew", moe_w_in)
            load(ebr, "eb", moe_w_in)
            load(gw, "gwT", moe_w_in)
            load(gbr, "gb", moe_w_in)
            load(iot, "iota", moe_w_in)
            sp.wait_ge(moe_acc, 2 * NT4 * 4)
            load(woC, "WoC", cpost_in)
            load(selC, "selC", cpost_in)
            load(hselC, "hselC", cpost_in)
            ctx_t = a["ctx"].rearrange("b (t p) d -> b t p d", p=P)

            def pair_w(w, dst, name, p):
                sp.dma_start(dst, a[name][bass.ds(p, 1), :, :, :].rearrange("a p c n -> p (a c) n")).then_inc(w, 16)

            with sp.Fori(0, B) as b:
                with sp.Fori(0, 8) as i:
                    sp.wait_ge(tile_turn, 2 * (b * 8 + i) + ONE)
                    if True:
                        sp.dma_start(ctile, ctx_t[bass.ds(b, 1), bass.ds(i * 4, 4), :, :]
                                     .rearrange("b t p d -> p (b t) d")).then_inc(tile_in, 16)
                with sp.Fori(0, 8) as p:
                    sp.wait_ge(pjc_out, (b * 8 + p) * NPC + ONE)
                    pair_w(wqc_in, wq, "WqC", p)
                    pair_w(wkc_in, wk, "WkC", p)
                    pair_w(wvc_in, wv, "WvC", p)
                sp.wait_ge(pa_x, QT * B + QT * b + QT)
                sp.sem_inc(waited, 1)
            sp.wait_ge(pa_x, QT * (2 * B))
            load(swq, "sWq", sw_in)
            load(swk, "sWk", sw_in)
            load(swv, "sWv", sw_in)
            load(swo, "sWo", sw_in)
            load(sbv, "sbv", sw_in)
            load(sbo, "sbo", sw_in)
            load(smask, "smask", sw_in)
            load(w1, "W1", fw_in)
            load(w2, "W2", fw_in)
            load(b2r, "b2", fw_in)
            load(fgw, "fWg", fw_in)
            load(fbg, "fbg", fw_in)
            load(fb1, "fb1", fw_in)
            load(iot2, "iota", fw_in)
            sp.wait_ge(f_acc, NT4 * E8)
            sp.dma_start(out.rearrange("b (t p) d -> p (b t) d", p=P), X[:, :, :]).then_inc(stored, 16)
            sp.wait_ge(stored, 16)

        @block.gpsimd
        def _(pool):
            pool.memset(ident[:, :], 0.0).then_inc(consts, 1)
            pool.memset(ones[:, :], 1.0).then_inc(consts, 1)
            pool.wait_ge(consts, 2)
            pool.affine_select(out=ident[:, :], in_=ident[:, :], compare_op=ALU.not_equal, fill=1.0, base=0,
                               pattern=[[-1, P]], channel_multiplier=1).then_inc(consts, 1)
            pool.wait_ge(cols_in, 64)
            pool.wait_ge(qa_out, DC)

            def queries_a(b, h, u):
                pool.tensor_tensor(QP[:, u, :], QTR[:, bass.ds(h // 8, 1), bass.ds(b * S, S)].rearrange("p a k -> p (a k)"),
                                   sel16[:, bass.ds(h, 1)].broadcast_to([P, S]), ALU.mult).then_inc(A.q_ready, 1)

            def values_a(h, u):
                pool.tensor_copy(VH[:, u, :, 0:16], val[:, :, bass.ds(h * 16, 16)]).then_inc(vh_ready, 1)

            with pool.Fori(0, B) as b:
                pool.wait_ge(A.scored, b * H * A.ns + ONE)
                queries_a(b, 0, 0)
                pool.wait_ge(pja_out, b * NPJ + RING + NPJ)
                pool.sem_inc(waited, 1)
                pool.memset(VH[:, :, :, 16:32], 0.0).then_inc(vh_zero, 1)
                values_a(0, 0)

                def step(h, u):
                    g = b * H + h
                    pool.wait_ge(A.scored, g * A.ns + ONE)
                    queries_a(b, h + 1, 1 - u)
                    pool.wait_ge(A.weighed, g * A.nt + ONE)
                    pool.sem_inc(waited, 1)
                    values_a(h + 1, 1 - u)

                with pool.Fori(0, H - 2, 2) as i:
                    for u in range(2):
                        step(i + u, u)
                step(H - 2, 0)

            pool.wait_ge(pa_x, QT * B)
            pool.memset(XG[:, :, :, 0:S], 0.0).then_inc(pad_zero, 1)

            with pool.Fori(0, B) as b:
                with pool.Fori(0, 8) as p:
                    pool.wait_ge(pjc_out, (b * 8 + p) * NPC + NKT + 1 + ONE)
                    for u in range(2):
                        pool.tensor_tensor(QP[:, u, :], qC, sel64[:, u:u + 1].broadcast_to([P, S]), ALU.mult)\
                            .then_inc(C.q_ready, 1)

            pool.wait_ge(sq_out, DC)
            for h in range(H):
                s_, g = h % 4, h // 4
                pool.tensor_tensor(sQ[:, h, :], QTR[:, s_ // 2, :],
                                   sel16[:, 4 * (s_ % 2) + g:4 * (s_ % 2) + g + 1].broadcast_to([P, B * S]),
                                   ALU.mult).then_inc(s_q, 1)

        @block.scalar
        def _(act):
            def ln_sqrt(k):
                act.wait_ge(ln_aggr, NT4 * (k + 1))
                if k:
                    act.wait_ge(ln_rstd, k)
                act.activation(std[:, :], mv[:, :, 1], ACT.Sqrt, bias=EPS).then_inc(ln_std, 1)

            def ln_evac(k, gain=None, shift=None):
                for c in range(DC):
                    act.wait_ge(ln_turn, DC * k + c + 1)
                    kw = {} if gain is None else dict(scale=cols[:, gain + c:gain + c + 1],
                                                      bias=cols[:, shift + c:shift + c + 1])
                    act.activation(XT[:, c, :], TP[c][:, :], ACT.Identity if kw else ACT.Copy, **kw).then_inc(ln_out, 1)

            def exps(at, score, g, h, u):
                for t in range(QT):
                    act.wait_ge(at.max_ready, 2 * g + t + 1)
                    act.activation(score[:, u, t, :], score[:, u, t, :], ACT.Exp, bias=nmax[:, u, t:t + 1],
                                   accum_out=den[:, t, bass.ds(h, 1)]).then_inc(at.exp_done, 1)

            def turned(at, g):
                for n in range(0, at.nt, 2):
                    act.wait_ge(at.turned, g * at.nt + n + 1)
                    act.wait_ge(at.weighed, g * at.nt + (0 if n < 4 else n - 3) + ONE)
                    act.activation(PT[:, n % 4, :], TP[0][:, :], ACT.Copy).then_inc(at.turned_act, 1)

            act.sem_inc(pja_out, RING)
            for s_ in (A.turned_act, C.turned_act, pjc_out, tile_out):
                act.sem_inc(s_, ONE)
            act.wait_ge(cols_in, 64)
            ln_sqrt(0)
            ln_evac(0)
            with act.Fori(0, B) as b:
                with act.Fori(0, 4) as i:
                    for e in range(4):
                        act.wait_ge(pja_mm, b * NPJ + i * 4 + e + 1)
                        act.activation(keyT[:, e % 2, bass.ds(i * 1024 + (e // 2) * 512, 512)], RB[e][:, :],
                                       ACT.Identity, bias=cols[:, C_BK + e % 2:C_BK + e % 2 + 1]).then_inc(pja_out, 1)
                for n in range(16):
                    act.wait_ge(pja_mm, b * NPJ + 16 + n + 1)
                    act.activation(val[:, 2 * n:2 * n + 2, :].rearrange("p k d -> p (k d)"), RB[n % 4][:, :],
                                   ACT.Copy).then_inc(pja_out, 1)
                with act.Fori(0, H - 2, 2) as i:
                    for u in range(2):
                        exps(A, scoreA, b * H + i + u, i + u, u)
                        turned(A, b * H + i + u)
                for h in range(H - 2, H):
                    exps(A, scoreA, b * H + h, h, h % 2)
                    turned(A, b * H + h)
                post_act(act, b, 0)

            ln_sqrt(1)
            ln_evac(1)
            for m in range(DC):
                act.wait_ge(gate_mm, m + 1)
                act.activation(GT[:, m, :], PJ[m][:, :], ACT.Sigmoid, bias=cols[:, C_BG + m:C_BG + m + 1])\
                    .then_inc(gate_act, 1)
            for t in range(NT4):
                act.wait_ge(y_turn, 2 * t + 2)
                act.activation(YT[:, t, :], SP_[t % 2][:, 0:D], ACT.Copy).then_inc(y_norm, 1)
            ln_sqrt(2)
            ln_sqrt(3)
            ln_evac(2)
            act.wait_ge(moe_g, MG_NEG)
            act.activation(G[:, 8, :, :], G[:, 7, :, :], ACT.Exp).then_inc(moe_g, 1)
            ln_sqrt(4)
            ln_sqrt(5)
            ln_evac(3, C_G2, C_B2)
            act.wait_ge(ln_out, 8)
            for c in range(DC):
                act.activation(latAll[:, c, :], XT[:, c, :], ACT.Copy).then_inc(lat_done, 1)
            with act.Fori(0, B) as b:
                with act.Fori(0, 8) as i:
                    act.wait_ge(tile_ag, (b * 8 + i + 1) * 4)
                    act.activation(std[:, :], mv[:, :, 1], ACT.Sqrt, bias=EPS).then_inc(tile_sq, 1)
                    for c in range(DC):
                        act.wait_ge(tile_turn, (b * 8 + i) * 2 + c + 1 + ONE)
                        act.activation(xlT[:, c, bass.ds(i * 512, 512)], TP[c][:, :], ACT.Identity,
                                       scale=cols[:, C_G1 + c:C_G1 + c + 1],
                                       bias=cols[:, C_B1 + c:C_B1 + c + 1]).then_inc(tile_out, 1)
                act.wait_ge(lat_done, DC)
                act.activation(latT, latAll[:, :, bass.ds(b * S, S)], ACT.Copy).then_inc(lat_copy, 1)

                def keys_c(p):
                    e0 = (b * 8 + p) * NPC
                    for n in range(NKT):
                        w = C.tiles[n]
                        act.wait_ge(pjc_mm, e0 + n + 1)
                        act.activation(keyC[:, n * 512:n * 512 + w], PJ[n % 2][:, 0:w], ACT.Copy, scale=SCL)\
                            .then_inc(pjc_out, 1)
                    act.wait_ge(pjc_mm, e0 + NKT + 1)
                    act.activation(qC, PJ[NKT % 2][:, 0:S], ACT.Copy, scale=SCL).then_inc(pjc_out, 1)

                def values_c(p):
                    e0 = (b * 8 + p) * NPC + NKT + 1
                    for n in range(9):
                        w = 4 if n < 8 else 2
                        act.wait_ge(pjc_mm, e0 + n + 1)
                        act.activation(valC[:, 4 * n:4 * n + w, :].rearrange("p k d -> p (k d)"),
                                       PJ[(NKT + 1 + n) % 2][:, 0:w * P], ACT.Copy).then_inc(pjc_out, 1)

                keys_c(0)
                values_c(0)
                exps(C, scoreC, b * H, 0, 0)
                turned(C, b * H)
                with act.Fori(1, 8) as p:
                    keys_c(p)
                    exps(C, scoreC, b * H + 2 * p - 1, 2 * p - 1, 1)
                    turned(C, b * H + 2 * p - 1)
                    values_c(p)
                    exps(C, scoreC, b * H + 2 * p, 2 * p, 0)
                    turned(C, b * H + 2 * p)
                exps(C, scoreC, b * H + H - 1, H - 1, 1)
                turned(C, b * H + H - 1)
                post_act(act, b, 1)
            ln_sqrt(6)
            ln_evac(4)
            act.wait_ge(skv_mm, 1)
            act.activation(sK, PJ[0][:, :], ACT.Identity, bias=cols[:, C_SK:C_SK + 1]).then_inc(skv_out, 1)
            for t in range(NT4):
                act.wait_ge(skv_mm, 1 + NT4)
                act.activation(sV[:, t, :], PJ[1][:, t * 64:t * 64 + 64], ACT.Copy).then_inc(skv_out, 1)
            for t in range(NT4):
                for h in range(H):
                    act.wait_ge(s_nm, t + 1)
                    act.activation(sS[:, t, h, :], sS[:, t, h, :], ACT.Exp, bias=smx[:, t, h:h + 1],
                                   accum_out=sden[:, t, h:h + 1]).then_inc(s_ex, 1)
            for c in range(DC):
                act.wait_ge(s_ot, c + 1)
                act.activation(sOT[:, c, :], TP[c][:, :], ACT.Copy).then_inc(s_oc, 1)
            ln_sqrt(7)
            ln_evac(5)
            for n in range(2 * E8):
                act.wait_ge(f_h, n + 1)
                act.activation(hT[:, n // 2, n % 2, :], RB[n % 4][:, :], ACT.Gelu, bias=fb1[:, n:n + 1])\
                    .then_inc(f_ge, 1)

        @block.tensor
        def _(pe):
            def ln_pe(k, kx):
                pe.wait_ge(ln_norm, NT4 * (k + 1))
                if kx:
                    pe.wait_ge(ln_out, DC * kx)
                for c in range(DC):
                    for t in range(NT4):
                        mm = pe.transpose(TP[c][:, t * P:(t + 1) * P], XN[:, t, c * P:(c + 1) * P], ident[:, :])
                    mm.then_inc(ln_turn, 1)

            def scores(at, g, u, rhs):
                pe.wait_ge(at.q_ready, g + 1)
                pe.wait_ge(at.score_out, g * at.ns + ONE)
                for t in range(QT):
                    for k, w in enumerate(at.tiles):
                        n = t * len(at.tiles) + k
                        if n >= 3:
                            pe.wait_ge(at.score_out, g * at.ns + n - 2 + ONE)
                        pe.matmul(SP_[n % 3][:, 0:w], QP[:, u, t * P:(t + 1) * P], rhs(k, w),
                                  start=True, stop=True).then_inc(at.scored, 1)

            def values(at, score, g, u, vals):
                def turn(n):
                    if n % 2 == 0:
                        pe.wait_ge(at.turned_act, g * at.na + n // 2 + ONE)
                    else:
                        pe.wait_ge(at.turned_dve, g * at.nd + n // 2 + ONE)
                    for cc in range(2):
                        for t in range(QT):
                            mm = pe.transpose(TP[n % 2][:, (cc * QT + t) * P:(cc * QT + t + 1) * P],
                                              score[:, u, t, (2 * n + cc) * P:(2 * n + cc + 1) * P], ident[:, :])
                    mm.then_inc(at.turned, 1)

                def weigh(n):
                    if n % 2 == 0:
                        pe.wait_ge(at.turned_act, g * at.na + n // 2 + 1 + ONE)
                    else:
                        pe.wait_ge(at.turned_dve, g * at.nd + n // 2 + 1 + ONE)
                    for cc in range(2):
                        k = 2 * n + cc
                        j = k % at.ct
                        mm = pe.matmul(OP[at.width * j:at.width * (j + 1), 0:S], vals(k),
                                       PT[:, n % 4, cc * S:(cc + 1) * S], start=k < at.ct,
                                       stop=k >= at.chunks - at.ct, skip_group_check=True)
                    mm.then_inc(at.weighed, 1)

                pe.wait_ge(at.exp_done, 2 * g + 2)
                pe.wait_ge(at.out_taken, g + ONE)
                for n in range(at.nt):
                    turn(n)
                    if n >= 2:
                        weigh(n - 2)
                weigh(at.nt - 2)
                weigh(at.nt - 1)

            for s_ in (A.scored, C.scored, A.weighed, C.weighed, tile_turn):
                pe.sem_inc(s_, ONE)
            pe.wait_ge(consts, 3)
            pe.wait_ge(wqa_in, 16)
            ln_pe(0, 0)
            pe.wait_ge(ln_out, DC)
            wqa = RV[:, 0:512].rearrange("p (c n) -> p c n", c=DC)
            for m in range(DC):
                for c in range(DC):
                    mm = pe.matmul(PJ[m][:, :], wqa[:, c, m * P:(m + 1) * P], XT[:, c, :],
                                   start=(c == 0), stop=(c == DC - 1))
                mm.then_inc(qa_mm, 1)
            pe.wait_ge(wa_in, 48)
            pe.wait_ge(qa_out, DC)
            with pe.Fori(0, B) as b:
                pe.wait_ge(ctx_in, 64 * b + 64)
                pe.sem_inc(waited, 1)
                with pe.Fori(0, 4) as i:
                    for e in range(4):
                        pe.wait_ge(pja_out, b * NPJ + i * 4 + e + 1)
                        for c in range(DC):
                            mm = pe.matmul(RB[e][:, :], WA[:, 0, c, (e % 2) * P:(e % 2 + 1) * P],
                                           ctxT[:, c, bass.ds(i * 1024 + (e // 2) * 512, 512)],
                                           start=(c == 0), stop=(c == DC - 1))
                        mm.then_inc(pja_mm, 1)
                for n in range(16):
                    pe.wait_ge(pja_out, b * NPJ + 16 + n + 1)
                    for kk in range(2):
                        for c in range(DC):
                            mm = pe.matmul(RB[n % 4][:, kk * D:(kk + 1) * D],
                                           ctxT[:, c, (2 * n + kk) * P:(2 * n + kk + 1) * P], WA[:, 1, c, :],
                                           start=(c == 0), stop=(c == DC - 1))
                    mm.then_inc(pja_mm, 1)
                pe.wait_ge(pja_out, b * NPJ + RING + NPJ)

                def scores_a(h, u):
                    scores(A, b * H + h, u, lambda k, w: keyT[:, bass.ds(h // 8, 1), k * 512:(k + 1) * 512]
                           .rearrange("p a k -> p (a k)"))

                def values_a(h, u):
                    pe.wait_ge(vh_zero, b + 1)
                    pe.wait_ge(vh_ready, b * H + h + 1)
                    values(A, scoreA, b * H + h, u, lambda k: VH[:, u, k, :])

                scores_a(0, 0)
                with pe.Fori(0, H - 2, 2) as i:
                    for u in range(2):
                        scores_a(i + u + 1, 1 - u)
                        values_a(i + u, u)
                scores_a(H - 1, 1)
                values_a(H - 2, 0)
                values_a(H - 1, 1)
                post_pe(pe, b, 0)

            ln_pe(1, 1)
            pe.wait_ge(ln_out, 2 * DC)
            pe.wait_ge(gate_w_in, 48)
            for m in range(DC):
                for c in range(DC):
                    mm = pe.matmul(PJ[m][:, :], wgT[:, c, m * P:(m + 1) * P], XT[:, c, :],
                                   start=(c == 0), stop=(c == DC - 1))
                mm.then_inc(gate_mm, 1)
            pe.wait_ge(conv, CONV_DONE)
            for t in range(NT4):
                if t >= 2:
                    pe.wait_ge(y_norm, t - 1)
                for m in range(DC):
                    pe.transpose(SP_[t % 2][:, m * P:(m + 1) * P],
                                 Y[:, 0, m, t // QT, (t % QT) * P:(t % QT + 1) * P], ident[:, :]).then_inc(y_turn, 1)
            ln_pe(3, 2)
            pe.wait_ge(ln_out, 3 * DC)
            pe.wait_ge(moe_w_in, 80)
            for t in range(NT4):
                for c in range(DC):
                    pe.matmul(OP[:, t * E8:(t + 1) * E8], XT[:, c, t * P:(t + 1) * P], gw[:, c, :],
                              start=(c == 0), stop=False)
                pe.matmul(OP[:, t * E8:(t + 1) * E8], ones[0:1, :], gbr, start=False, stop=True).then_inc(moe_lg, 1)
            for n in range(NT4 * 4):
                t, e2 = n // 4, n % 4
                if n >= 4:
                    pe.wait_ge(moe_acc, 2 * (n - 3))
                for c in range(DC):
                    pe.matmul(RB[n % 4][:, :], XT[:, c, t * P:(t + 1) * P], ew[:, c, e2 * 512:(e2 + 1) * 512],
                              start=(c == 0), stop=False)
                pe.matmul(RB[n % 4][:, :], ones[0:1, :], ebr[:, e2 * 512:(e2 + 1) * 512],
                          start=False, stop=True).then_inc(moe_mm, 1)
            pe.wait_ge(moe_acc, 2 * NT4 * 4)
            ln_pe(5, 3)
            with pe.Fori(0, B) as b:
                with pe.Fori(0, 8) as i:
                    pe.wait_ge(tile_norm, (b * 8 + i) * 4 + 4)
                    pe.wait_ge(tile_out, (b * 8 + i) * 2 + ONE)
                    for c in range(DC):
                        for t in range(4):
                            mm = pe.transpose(TP[c][:, t * P:(t + 1) * P], cnorm[:, t, c * P:(c + 1) * P], ident[:, :])
                        mm.then_inc(tile_turn, 1)
                pe.wait_ge(tile_out, (b + 1) * 16 + ONE)
                pe.wait_ge(lat_copy, b + 1)

                def lhs(k, c):
                    return xlT[:, c, k * P:(k + 1) * P] if k < S2 // P else latT[:, c, (k - S2 // P) * P:(k - S2 // P + 1) * P]

                def project(p, n, mms):
                    pe.wait_ge(pjc_out, (b * 8 + p) * NPC + max(0, n - 1) + ONE)
                    for o, l, r, st, sp_ in mms:
                        mm = pe.matmul(PJ[n % 2][:, o[0]:o[1]], l, r, start=st, stop=sp_)
                    mm.then_inc(pjc_mm, 1)

                def keys_c(p):
                    pe.wait_ge(wkc_in, (b * 8 + p) * 16 + 16)
                    for n in range(NKT):
                        w = C.tiles[n]
                        project(p, n, [((0, w), wk[:, c, :], xlT[:, c, n * 512:n * 512 + w] if n < 8 else latT[:, c, :],
                                        c == 0, c == DC - 1) for c in range(DC)])
                    pe.wait_ge(wqc_in, (b * 8 + p) * 16 + 16)
                    project(p, NKT, [((0, S), wq[:, c, :], latT[:, c, :], c == 0, c == DC - 1) for c in range(DC)])

                def values_p(p):
                    pe.wait_ge(wvc_in, (b * 8 + p) * 16 + 16)
                    for n in range(9):
                        w = 4 if n < 8 else 2
                        project(p, NKT + 1 + n, [((kk * P, (kk + 1) * P), lhs(4 * n + kk, c), wv[:, c, :],
                                                  c == 0, c == DC - 1) for kk in range(w) for c in range(DC)])

                def scores_c(p, u):
                    pe.wait_ge(pjc_out, (b * 8 + p) * NPC + NKT + 1 + ONE)
                    scores(C, b * H + 2 * p + u, u, lambda k, w: keyC[:, k * 512:k * 512 + w])

                def values_c(g, u, p):
                    pe.wait_ge(pjc_out, (b * 8 + p) * NPC + NPC + ONE)
                    values(C, scoreC, g, u, lambda k: valC[:, k, 64 * u:64 * u + 64])

                keys_c(0)
                scores_c(0, 0)
                values_p(0)
                scores_c(0, 1)
                values_c(b * H, 0, 0)
                with pe.Fori(1, 8) as p:
                    keys_c(p)
                    scores_c(p, 0)
                    values_c(b * H + 2 * p - 1, 1, p - 1)
                    values_p(p)
                    scores_c(p, 1)
                    values_c(b * H + 2 * p, 0, p)
                values_c(b * H + H - 1, 1, 7)
                post_pe(pe, b, 1)
            ln_pe(6, 4)
            pe.wait_ge(ln_out, 5 * DC)
            pe.wait_ge(sw_in, 7 * 16)
            for m in range(DC):
                for c in range(DC):
                    mm = pe.matmul(SP_[m][:, :], swq[:, c, m * P:(m + 1) * P], XT[:, c, :],
                                   start=(c == 0), stop=(c == DC - 1))
                mm.then_inc(sq_mm, 1)
            for c in range(DC):
                mm = pe.matmul(PJ[0][:, :], swk[:, c, :], XT[:, c, :], start=(c == 0), stop=(c == DC - 1))
            mm.then_inc(skv_mm, 1)
            for t in range(NT4):
                for c in range(DC):
                    pe.matmul(PJ[1][:, t * 64:t * 64 + 64], XT[:, c, t * P:(t + 1) * P], swv[:, c, :],
                              start=(c == 0), stop=False)
                pe.matmul(PJ[1][:, t * 64:t * 64 + 64], ones[0:1, :], sbv, start=False, stop=True).then_inc(skv_mm, 1)
            pe.wait_ge(sq_out, DC)
            pe.wait_ge(skv_out, 1 + NT4)
            for t in range(NT4):
                b = t // QT
                for h2 in range(H // 2):
                    n = t * 8 + h2
                    pe.wait_ge(s_q, 2 * h2 + 2)
                    if n >= 3:
                        pe.wait_ge(s_ev, n - 2)
                    for hh in range(2):
                        mm = pe.matmul(SP_[n % 3][:, hh * S:(hh + 1) * S], sQ[:, 2 * h2 + hh, t * P:(t + 1) * P],
                                       sK[:, b * S:(b + 1) * S], start=True, stop=True)
                    mm.then_inc(s_mm, 1)
            for n, (t, h) in enumerate((t, h) for t in range(NT4) for h in range(H)):
                nb = t % QT + 1
                pe.wait_ge(s_ex, n + 1)
                if n >= 2:
                    pe.wait_ge(s_tc, n - 1)
                for k in range(nb):
                    mm = pe.transpose(TP[n % 2][:, k * P:(k + 1) * P], sS[:, t, h, k * P:(k + 1) * P], ident[:, :])
                mm.then_inc(s_t, 1)
                if n >= 1:
                    self_weigh(pe, n - 1)
            self_weigh(pe, NT4 * H - 1)
            for c in range(DC):
                pe.wait_ge(s_on, NT4)
                pe.wait_ge(s_tc, NT4 * H)
                for t in range(NT4):
                    mm = pe.transpose(TP[c][:, t * P:(t + 1) * P], sO[:, t, c * P:(c + 1) * P], ident[:, :])
                mm.then_inc(s_ot, 1)
            pe.wait_ge(s_oc, DC)
            for t in range(NT4):
                for c in range(DC):
                    pe.matmul(RB[t][:, 0:D], sOT[:, c, t * P:(t + 1) * P], swo[:, c, :], start=(c == 0), stop=False)
                pe.matmul(RB[t][:, 0:D], ones[0:1, :], sbo, start=False, stop=True).then_inc(s_y, 1)
            ln_pe(7, 5)
            pe.wait_ge(ln_out, 6 * DC)
            pe.wait_ge(fw_in, 7 * 16)
            for t in range(NT4):
                for c in range(DC):
                    pe.matmul(OP[:, t * E8:(t + 1) * E8], XT[:, c, t * P:(t + 1) * P], fgw[:, c, :],
                              start=(c == 0), stop=False)
                pe.matmul(OP[:, t * E8:(t + 1) * E8], ones[0:1, :], fbg, start=False, stop=True).then_inc(f_lg, 1)
            for n in range(2 * E8):
                if n >= 4:
                    pe.wait_ge(f_ge, n - 3)
                for c in range(DC):
                    mm = pe.matmul(RB[n % 4][:, :], w1[:, c, n * P:(n + 1) * P], XT[:, c, :],
                                   start=(c == 0), stop=(c == DC - 1))
                mm.then_inc(f_h, 1)
            for n in range(NT4 * E8):
                t, e = n % NT4, n // NT4
                pe.wait_ge(f_ge, 2 * E8)
                if n >= 4:
                    pe.wait_ge(f_acc, n - 3)
                for c in range(DC):
                    pe.matmul(RB[n % 4][:, 0:D], hT[:, e, c, t * P:(t + 1) * P], w2[:, e, c, :],
                              start=(c == 0), stop=False)
                pe.matmul(RB[n % 4][:, 0:D], ones[0:1, :], b2r[:, e * D:(e + 1) * D],
                          start=False, stop=True).then_inc(f_y, 1)

        @block.vector
        def _(dve):
            def ln_dve(k, src):
                for t in range(NT4):
                    dve.bn_stats(stats[:, t, :], src[:, t, :]).then_inc(ln_stat, 1)
                for t in range(NT4):
                    dve.wait_ge(ln_stat, NT4 * k + t + 1)
                    dve.bn_aggr(mv[:, t, :], stats[:, t, :]).then_inc(ln_aggr, 1)
                dve.wait_ge(ln_aggr, NT4 * (k + 1))
                dve.wait_ge(ln_std, k + 1)
                dve.reciprocal(rstd[:, :], std[:, :]).then_inc(ln_rstd, 1)
                dve.wait_ge(ln_rstd, k + 1)
                for t in range(NT4):
                    dve.tensor_scalar(XN[:, t, :], src[:, t, :], mv[:, t, 0:1], rstd[:, t:t + 1],
                                      ALU.subtract, ALU.mult).then_inc(ln_norm, 1)

            def taken(at, score, g, u, mask=None):
                L = len(at.tiles)
                for t in range(QT):
                    for k, w in enumerate(at.tiles):
                        n = t * L + k
                        dve.wait_ge(at.scored, g * at.ns + n + 1 + ONE)
                        if mask is not None:
                            dve.sem_inc(waited, 1)
                        dst = score[:, u, t, k * 512:k * 512 + w]
                        if mask is not None:
                            dve.tensor_tensor_reduce(dst, SP_[n % 3][:, 0:w], mask[:, t, k * 512:k * 512 + w], 1.0,
                                                     NEG, ALU.add, ALU.max, mpart[:, u, t, k:k + 1])\
                                .then_inc(at.score_out, 1)
                        else:
                            dve.tensor_scalar(dst, SP_[n % 3][:, 0:w], 0.0, NEG, ALU.add, ALU.max,
                                              accum_out=mpart[:, u, t, k:k + 1]).then_inc(at.score_out, 1)
                    dve.wait_ge(at.score_out, g * at.ns + (t + 1) * L + ONE)
                    dve.tensor_reduce(nmax[:, u, t:t + 1], mpart[:, u, t, 0:L], AX.X, ALU.max, negate=True)\
                        .then_inc(at.max_ready, 1)

            def turned(at, g, h):
                for n in range(1, at.nt, 2):
                    dve.wait_ge(at.turned, g * at.nt + n + 1)
                    dve.wait_ge(at.weighed, g * at.nt + (0 if n < 4 else n - 3) + ONE)
                    dve.tensor_copy(PT[:, n % 4, :], TP[1][:, :]).then_inc(at.turned_dve, 1)
                dve.wait_ge(at.weighed, g * at.nt + at.nt + ONE)
                dve.tensor_copy(OA[:, bass.ds(h, 1), :].rearrange("p a k -> p (a k)"), OP[:, 0:S])\
                    .then_inc(at.out_taken, 1)

            for s_ in (A.score_out, C.score_out, A.turned_dve, C.turned_dve, A.out_taken, C.out_taken):
                dve.sem_inc(s_, ONE)
            dve.wait_ge(x_in, 16)
            ln_dve(0, X)
            dve.wait_ge(cols_in, 64)
            for m in range(DC):
                dve.wait_ge(qa_mm, m + 1)
                dve.tensor_scalar(QTR[:, m, :], PJ[m][:, :], cols[:, C_BQ + m:C_BQ + m + 1], 0.25,
                                  ALU.add, ALU.mult).then_inc(qa_out, 1)

            dve.wait_ge(scan_in, 48)
            done = [0]

            def tap(ins):
                done[0] += 1
                ins.then_inc(taps, 1)
                dve.wait_ge(taps, done[0])

            tap(dve.tensor_copy(kW[:, 0, :, :], kB))
            tap(dve.tensor_copy(kV[:, 0, :, :], kC))
            mv_tmp = kT[:, 0:512].rearrange("p (h a c) -> p h a c", h=2, a=NST)
            base = done[0]
            with dve.Fori(0, TAU - 1) as j:
                dve.wait_ge(taps, base + 2 * j)
                dve.tensor_tensor(mv_tmp, kA.rearrange("p h n m -> p h m n"),
                                  kW[:, bass.ds(j, 1), :, :].rearrange("p j h n -> p (j h) n").unsqueeze(2)
                                  .broadcast_to([P, 2, NST, NST]), ALU.mult).then_inc(taps, 1)
                dve.wait_ge(taps, base + 2 * j + 1)
                dve.tensor_reduce(kW[:, bass.ds(j + 1, 1), :, :].rearrange("p j h n -> p (j h) n"), mv_tmp, AX.X, ALU.add)\
                    .then_inc(taps, 1)
            done[0] += 2 * (TAU - 1)
            dve.wait_ge(taps, done[0])
            sq_tmp = kT.rearrange("p (n m k) -> p n m k", n=NST, m=NST)
            cur = kA
            for s_ in range(4):
                nxt = kP[:, s_ % 2, :, :, :]
                for h in range(2):
                    tap(dve.tensor_tensor(sq_tmp, cur[:, h, :, :].unsqueeze(2).broadcast_to([P, NST, NST, NST]),
                                          cur[:, h, :, :].rearrange("p k m -> p m k").unsqueeze(1)
                                          .broadcast_to([P, NST, NST, NST]), ALU.mult))
                    tap(dve.tensor_reduce(nxt[:, h, :, :], sq_tmp, AX.X, ALU.add))
                cur = nxt
            base2 = done[0]
            with dve.Fori(0, TAU - 1) as j:
                dve.wait_ge(taps, base2 + 2 * j)
                dve.tensor_tensor(mv_tmp, cur,
                                  kV[:, bass.ds(j, 1), :, :].rearrange("p j h n -> p (j h) n").unsqueeze(2)
                                  .broadcast_to([P, 2, NST, NST]), ALU.mult).then_inc(taps, 1)
                dve.wait_ge(taps, base2 + 2 * j + 1)
                dve.tensor_reduce(kV[:, bass.ds(j + 1, 1), :, :].rearrange("p j h n -> p (j h) n"), mv_tmp, AX.X, ALU.add)\
                    .then_inc(taps, 1)
            done[0] += 2 * (TAU - 1)
            dve.wait_ge(taps, done[0])
            for h in range(2):
                tap(dve.tensor_tensor(sq_tmp, kV[:, :, h, :].unsqueeze(2).broadcast_to([P, TAU, TAU, NST]),
                                      kW[:, :, h, :].unsqueeze(1).broadcast_to([P, TAU, TAU, NST]), ALU.mult))
                tap(dve.tensor_reduce(KC[:, h, :].rearrange("p (i j) -> p i j", i=TAU), sq_tmp, AX.X, ALU.add))
            assert done[0] == TAPS_DONE, done[0]

            with dve.Fori(0, B) as b:
                dve.wait_ge(mask_in, 32 * b + 32)
                dve.wait_ge(pja_out, b * NPJ + RING + NPJ)
                for t in range(QT):
                    dve.tensor_scalar(maskb[:, t, :], maskw[:, t, :], 0.0, NEG, ALU.is_equal, ALU.mult)\
                        .then_inc(mask_ready, 1)
                dve.wait_ge(mask_ready, 2 * b + 2)
                taken(A, scoreA, b * H, 0, maskb)
                with dve.Fori(0, H - 2, 2) as i:
                    for u in range(2):
                        taken(A, scoreA, b * H + i + u + 1, 1 - u, maskb)
                        turned(A, b * H + i + u, i + u)
                taken(A, scoreA, b * H + H - 1, 1, maskb)
                turned(A, b * H + H - 2, H - 2)
                turned(A, b * H + H - 1, H - 1)
                post_dve(dve, b, 0)

            ln_dve(1, X)
            dve.wait_ge(pad_zero, 1)
            for m in range(DC):
                dve.wait_ge(gate_act, m + 1)
                dve.tensor_tensor(XG[:, m, :, S:2 * S], XT[:, m, :].rearrange("p (b k) -> p b k", b=B),
                                  GT[:, m, :].rearrange("p (b k) -> p b k", b=B), ALU.mult).then_inc(gated, 1)
            dve.wait_ge(gated, DC)
            dve.wait_ge(cols_in, 64)
            for m in range(DC):
                dve.tensor_scalar(Y[:, 0, m, :, :], XG[:, m, :, S:2 * S], cols[:, C_DP + m:C_DP + m + 1], None,
                                  ALU.mult).then_inc(conv, 1)
                dve.wait_ge(conv, 2 * m + 1)
                dve.tensor_tensor(Y[:, 0, m, :, :], Y[:, 0, m, :, :], XG[:, m, :, S:2 * S], ALU.add).then_inc(conv, 1)
                dve.memset(Y[:, 1, m, :, :], 0.0).then_inc(gated, 1)
            dve.wait_ge(conv, 4)
            dve.wait_ge(gated, 2 * DC)
            c0 = 4
            for blk in range(S // KB):
                L = S - blk * KB
                with dve.Fori(0, KB // 2) as k2:
                    k = 2 * k2
                    back = k2 * (-2) + S
                    for aa in range(2):
                        for m in range(DC):
                            dve.wait_ge(conv, c0 + blk * KB * 2 + 2 * k + 2 * aa + m - 3)
                            dve.scalar_tensor_tensor(
                                out=Y[:, aa, m, :, blk * KB:S],
                                in0=XG[:, m, :, bass.ds(back - aa, L)],
                                scalar=KC[:, m, bass.ds(k + (blk * KB + aa), 1)],
                                in1=Y[:, aa, m, :, blk * KB:S],
                                op0=ALU.mult, op1=ALU.add).then_inc(conv, 1)
            dve.wait_ge(conv, c0 + 2 * S)
            for m in range(DC):
                dve.tensor_tensor(Y[:, 0, m, :, :], Y[:, 0, m, :, :], Y[:, 1, m, :, :], ALU.add).then_inc(conv, 1)
            dve.wait_ge(y_norm, NT4)
            dve.wait_ge(gate_w_in, 48)
            ln_dve(2, YT)
            for t in range(NT4):
                dve.wait_ge(ln_norm, NT4 * 2 + t + 1)
                dve.tensor_tensor(XN[:, t, :], XN[:, t, :], gamma_r, ALU.mult).then_inc(scan_done, 1)
                dve.wait_ge(scan_done, 3 * t + 1)
                dve.tensor_tensor(XN[:, t, :], XN[:, t, :], beta_r, ALU.add).then_inc(scan_done, 1)
                dve.wait_ge(scan_done, 3 * t + 2)
                dve.tensor_tensor(X[:, t, :], X[:, t, :], XN[:, t, :], ALU.add).then_inc(scan_done, 1)
            dve.wait_ge(scan_done, 3 * NT4)

            def gate_steps(Gt, iota, chain, logits, first, second):
                n = [0]

                def st(ins):
                    n[0] += 1
                    ins.then_inc(chain, 1)
                    dve.wait_ge(chain, n[0])

                def wide(v):
                    return v.broadcast_to([P, NT4, E8])

                def pick(src, hot, tmp, col):
                    mxv = Gt[:, col, :, 0:1]
                    st(dve.tensor_reduce(mxv, src, AX.X, ALU.max))
                    st(dve.tensor_tensor(tmp, src, wide(mxv), ALU.is_equal))
                    st(dve.tensor_tensor(tmp, tmp, iota.unsqueeze(1).broadcast_to([P, NT4, E8]), ALU.mult))
                    st(dve.tensor_reduce(Gt[:, col, :, 1:2], tmp, AX.X, ALU.min))
                    st(dve.tensor_tensor(hot, iota.unsqueeze(1).broadcast_to([P, NT4, E8]), wide(Gt[:, col, :, 1:2]),
                                         ALU.is_equal))
                    return mxv

                lg = Gt[:, 0, :, :]
                st(dve.tensor_copy(lg.rearrange("p t e -> p (t e)"), logits))
                m1 = pick(lg, Gt[:, 1, :, :], Gt[:, 2, :, :], 9)
                if not second:
                    return n[0]
                st(dve.tensor_scalar(Gt[:, 3, :, :], Gt[:, 1, :, :], NEG, None, ALU.mult))
                st(dve.tensor_tensor(Gt[:, 4, :, :], lg, Gt[:, 3, :, :], ALU.add))
                pick(Gt[:, 4, :, :], Gt[:, 5, :, :], Gt[:, 2, :, :], 10)
                st(dve.tensor_tensor(Gt[:, 6, :, :], Gt[:, 1, :, :], Gt[:, 5, :, :], ALU.add))
                st(dve.tensor_tensor(Gt[:, 7, :, :], lg, wide(m1), ALU.subtract))
                return n[0]

            ln_dve(3, X)
            dve.wait_ge(moe_lg, NT4)
            n_ = gate_steps(G, iot, moe_g, OP[:, 0:NT4 * E8], True, True)
            assert n_ == MG_NEG, n_
            dve.wait_ge(moe_g, n_ + 1)
            dve.tensor_tensor(G[:, 2, :, :], G[:, 8, :, :], G[:, 6, :, :], ALU.mult).then_inc(moe_g, 1)
            dve.wait_ge(moe_g, n_ + 2)
            dve.tensor_reduce(G[:, 11, :, 0:1], G[:, 2, :, :], AX.X, ALU.add).then_inc(moe_g, 1)
            dve.wait_ge(moe_g, n_ + 3)
            dve.reciprocal(G[:, 11, :, 1:2], G[:, 11, :, 0:1]).then_inc(moe_g, 1)
            dve.wait_ge(moe_g, n_ + 4)
            dve.tensor_tensor(G[:, 12, :, :], G[:, 2, :, :], G[:, 11, :, 1:2].broadcast_to([P, NT4, E8]), ALU.mult)\
                .then_inc(moe_g, 1)
            dve.wait_ge(moe_g, n_ + 5)
            for n in range(NT4 * 4):
                t, e2 = n // 4, n % 4
                dve.wait_ge(moe_mm, n + 1)
                for ee in range(2):
                    if n + ee:
                        dve.wait_ge(moe_acc, 2 * n + ee)
                    dve.scalar_tensor_tensor(out=X[:, t, :], in0=RB[n % 4][:, ee * D:(ee + 1) * D],
                                             scalar=G[:, 12, t, 2 * e2 + ee:2 * e2 + ee + 1], in1=X[:, t, :],
                                             op0=ALU.mult, op1=ALU.add).then_inc(moe_acc, 1)
            dve.wait_ge(moe_acc, 2 * NT4 * 4)
            ln_dve(4, X)
            dve.wait_ge(ln_norm, NT4 * 5)
            ln_dve(5, XN)
            dve.wait_ge(ln_turn, 4 * DC)
            with dve.Fori(0, B) as b:
                with dve.Fori(0, 8) as i:
                    e = b * 8 + i
                    dve.wait_ge(tile_in, e * 16 + 16)
                    for t in range(4):
                        dve.bn_stats(stats[:, t, :], ctile[:, t, :]).then_inc(tile_st, 1)
                    for t in range(4):
                        dve.wait_ge(tile_st, e * 4 + t + 1)
                        dve.sem_inc(waited, 1)
                        dve.bn_aggr(mv[:, t, :], stats[:, t, :]).then_inc(tile_ag, 1)
                    dve.wait_ge(tile_ag, e * 4 + 4)
                    dve.wait_ge(tile_sq, e + 1)
                    dve.reciprocal(rstd[:, :], std[:, :]).then_inc(tile_rs, 1)
                    dve.wait_ge(tile_rs, e + 1)
                    dve.wait_ge(tile_turn, e * 2 + ONE)
                    for t in range(4):
                        dve.tensor_scalar(cnorm[:, t, :], ctile[:, t, :], mv[:, t, 0:1], rstd[:, t:t + 1],
                                          ALU.subtract, ALU.mult).then_inc(tile_norm, 1)
                taken(C, scoreC, b * H, 0)
                taken(C, scoreC, b * H + 1, 1)
                turned(C, b * H, 0)
                with dve.Fori(1, 8) as p:
                    taken(C, scoreC, b * H + 2 * p, 0)
                    turned(C, b * H + 2 * p - 1, 2 * p - 1)
                    taken(C, scoreC, b * H + 2 * p + 1, 1)
                    turned(C, b * H + 2 * p, 2 * p)
                turned(C, b * H + H - 1, H - 1)
                post_dve(dve, b, 1)
            ln_dve(6, X)
            dve.wait_ge(sw_in, 7 * 16)
            for m in range(DC):
                dve.wait_ge(sq_mm, m + 1)
                dve.tensor_scalar(QTR[:, m, :], SP_[m][:, :], cols[:, C_SQ + m:C_SQ + m + 1], 0.25,
                                  ALU.add, ALU.mult).then_inc(sq_out, 1)
            for t in range(NT4):
                for h2 in range(H // 2):
                    n = t * 8 + h2
                    dve.wait_ge(s_mm, n + 1)
                    dve.tensor_tensor(sS[:, t, 2 * h2:2 * h2 + 2, :],
                                      SP_[n % 3][:, :].rearrange("p (a k) -> p a k", a=2),
                                      smask[:, t % QT, :].unsqueeze(1).broadcast_to([P, 2, S]), ALU.add)\
                        .then_inc(s_ev, 1)
                dve.wait_ge(s_ev, (t + 1) * 8)
                dve.tensor_reduce(smx[:, t, :], sS[:, t, :, :], AX.X, ALU.max, negate=True).then_inc(s_nm, 1)
            for n, (t, h) in enumerate((t, h) for t in range(NT4) for h in range(H)):
                nb = t % QT + 1
                dve.wait_ge(s_t, n + 1)
                if n >= 4:
                    dve.wait_ge(s_pv, n - 3)
                dve.tensor_copy(sPT[:, n % 4, 0:nb * P], TP[n % 2][:, 0:nb * P]).then_inc(s_tc, 1)
                if h == H - 1:
                    self_norm(dve, t)
            for t in range(NT4):
                dve.wait_ge(s_y, t + 1)
                dve.tensor_tensor(X[:, t, :], X[:, t, :], RB[t][:, 0:D], ALU.add).then_inc(s_x, 1)
            dve.wait_ge(s_x, NT4)
            ln_dve(7, X)
            dve.wait_ge(f_lg, NT4)
            gate_steps(G2, iot2, f_g, OP[:, 0:NT4 * E8], True, False)
            for n in range(NT4 * E8):
                t, e = n % NT4, n // NT4
                dve.wait_ge(f_y, n + 1)
                if n >= NT4:
                    dve.wait_ge(f_acc, n - NT4 + 1)
                dve.scalar_tensor_tensor(out=X[:, t, :], in0=RB[n % 4][:, 0:D], scalar=G2[:, 1, t, e:e + 1],
                                         in1=X[:, t, :], op0=ALU.mult, op1=ALU.add).then_inc(f_acc, 1)


def kernel(**inputs):
    import numpy as np
    import concourse.bacc as bacc
    from concourse import mybir as mb
    from concourse.bass_utils import run_bass_kernel_spmd as run

    v = {k: np.asarray(x) for k, x in inputs.items()}

    def rows(w):
        return np.ascontiguousarray(w.reshape(2, 128, -1).transpose(1, 0, 2))

    def col(x):
        return x.reshape(-1, 128).T

    f = np.float32
    p = np.arange(128)
    order = np.arange(256).reshape(4, 4, 16).transpose(1, 0, 2).reshape(-1)
    twice = np.concatenate([np.arange(64), np.arange(64)])
    selA = np.zeros((128, 8, 128), f)
    for j in range(8):
        for d in range(16):
            selA[d::32, j, 16 * j + d] = 1
    selC = np.zeros((128, 2, 128), f)
    for u in range(2):
        for d in range(64):
            selC[d::64, u, 64 * u + d] = 1
    h16 = np.arange(16)
    i, j = np.arange(256)[:, None], np.arange(256)[None, :]
    smask = np.where((i - 128 >= j) | (i < j), f(NEG), f(0)).astype(f).reshape(2, 128, 256).transpose(1, 0, 2)
    arrays = {
        "x": v["x"], "ctx": v["ctx_1024"], "ctxT": np.ascontiguousarray(v["ctx_1024"].transpose(0, 2, 1)),
        "mask": v["mask_BxSxS2_ik1"],
        "WqT": rows(v["L0_xattn_Wq"].T), "WkT": rows(v["L0_xattn_Wk"].T), "WvT": rows(v["L0_xattn_Wv"].T),
        "WoT": rows(v["L0_xattn_Wo"].T), "bo": v["L0_xattn_bo"][None, :],
        "cols": np.concatenate([col(v[n]) for n in (
            "L0_xattn_bq", "L0_xattn_bk", "L0_xattn_bv", "L0_attn_bg", "L0_attn_Dp", "L1_xattn_ln1_g",
            "L1_xattn_ln1_b", "L1_xattn_ln2_g", "L1_xattn_ln2_b")]
            + [col(v["L1_attn_bq"][order]), col(v["L1_attn_bk"][twice]), np.zeros((128, 1), f)], 1),
        "sel16": (p[:, None] // 16 == h16[None, :] % 8).astype(f),
        "sel64": (p[:, None] // 64 == np.arange(2)[None, :]).astype(f),
        "selA": selA, "hselA": (h16[:, None, None] == 8 * np.arange(2)[None, :, None] + p[None, None, :] // 16).astype(f),
        "selC": selC, "hselC": (h16[:, None, None] == 2 * np.arange(8)[None, :, None] + p[None, None, :] // 64).astype(f),
        "A": v["L0_attn_A"].reshape(2, 128, 16, 16).transpose(1, 0, 2, 3),
        "Bp": rows(v["L0_attn_Bp"]), "Cp": rows(v["L0_attn_Cp"]),
        "WgT": rows(v["L0_attn_Wg"].T),
        "gamma": np.broadcast_to(v["L0_attn_gamma"], (128, 256)), "beta": np.broadcast_to(v["L0_attn_beta"], (128, 256)),
        "ew": v["L0_ffn_expert_w"].reshape(8, 2, 128, 256).transpose(2, 1, 0, 3).reshape(128, 2, 2048),
        "eb": v["L0_ffn_expert_b"].reshape(1, 2048), "gwT": rows(v["L0_ffn_gate_w"].T), "gb": v["L0_ffn_gate_b"][None, :],
        "iota": np.broadcast_to(np.arange(8, dtype=f) - 8, (128, 8)),
        "WqC": v["L1_xattn_Wq"].reshape(2, 128, 8, 128).transpose(2, 1, 0, 3),
        "WkC": v["L1_xattn_Wkv"][:, :1024].reshape(2, 128, 8, 128).transpose(2, 1, 0, 3),
        "WvC": v["L1_xattn_Wkv"][:, 1024:].reshape(2, 128, 8, 128).transpose(2, 1, 0, 3),
        "WoC": v["L1_xattn_Wo"].reshape(8, 128, 256).transpose(1, 0, 2),
        "sWq": rows(v["L1_attn_Wq"][:, order]), "sWk": rows(v["L1_attn_Wk"][:, twice]), "sWv": rows(v["L1_attn_Wv"]),
        "sWo": rows(v["L1_attn_Wo"]), "sbv": v["L1_attn_bv"][None, :], "sbo": v["L1_attn_bo"][None, :], "smask": smask,
        "fWg": rows(v["L1_ffn_Wg"]), "fbg": v["L1_ffn_bg"][None, :],
        "W1": v["L1_ffn_W1"].reshape(8, 2, 128, 256).transpose(2, 1, 0, 3).reshape(128, 2, 2048),
        "fb1": v["L1_ffn_b1"].reshape(16, 128).T,
        "W2": v["L1_ffn_W2"].reshape(8, 2, 128, 256).transpose(2, 0, 1, 3), "b2": v["L1_ffn_b2"].reshape(1, 2048),
    }
    arrays = {k: np.ascontiguousarray(x) for k, x in arrays.items()}
    nc = bacc.Bacc("TRN2", target_bir_lowering=False, num_devices=1)
    aps = {k: nc.dram_tensor(k + "_dram", x.shape, mb.dt.from_np(x.dtype), kind="ExternalInput").ap()
           for k, x in arrays.items()}
    res = nc.dram_tensor("result_dram", (2, 256, 256), mb.dt.float32, kind="ExternalOutput").ap()
    program(nc, aps, res)
    r = run(nc, [{k + "_dram": x for k, x in arrays.items()}], core_ids=[0])
    return r.results[0]["result_dram"]
```

```python
from contextlib import ExitStack

import concourse.bass as bass
from concourse import mybir
from concourse.alu_op_type import AluOpType as ALU

ACT = mybir.ActivationFunctionType
AX = mybir.AxisListType
F32 = mybir.dt.float32
BF16 = mybir.dt.bfloat16
I32 = mybir.dt.int32

P = 128
B = 2
S = 256
QT = S // P
NT4 = B * QT
D = 256
DC = D // P
S2 = 4096
H = 16
NEG = -3.0e38
EPS = 1e-5
E8 = 8
RING = 4
NPK = 16
NPJ = 16
QK_IN = 6 * 16
NKT = 9
NPC = NKT + 1 + 9
SCL = 64 ** -0.25
ONE = 1
MG_NEG = 15
TAU = 16
NBK = S // TAU
TAP_OPS = 10
NST = 16


class Attention:

    def __init__(self, sem, name, keys, width, ct, ring, units, by_dve):
        self.tiles = [min(512, keys - k) for k in range(0, keys, 512)]
        self.keys = keys
        self.width = width
        self.ct = ct
        self.chunks = keys // P
        self.ns = QT * len(self.tiles)
        self.nt = self.chunks // 2 // units
        self.out = units
        self.ring = ring
        self.by_dve = by_dve
        self.by_act = [n for n in range(self.nt) if n not in by_dve]
        self.na = len(self.by_act)
        self.nd = len(by_dve)
        self.scored = sem(name + "_scored")
        self.free_scores, self.free_places, self.free_out, self.free_act, self.free_dve = (
            (ONE,) * 5 if units == 1 else (2, 4, units, self.na, self.nd))
        self.score_out = sem(name + "_score_out")
        self.max_ready = sem(name + "_max_ready")
        self.exp_done = sem(name + "_exp_done")
        self.turned = sem(name + "_turned")
        self.turned_act = sem(name + "_turned_act")
        self.turned_dve = sem(name + "_turned_dve")
        self.weighed = sem(name + "_weighed")
        self.out_taken = sem(name + "_out_taken")

    def copied(self, g, n, before=0):
        if n in self.by_dve:
            return self.turned_dve, g * self.nd + (self.by_dve.index(n) + 1 + before * self.nd + self.free_dve)
        return self.turned_act, g * self.na + (self.by_act.index(n) + 1 + before * self.na + self.free_act)


def program(nc, a, out):
    with ExitStack() as ctx:
        def sb(name, shape, dt=F32):
            return ctx.enter_context(nc.sbuf_tensor(name, shape, dt))

        def sem(name):
            return ctx.enter_context(nc.semaphore(name))

        RX = sb("RX", [P, 8192])
        RK = sb("RK", [P, 8192])
        RV = sb("RV", [P, 8192])
        RS = sb("RS", [P, 2 * 2 * 4352])
        PT = sb("PT", [P, 4, 512])
        OA = sb("OA", [P, H, S])
        X = sb("X", [P, NT4, D])
        QTR = RS[:, 16384:17408].rearrange("p (m k) -> p m k", m=DC)
        WA = sb("WA", [P, 3, DC, D])
        QR = sb("QR", [P, S + 2 * NST * NST + (2 * TAU + 1) * 2 * NST])
        ident = sb("ident", [P, P])
        ones = sb("ones", [1, P])
        sel16 = sb("sel16", [P, H])
        sel64 = sb("sel64", [P, 2])
        mpart = sb("mpart", [P, 2, QT, 9])
        nmax = sb("nmax", [P, 2, QT])
        den = sb("den", [P, QT, H])
        dpart = sb("dpart", [P, QT, H * 4])
        rden = sb("rden", [P, QT, H])
        cols = sb("cols", [P, 32])
        mv = sb("mv", [P, NT4, 2])
        std = sb("std", [P, NT4])
        rstd = sb("rstd", [P, NT4])
        stats = sb("stats", [P, NT4, 6])

        def bank(name):
            return ctx.enter_context(nc.psum_tensor(name, [P, 512], F32))

        SP_ = [bank(f"score_bank{i}") for i in range(3)]
        TP = [bank(f"turn_bank{i}") for i in range(2)]
        OP = bank("out_bank")
        PJ = [bank(f"proj_bank{i}") for i in range(2)]

        XN = OA[:, 0:4, :]
        XT = OA[:, 4:8, :].rearrange("p (c u) s -> p c (u s)", c=DC)
        ctxT = RX[:, :].rearrange("p (c k) -> p c k", c=DC)
        keyS = RK[0:6 * 16, 0:4096].bitcast(BF16).rearrange("p (u k) -> p u k", u=2)
        qryS = QR[0:6 * 16, 0:S].bitcast(BF16).rearrange("p (u k) -> p u k", u=2)
        QP = QR[:, 0:2 * S].rearrange("p (u k) -> p u k", u=2)
        parts = RK[:, 4096:7168].bitcast(BF16).rearrange("p (s g k) -> p s g k", s=4, g=3)
        rest = RK[:, 7168:8192].rearrange("p (s k) -> p s k", s=2)
        val = RV[:, :].rearrange("p (k d) -> p k d", d=D)
        maskb = RX[:, 0:4096].bitcast(BF16).rearrange("p (t k) -> p t k", t=QT)
        VH = RX[:, 4096:6144].rearrange("p (u k d) -> p u k d", u=2, d=32)
        selA = RX[:, 6144:7168].rearrange("p (j c) -> p j c", j=8)
        hselA = RX[0:H, 7168:7424].rearrange("p (m c) -> p m c", m=2)
        scoreA = RS[:, 0:16384].rearrange("p (u t k) -> p u t k", u=2, t=QT)
        maskw = RS[:, 8192:16384].bitcast(I32).rearrange("p (t k) -> p t k", t=QT)
        scoreC = RS[:, :].rearrange("p (u t k) -> p u t k", u=2, t=QT)
        BOR = RX[0:1, 7424:7680]
        RB = [TP[0], TP[1], PJ[0], PJ[1]]
        OT = [OP, SP_[2]]
        recT = PT[0:H, 0, 0:S]
        ON = RS[:, 0:2048].rearrange("p (j k) -> p j k", j=8)
        OC = RS[:, 2048:4096].rearrange("p (j k) -> p j k", j=8)
        ctile = RX[:, 0:4096].rearrange("p (s t d) -> p s t d", s=4, t=4)
        cnorm = RX[:, 4096:6144].rearrange("p (s t d) -> p s t d", s=2, t=4)
        cturn = RX[:, 6144:8192].rearrange("p (s c k) -> p s c k", s=2, c=DC)
        cstats = RV[:, 7712:7808].rearrange("p (s t n) -> p s t n", s=4, t=4)
        cmv = RV[:, 7808:7840].rearrange("p (s t n) -> p s t n", s=4, t=4)
        cstd = RV[:, 7840:7856].rearrange("p (s t) -> p s t", s=4)
        crstd = RV[:, 7856:7872].rearrange("p (s t) -> p s t", s=4)
        cshift = RV[:, 7872:7888].rearrange("p (s t) -> p s t", s=4)
        xlT = RX[:, :].rearrange("p (c k) -> p c k", c=DC)
        keyC = RK[:, 0:4352]
        latT = RK[:, 4352:4864].rearrange("p (c k) -> p c k", c=DC)
        wq = RK[:, 4864:5120].rearrange("p (c n) -> p c n", c=DC)
        wk = RK[:, 5120:5376].rearrange("p (c n) -> p c n", c=DC)
        wv = RK[:, 5376:5632].rearrange("p (c n) -> p c n", c=DC)
        qC = RK[:, 5632:5888]
        latAll = RK[:, 5888:6912].rearrange("p (c k) -> p c k", c=DC)
        valC = RV[:, 0:4352].rearrange("p (k d) -> p k d", d=P)
        woC = RV[:, 4352:6400].rearrange("p (j n) -> p j n", n=D)
        selC = RV[:, 6400:6656].rearrange("p (u c) -> p u c", u=2)
        hselC = RV[0:H, 6656:7680].rearrange("p (j c) -> p j c", j=8)

        key_parts = nc.dram_tensor("key_parts", (B, DC, 3, P, S2), BF16, kind="Internal").ap()
        xl_dram = nc.dram_tensor("context_normed", (B * 8, P, DC, 512), F32, kind="Internal").ap()
        qry_parts = nc.dram_tensor("query_parts", (DC, 3, P, B * S), BF16, kind="Internal").ap()

        block = ctx.enter_context(nc.Block())

        A = Attention(sem, "a", S2, 32, 4, 4, QT, [3, 6])
        C = Attention(sem, "c", S2 + S, 64, 2, 2, 1, list(range(1, 17, 2)))

        x_in, wqa_in, wa_in, cols_in = sem("x_in"), sem("wqa_in"), sem("wa_in"), sem("cols_in")
        scan_in = sem("scan_in")
        consts = sem("consts")
        ctx_in, mask_in, sela_in = sem("ctx_in"), sem("mask_in"), sem("sela_in")
        ln_stat, ln_aggr, ln_std, ln_rstd = sem("ln_stat"), sem("ln_aggr"), sem("ln_std"), sem("ln_rstd")
        ln_norm, ln_turn, ln_out = sem("ln_norm"), sem("ln_turn"), sem("ln_out")
        qa_mm, qa_out, qa_r, qa_m, qa_l, qa_d = [sem("qa_" + n) for n in ("mm", "out", "rest", "mid", "low", "dram")]
        qa_h = sem("qa_high")
        q_ready = sem("q_ready")
        den_sum = sem("den_sum")
        ks_in = [sem(f"head_in_{u}") for u in range(2)]
        kp_mm, kp_h, kp_r, kp_m, kp_l = [sem("keys_" + n) for n in ("mm", "high", "rest", "mid", "low")]
        kp_d = [sem(f"keys_dram_{e}") for e in range(4)]
        pja_mm, pja_out = sem("pja_mm"), sem("pja_out")
        mask_ready = sem("mask_ready")
        vh_zero, vh_ready = sem("vh_zero"), sem("vh_ready")
        pa_rden, pa_rt, pa_rtc, pa_sum, pa_oc, pa_on, pa_y, pa_x = [sem("post_" + n) for n in (
            "recip", "recip_turned", "recip_in_sbuf", "summed", "sum_in_sbuf", "normed", "projected", "added")]
        taps = sem("taps")
        gate_w_in, gate_mm, gate_act, gated = sem("gate_w_in"), sem("gate_mm"), sem("gate_act"), sem("gated")
        conv, y_turn, y_norm, scan_done = sem("conv"), sem("y_turn"), sem("y_norm"), sem("scan_done")
        reversed_ = sem("scan_reversed")
        y_done = sem("y_done")
        moe_w_in, moe_lg, moe_g, moe_mm, moe_acc = (
            sem("moe_w_in"), sem("moe_logits"), sem("moe_gate"), sem("moe_mm"), sem("moe_acc"))
        lat_done = sem("lat_done")
        cw_in, cpost_in = sem("cw_in"), sem("cpost_in")
        tile_in = [sem(f"tile_in_{i}") for i in range(4)]
        tile_shift, tile_norm_act = sem("tile_shift"), sem("tile_norm_act")
        tile_kept = [sem(f"tile_stored_{i}") for i in range(2)]
        xl_in = sem("context_in")
        tile_norm, tile_turn, tile_out, tile_st = (
            sem("tile_norm"), sem("tile_turn"), sem("tile_out"), sem("tile_stat"))
        tile_ag, tile_sq, tile_rs = sem("tile_aggr"), sem("tile_std"), sem("tile_rstd")
        lat_copy = sem("lat_copy")
        wqc_in, wkc_in, wvc_in = sem("wqc_in"), sem("wkc_in"), sem("wvc_in")
        pjc_mm, pjc_out = sem("pjc_mm"), sem("pjc_out")
        sw_in, sq_mm, sq_out, skv_mm, skv_out = [sem("self_" + n) for n in ("w_in", "q_mm", "q_out", "kv_mm", "kv_out")]
        s_q, s_mm, s_ev, s_nm, s_ex, s_t, s_tc, s_pv, s_on, s_rd, s_ot, s_oc, s_y, s_x = [
            sem("self_" + n) for n in ("q", "scored", "score_out", "max", "exp", "turned", "turned_out", "weighed",
                                       "normed", "recip", "out_turned", "out_in_sbuf", "projected", "added")]
        fw_in, f_lg, f_g, f_h, f_ge, f_y, f_acc = [sem("ffn_" + n) for n in (
            "w_in", "logits", "gate", "hidden", "gelu", "mm", "acc")]
        stored = sem("stored")
        waited = sem("waited")

        C_BQ, C_BK, C_BV, C_BG, C_DP, C_G1, C_B1, C_G2, C_B2 = range(0, 18, 2)
        C_SQ, C_SK = 18, 20

        wgT = RV[:, 4096:4608].rearrange("p (c n) -> p c n", c=DC)
        gamma_r, beta_r = RV[:, 4608:4864], RV[:, 4864:5120]
        GT = RV[:, 5120:6144].rearrange("p (m k) -> p m k", m=DC)
        XG = RK[:, 0:1024].rearrange("p (m b k) -> p m b k", m=DC, b=B)
        Y = RK[:, 2048:3072].rearrange("p (m b k) -> p m b k", m=DC, b=B)
        YT = RV[:, 6144:7168].rearrange("p (t d) -> p t d", t=NT4)
        ew = RV[:, 0:4096].rearrange("p (c n) -> p c n", c=DC)
        ebr = RK[0:1, 4096:6144]
        gw = RV[:, 7168:7184].rearrange("p (c n) -> p c n", c=DC)
        gbr = RV[0:1, 7184:7192]
        iot = RV[:, 7192:7200]
        G = RV[:, 7200:7712].rearrange("p (n t e) -> p n t e", n=16, t=NT4)
        swq = RX[:, 0:512].rearrange("p (c n) -> p c n", c=DC)
        swk = RX[:, 512:768].rearrange("p (c n) -> p c n", c=DC)
        swv = RX[:, 768:896].rearrange("p (c n) -> p c n", c=DC)
        swo = RX[:, 896:1408].rearrange("p (c n) -> p c n", c=DC)
        sbv = RX[0:1, 1408:1472]
        sbo = RX[0:1, 1472:1728]
        smask = RX[:, 1728:2240].rearrange("p (t k) -> p t k", t=QT)
        sK = RX[:, 2240:2752]
        sV = RX[:, 2752:3008].rearrange("p (t d) -> p t d", t=NT4)
        sQ = RK[:, 0:8192].rearrange("p (h k) -> p h k", h=H)
        sS = RS[:, 0:16384].rearrange("p (t h k) -> p t h k", t=NT4, h=H)
        sPT = RV[:, 0:1024].rearrange("p (n k) -> p n k", n=4)
        sO = RV[:, 1024:2048].rearrange("p (t d) -> p t d", t=NT4)
        sOT = RV[:, 2048:3072].rearrange("p (c k) -> p c k", c=DC)
        smx = RV[:, 3072:3136].rearrange("p (t h) -> p t h", t=NT4)
        sden = RV[:, 3136:3200].rearrange("p (t h) -> p t h", t=NT4)
        srd = RV[:, 3200:3264].rearrange("p (t h) -> p t h", t=NT4)
        w1 = RV[:, 4096:8192].rearrange("p (c n) -> p c n", c=DC)
        w2 = RX[:, 4096:8192].rearrange("p (e c n) -> p e c n", e=E8, c=DC)
        b2r = PT[0:1, :, :].rearrange("p a b -> p (a b)")
        fgw = RX[:, 3008:3024].rearrange("p (c n) -> p c n", c=DC)
        fbg = RX[0:1, 3024:3032]
        fb1 = RX[:, 3040:3056]
        iot2 = RX[:, 3056:3064]
        G2 = RX[:, 3072:3584].rearrange("p (n t e) -> p n t e", n=16, t=NT4)
        hT = RK[:, 0:8192].rearrange("p (e c k) -> p e c k", e=E8, c=DC)

        kA = QR[:, S:S + 512].rearrange("p (h a c) -> p h a c", h=2, a=NST)
        kU = QR[:, S + 512:].rearrange("p (j h n) -> p j h n", h=2, n=NST)
        kP = RS[:, 16384:17408].rearrange("p (s n m) -> p s n m", s=4, n=NST)
        kT = rest.rearrange("p s k -> p (s k)")
        kTv = kT[:, 0:512].rearrange("p (h a c) -> p h a c", h=2, a=NST)
        kTs = kT.rearrange("p (n m k) -> p n m k", n=4, m=NST)
        kW = RS[:, 10784:11296].rearrange("p (j h n) -> p j h n", h=2, n=NST)
        K16 = RS[:, 11296:11328].rearrange("p (j h) -> p j h", h=2)
        terms = [RS[:, 4096 * i:4096 * i + (NBK - 1) * TAU * NST].rearrange("p (c a n) -> p c a n", c=NBK - 1, a=TAU)
                 for i in range(2)]
        ST = RS[:, 8192:9152].rearrange("p (m c b n) -> p m c b n", m=DC, c=NBK - 1, b=B)
        st_terms = RS[:, 9216:10240].rearrange("p (m b a n) -> p m b a n", m=DC, b=B, a=NST)
        st_sums = RS[:, 10240:10304].rearrange("p (m b a) -> p m b a", m=DC, b=B)
        y_sums = RS[:, 10304:10784].rearrange("p (i c j) -> p i c j", i=2, c=NBK - 1)

        def ctx_views(b):
            return a["ctxT"][bass.ds(b, 1), :, :].rearrange("b (c p) k -> p (b c) k", p=P)

        def groups(second):
            return 8 if second else 2

        def normed_before(b, second):
            return b * 8 + 4 * B if second else b * 4

        def post_pe(pe, b, second):
            k = b + B * second
            at = C if second else A
            pe.wait_ge(at.out_taken, (b * H + H) * at.out + at.free_out)
            if second:
                pe.wait_ge(cpost_in, 48)
            else:
                pe.wait_ge(sela_in, 48 * b + 48)
            pe.wait_ge(pa_rden, k + 1)
            for t in range(QT):
                mm = pe.transpose(TP[0][0:H, t * P:(t + 1) * P], rden[:, t, :], ident[:, :])
            mm.then_inc(pa_rt, 1)
            pe.wait_ge(pa_rtc, k + 1)
            for j in range(groups(second)):
                if j >= 2:
                    pe.wait_ge(pa_on, normed_before(b, second) + j - 1)
                pe.matmul(PJ[j % 2][:, 0:S], (hselC if second else hselA)[:, j, :], recT, start=True, stop=True)
                n = 2 if second else 8
                for u in range(n):
                    mm = pe.matmul(SP_[j % 2][:, 0:S], (selC if second else selA)[:, u, :], OA[:, n * j + u, :],
                                   start=(u == 0), stop=(u == n - 1))
                mm.then_inc(pa_sum, 1)
            pe.wait_ge(pa_on, normed_before(b, second) + (8 if second else 4))
            for t in range(QT):
                for j in range(groups(second)):
                    mm = pe.matmul(TP[t][:, 0:D], ON[:, j, t * P:(t + 1) * P], woC[:, j, :] if second else WA[:, 2, j, :],
                                   start=(j == 0), stop=bool(second and j == 7))
                if not second:
                    mm = pe.matmul(TP[t][:, 0:D], ones[0:1, :], BOR, start=False, stop=True)
                mm.then_inc(pa_y, 1)
            pe.wait_ge(pa_x, QT * k + QT)

        def post_act(act, b, second):
            k = b + B * second
            act.wait_ge(pa_rt, k + 1)
            act.activation(recT, TP[0][0:H, 0:S], ACT.Copy).then_inc(pa_rtc, 1)
            before = b * 8 + 2 * B if second else b * 2
            for j in range(groups(second)):
                act.wait_ge(pa_sum, before + j + 1)
                act.activation(OC[:, j, :], SP_[j % 2][:, 0:S], ACT.Copy).then_inc(pa_oc, 1)

        def post_dve(dve, b, second):
            k = b + B * second
            if not second:
                dve.wait_ge(A.exp_done, (b * H + H) * QT * 4)
                dve.tensor_reduce(den[:, :, :], dpart[:, :, :].rearrange("p t (h q) -> p t h q", q=4), AX.X, ALU.add)\
                    .then_inc(den_sum, 1)
                dve.wait_ge(den_sum, b + 1)
            dve.reciprocal(rden[:, :, :], den[:, :, :]).then_inc(pa_rden, 1)
            before = b * 8 + 2 * B if second else b * 2
            for j in range(groups(second)):
                dve.wait_ge(pa_oc, before + j + 1)
                dve.tensor_tensor(ON[:, j, :], OC[:, j, :], PJ[j % 2][:, 0:S], ALU.mult).then_inc(pa_on, 1)
                if not second:
                    dve.wait_ge(pa_on, b * 4 + 2 * j + 1)
                    dve.tensor_scalar(ON[:, j, :], ON[:, j, :], cols[:, C_BV + j:C_BV + j + 1], None, ALU.add)\
                        .then_inc(pa_on, 1)
            for t in range(QT):
                dve.wait_ge(pa_y, QT * k + t + 1)
                x = X[:, bass.ds(b * QT + t, 1), :].rearrange("p a d -> p (a d)")
                dve.tensor_tensor(x, x, TP[t][:, 0:D], ALU.add).then_inc(pa_x, 1)
            dve.wait_ge(pa_x, QT * k + QT)

        def self_weigh(pe, n):
            t, h = divmod(n, H)
            nb = t % QT + 1
            pe.wait_ge(s_tc, n + 1)
            if h == 0 and t >= 2:
                pe.wait_ge(s_on, t - 1)
            for k in range(nb):
                mm = pe.matmul([OP, PJ[0]][t % 2][:, h * 16:h * 16 + 16], sPT[:, n % 4, k * P:(k + 1) * P],
                               sV[:, t // QT * QT + k, (h // 4) * 16:(h // 4) * 16 + 16], start=(k == 0), stop=(k == nb - 1))
            mm.then_inc(s_pv, 1)

        def self_norm(dve, t):
            dve.wait_ge(s_pv, (t + 1) * H)
            dve.reciprocal(srd[:, t, :], sden[:, t, :]).then_inc(s_rd, 1)
            dve.wait_ge(s_rd, t + 1)
            dve.tensor_tensor(sO[:, t, :].rearrange("p (h d) -> p h d", h=H),
                              [OP, PJ[0]][t % 2][:, 0:D].rearrange("p (h d) -> p h d", h=H),
                              srd[:, t, :].unsqueeze(2).broadcast_to([P, H, 16]), ALU.mult).then_inc(s_on, 1)

        @block.sync
        def _(sp):
            def load(dst, name, s_):
                return sp.dma_start(dst, a[name]).then_inc(s_, 16)

            sp.dma_start(X[:, :, :], a["x"].rearrange("b (t p) d -> p (b t) d", p=P)).then_inc(x_in, 16)
            for e in range(4):
                sp.sem_inc(kp_d[e], 16)
            load(RV[:, 0:512].rearrange("p (c n) -> p c n", c=DC), "WqT", wqa_in)
            load(WA[:, 0, :, :], "WkT", wa_in)
            load(WA[:, 1, :, :], "WvT", wa_in)
            load(WA[:, 2, :, :], "WoT", wa_in)
            load(cols[:, 0:22], "cols", cols_in)
            load(sel16[:, :], "sel16", cols_in)
            load(sel64[:, :], "sel64", cols_in)
            load(kP[:, 0:2, :, :], "A", scan_in)
            for m in range(DC):
                sp.wait_ge(qa_out, (m + 1) * 5)
                sp.dma_start(qry_parts[m].rearrange("g p k -> p g k"), parts[:, 2 + m, :, :]).then_inc(qa_d, 16)
            sp.wait_ge(qa_d, 32)
            with sp.Fori(0, B) as b:
                sp.wait_ge(A.out_taken, b * H * QT + A.free_out)
                for c in range(DC):
                    for k in range(2):
                        sp.dma_start(ctxT[:, c, 2048 * k:2048 * k + 2048],
                                     ctx_views(b)[:, c, 2048 * k:2048 * k + 2048]).then_inc(ctx_in, 16)
                for t in range(QT):
                    sp.dma_start(maskw[:, t, :], a["mask"][bass.ds(b, 1), t * P:(t + 1) * P, :]
                                 .rearrange("b p k -> p (b k)")).then_inc(mask_in, 16)
                sp.wait_ge(taps, b * H * TAP_OPS + ONE)
                sp.dma_start(kA, a["AA"][bass.ds(b, 1), :, :, :, :].rearrange("b p h n m -> p (b h) n m"))\
                    .then_inc(scan_in, 16)
                sp.dma_start(kU[:, bass.ds(b * TAU, 1), :, :], a["BC"][bass.ds(b, 1), :, :, :]
                             .rearrange("b p h n -> p b h n")).then_inc(scan_in, 16)
                with sp.Fori(0, NPK // 4) as i:
                    for e in range(4):
                        sp.wait_ge(kp_l, b * NPK + i * 4 + e + 1 + 2)
                        sp.dma_start(key_parts[bass.ds(b, 1), e % 2, :, :, bass.ds(i * 1024 + (e // 2) * 512, 512)]
                                     .rearrange("b g p k -> p (b g) k"), parts[:, e, :, :]).then_inc(kp_d[e], 16)
                for e in range(4):
                    sp.wait_ge(kp_d[e], 64 * b + 64 + 16)

                def head_in(h, u):
                    row = (h % 8) * 16
                    for n, (lo, hi) in enumerate(((0, 3), (0, 2), (0, 1))):
                        p0, p1 = (0, 48, 80)[n], (48, 80, 96)[n]
                        sp.dma_start(keyS[p0:p1, u, :],
                                     key_parts[bass.ds(b, 1), bass.ds(h // 8, 1), lo:hi, bass.ds(row, 16), :]
                                     .rearrange("a m g p k -> (a m g) p k")).then_inc(ks_in[u], 16)
                        sp.dma_start(qryS[p0:p1, u, :],
                                     qry_parts[bass.ds(h // 8, 1), n:n + 1, bass.ds(row, 16), bass.ds(b * S, S)]
                                     .rearrange("m g p k -> (m g) p k").broadcast_to([hi, 16, S])).then_inc(ks_in[u], 16)

                head_in(0, 0)
                head_in(1, 1)
                sp.wait_ge(pja_out, b * NPJ + RING + NPJ)
                sp.dma_start(selA, a["selA"]).then_inc(sela_in, 16)
                sp.dma_start(hselA, a["hselA"]).then_inc(sela_in, 16)
                sp.dma_start(BOR, a["bo"]).then_inc(sela_in, 16)
                with sp.Fori(1, H // 2) as p:
                    for u in range(2):
                        sp.wait_ge(A.scored, (b * H + 2 * p + u - 1) * A.ns + ONE)
                        head_in(2 * p + u, u)
                sp.wait_ge(pa_x, QT * b + QT)
                sp.sem_inc(waited, 1)

            load(wgT, "WgT", gate_w_in)
            load(gamma_r, "gamma", gate_w_in)
            load(beta_r, "beta", gate_w_in)
            load(ew, "ew", moe_w_in)
            load(ebr, "eb", moe_w_in)
            load(gw, "gwT", moe_w_in)
            load(gbr, "gb", moe_w_in)
            load(iot, "iota", moe_w_in)
            ctx_t = a["ctx"].rearrange("b (t p) d -> (b t) p d", p=P)

            def tile_load(i, u):
                sp.dma_start(ctile[:, u, :, :], ctx_t[bass.ds(i * 4, 4), :, :].rearrange("t p d -> p t d"))\
                    .then_inc(tile_in[u], 16)

            def tile_store(i, u):
                sp.wait_ge(tile_out, i * 2 + DC + 4)
                sp.dma_start(xl_dram[bass.ds(i, 1), :, :, :].rearrange("a p c k -> p (a c) k"), cturn[:, u, :, :])\
                    .then_inc(tile_kept[u], 16)

            for u in range(2):
                sp.sem_inc(tile_kept[u], 16)
            for u in range(4):
                tile_load(u, u)
            with sp.Fori(0, B * 2 - 1) as i:
                for u in range(4):
                    sp.wait_ge(tile_norm, (4 * i + u) * 2 + 2)
                    sp.wait_ge(tile_norm_act, (4 * i + u) * 2 + 2)
                    tile_load(4 * i + u + 4, u)
                    tile_store(4 * i + u, u % 2)
            for u in range(4):
                tile_store(B * 8 - 4 + u, u % 2)
            for u in range(2):
                sp.wait_ge(tile_kept[u], 16 * (B * 4 + 1))

            def pair_w(w, dst, name, p):
                sp.dma_start(dst, a[name][bass.ds(p, 1), :, :, :].rearrange("a p c n -> p (a c) n")).then_inc(w, 16)

            def context_in(b):
                for k in range(8):
                    sp.dma_start(xlT[:, :, 512 * k:512 * k + 512], xl_dram[b * 8 + k]).then_inc(xl_in, 16)

            context_in(0)
            sp.wait_ge(moe_acc, 2 * NT4 * 4)
            load(woC, "WoC", cpost_in)
            load(selC, "selC", cpost_in)
            load(hselC, "hselC", cpost_in)
            for b in range(B):
                with sp.Fori(0, 8) as p:
                    sp.wait_ge(pjc_out, (b * 8 + p) * NPC + ONE)
                    pair_w(wqc_in, wq, "WqC", p)
                    pair_w(wkc_in, wk, "WkC", p)
                    pair_w(wvc_in, wv, "WvC", p)
                if b + 1 < B:
                    sp.wait_ge(pjc_out, (b + 1) * 8 * NPC + ONE)
                    context_in(b + 1)
            sp.wait_ge(pa_x, QT * (2 * B))
            load(swq, "sWq", sw_in)
            load(swk, "sWk", sw_in)
            load(swv, "sWv", sw_in)
            load(swo, "sWo", sw_in)
            load(sbv, "sbv", sw_in)
            load(sbo, "sbo", sw_in)
            load(smask, "smask", sw_in)
            load(w1, "W1", fw_in)
            load(w2, "W2", fw_in)
            load(b2r, "b2", fw_in)
            load(fgw, "fWg", fw_in)
            load(fbg, "fbg", fw_in)
            load(fb1, "fb1", fw_in)
            load(iot2, "iota", fw_in)
            sp.wait_ge(f_acc, NT4 * E8)
            sp.dma_start(out.rearrange("b (t p) d -> p (b t) d", p=P), X[:, :, :]).then_inc(stored, 16)
            sp.wait_ge(stored, 16)

        @block.gpsimd
        def _(pool):
            pool.sem_inc(kp_l, 2)
            pool.sem_inc(taps, ONE)
            pool.memset(ident[:, :], 0.0).then_inc(consts, 1)
            pool.memset(ones[:, :], 1.0).then_inc(consts, 1)
            pool.wait_ge(consts, 2)
            pool.affine_select(out=ident[:, :], in_=ident[:, :], compare_op=ALU.not_equal, fill=1.0, base=0,
                               pattern=[[-1, P]], channel_multiplier=1).then_inc(consts, 1)
            def values_a(h, u):
                pool.tensor_copy(VH[:, u, :, 0:16], val[:, :, bass.ds(h * 16, 16)]).then_inc(vh_ready, 1)

            with pool.Fori(0, B) as b:
                with pool.Fori(0, NPK // 4) as i:
                    for e in range(4):
                        pool.wait_ge(kp_m, b * NPK + i * 4 + e + 1)
                        pool.sem_inc(waited, 1)
                        pool.tensor_tensor(parts[:, e, 2, :], rest[:, e % 2, :], parts[:, e, 1, :], ALU.subtract)\
                            .then_inc(kp_l, 1)
                pool.wait_ge(pja_out, b * NPJ + RING + NPJ)
                pool.sem_inc(waited, 1)
                pool.memset(VH[:, :, :, 16:32], 0.0).then_inc(vh_zero, 1)
                values_a(0, 0)

                def tap(n, ins_of):
                    pool.wait_ge(taps, n + ONE)
                    pool.sem_inc(waited, 1)
                    ins_of().then_inc(taps, 1)

                def fold(n, t, out_):
                    w = NST // 2
                    while w:
                        lo, hi = t[..., 0:w], t[..., w:2 * w]
                        dst = lo if w > 1 else out_.unsqueeze(len(lo.shape) - 1)
                        tap(n, lambda: pool.tensor_tensor(dst, lo, hi, ALU.add))
                        n = n + 1
                        w //= 2

                def weights(h, s_, d_, r_):
                    n = (b * H + h) * TAP_OPS
                    src = kU[:, bass.ds(b * TAU + h, 1), :, :].rearrange("p j h n -> p (j h) n")
                    dst = kU[:, bass.ds(b * TAU + h + 1, 1), :, :].rearrange("p j h n -> p (j h) n")
                    tap(n, lambda: pool.tensor_tensor(kTv, kA, src.unsqueeze(2).broadcast_to([P, 2, NST, NST]), ALU.mult))
                    fold(n + 1, kTv, dst)
                    power = kP[:, bass.ds(s_, 1), :, :].rearrange("p s n m -> p (s n) m")
                    square = kP[:, bass.ds(d_, 1), 4 * r_:4 * r_ + 4, :].rearrange("p s n m -> p (s n) m")
                    tap(n + 5, lambda: pool.tensor_tensor(
                        kTs, power[:, 4 * r_:4 * r_ + 4, :].unsqueeze(2).broadcast_to([P, 4, NST, NST]),
                        power.rearrange("p k m -> p m k").unsqueeze(1).broadcast_to([P, 4, NST, NST]), ALU.mult))
                    fold(n + 6, kTs, square)

                def step(h, u, s_, d_, r_):
                    g = b * H + h
                    pool.wait_ge(A.weighed, g * QT * A.nt + A.free_places)
                    pool.sem_inc(waited, 1)
                    values_a(h + 1, 1 - u)
                    weights(h, s_, d_, r_)

                pool.wait_ge(scan_in, 32 * b + 48)
                pool.sem_inc(waited, 1)
                pool.wait_ge(kp_l, b * NPK + NPK + 2)
                pool.sem_inc(waited, 1)
                with pool.Fori(0, 2) as i:
                    for r_ in range(4):
                        step(4 * i + r_, r_ % 2, i, i + 2, r_)
                for r_ in range(7):
                    step(8 + r_, r_ % 2, 2 + r_ // 4, r_ // 4, r_ % 4)
                weights(15, 3, 1, 3)

            pool.wait_ge(pa_x, QT * B)
            pool.wait_ge(taps, B * H * TAP_OPS + ONE)
            for j in range(TAU):
                pool.tensor_copy(kW[:, j, :, :], kU[:, TAU - 1 - j, :, :]).then_inc(reversed_, 1)

            with pool.Fori(0, B * 2) as i:
                for u in range(4):
                    for t in range(2):
                        pool.wait_ge(tile_rs, 4 * i + u + 1)
                        pool.wait_ge(tile_turn, (4 * i + u) * 2 + 1)
                        pool.sem_inc(waited, 1)
                        pool.tensor_scalar(cnorm[:, u % 2, t, :], ctile[:, u, t, :], cmv[:, u, t, 0:1],
                                           crstd[:, u, t:t + 1], ALU.subtract, ALU.mult).then_inc(tile_norm, 1)
            pool.wait_ge(cols_in, 48)
            with pool.Fori(0, B) as b:
                with pool.Fori(0, 8) as p:
                    pool.wait_ge(pjc_out, (b * 8 + p) * NPC + NKT + 1 + ONE)
                    for u in range(2):
                        pool.tensor_tensor(QP[:, u, :], qC, sel64[:, u:u + 1].broadcast_to([P, S]), ALU.mult)\
                            .then_inc(q_ready, 1)

            pool.wait_ge(sq_out, DC)
            for h in range(H):
                s_, g = h % 4, h // 4
                pool.tensor_tensor(sQ[:, h, :], QTR[:, s_ // 2, :],
                                   sel16[:, 4 * (s_ % 2) + g:4 * (s_ % 2) + g + 1].broadcast_to([P, B * S]),
                                   ALU.mult).then_inc(s_q, 1)

        @block.scalar
        def _(act):
            def ln_sqrt(k):
                act.wait_ge(ln_aggr, NT4 * (k + 1))
                if k:
                    act.wait_ge(ln_rstd, k)
                act.activation(std[:, :], mv[:, :, 1], ACT.Sqrt, bias=EPS).then_inc(ln_std, 1)

            def ln_evac(k, gain=None, shift=None):
                for c in range(DC):
                    act.wait_ge(ln_turn, DC * k + c + 1)
                    kw = {} if gain is None else dict(scale=cols[:, gain + c:gain + c + 1],
                                                      bias=cols[:, shift + c:shift + c + 1])
                    act.activation(XT[:, c, :], TP[c][:, :], ACT.Identity if kw else ACT.Copy, **kw).then_inc(ln_out, 1)

            def exps(at, score, g, h, u):
                for t in range(QT):
                    act.wait_ge(at.max_ready, 2 * g + t + 1)
                    act.activation(score[:, u, t, :], score[:, u, t, :], ACT.Exp, bias=nmax[:, u, t:t + 1],
                                   accum_out=den[:, t, bass.ds(h, 1)]).then_inc(at.exp_done, 1)

            def turned(at, g):
                for n in at.by_act:
                    act.wait_ge(at.turned, g * at.nt + n + 1)
                    act.wait_ge(at.weighed, g * at.nt + (0 if n < 4 else n - 3) + ONE)
                    act.activation(PT[:, n % 4, :], RB[n % at.ring][:, :], ACT.Copy).then_inc(at.turned_act, 1)

            act.sem_inc(pja_out, RING)
            act.sem_inc(A.turned_act, A.free_act)
            act.sem_inc(C.turned_act, C.free_act)
            act.sem_inc(pjc_out, ONE)
            act.sem_inc(tile_out, 4)
            act.wait_ge(cols_in, 48)
            ln_sqrt(0)
            ln_evac(0)
            act.wait_ge(qa_d, 32)
            with act.Fori(0, B) as b:
                with act.Fori(0, NPK // 4) as i:
                    def high(e):
                        act.wait_ge(kp_mm, b * NPK + i * 4 + e + 1)
                        act.wait_ge(kp_d[e], (b * 4 + i + 1) * 16)
                        act.activation(parts[:, e, 0, :], RB[e][:, :], ACT.Identity,
                                       bias=cols[:, C_BK + e % 2:C_BK + e % 2 + 1]).then_inc(kp_h, 1)

                    def middle(e):
                        act.wait_ge(kp_r, b * NPK + i * 4 + e + 1 + 4)
                        act.activation(parts[:, e, 1, :], rest[:, e % 2, :], ACT.Copy).then_inc(kp_m, 1)

                    high(0)
                    high(1)
                    middle(0)
                    high(2)
                    middle(1)
                    high(3)
                    middle(2)
                    middle(3)
                for n in range(NPJ):
                    act.wait_ge(pja_mm, b * NPJ + n + 1)
                    act.activation(val[:, 2 * n:2 * n + 2, :].rearrange("p k d -> p (k d)"), RB[n % 4][:, :],
                                   ACT.Copy).then_inc(pja_out, 1)

                def exp_quarter(h, u, t, q):
                    g = b * H + h
                    act.wait_ge(A.max_ready, QT * g + t + 1)
                    act.activation(scoreA[:, u, t, q * 1024:(q + 1) * 1024], scoreA[:, u, t, q * 1024:(q + 1) * 1024],
                                   ACT.Exp, bias=nmax[:, u, t:t + 1],
                                   accum_out=dpart[:, t, bass.ds(h * 4 + q, 1)]).then_inc(A.exp_done, 1)

                def unit(h, u, t, last=False):
                    y = QT * (b * H + h) + t
                    for n in range(A.nt):
                        if n in A.by_act:
                            act.wait_ge(A.turned, y * A.nt + n + 1)
                            act.wait_ge(A.weighed, y * A.nt + n + 1)
                            act.activation(PT[:, n % 4, :], RB[n % 4][:, :], ACT.Copy).then_inc(A.turned_act, 1)
                        if n % 2 == 0 and not last:
                            if t + 1 < QT:
                                exp_quarter(h, u, t + 1, n // 2)
                            else:
                                exp_quarter(h + 1, 1 - u, 0, n // 2)

                for q in range(4):
                    exp_quarter(0, 0, 0, q)
                with act.Fori(0, H - 2, 2) as i:
                    for u in range(2):
                        for t in range(QT):
                            unit(i + u, u, t)
                for h in range(H - 2, H):
                    for t in range(QT):
                        unit(h, h % 2, t, last=(h == H - 1 and t == QT - 1))
                post_act(act, b, 0)

            ln_sqrt(1)
            ln_evac(1)
            for m in range(DC):
                act.wait_ge(gate_mm, m + 1)
                act.activation(GT[:, m, :], PJ[m][:, :], ACT.Sigmoid, bias=cols[:, C_BG + m:C_BG + m + 1])\
                    .then_inc(gate_act, 1)
            def tile_turned(e, u):
                for c in range(DC):
                    act.wait_ge(tile_turn, e * 2 + c + 1 + 4)
                    act.wait_ge(tile_kept[u], e // 2 * 16 + 16)
                    act.activation(cturn[:, u, c, :], RB[2 * u + c][:, :], ACT.Identity,
                                   scale=cols[:, C_G1 + c:C_G1 + c + 1],
                                   bias=cols[:, C_B1 + c:C_B1 + c + 1]).then_inc(tile_out, 1)

            def tile_normed(e, u, first=False):
                act.wait_ge(tile_ag, (e + 1) * 4)
                act.activation(cstd[:, u, :], cmv[:, u, :, 1], ACT.Sqrt, bias=EPS).then_inc(tile_sq, 1)
                for t in range(2, 4):
                    act.wait_ge(tile_shift, e + 1)
                    act.wait_ge(tile_turn, e * 2 + 1)
                    act.activation(cnorm[:, u % 2, t, :], ctile[:, u, t, :], ACT.Identity, scale=crstd[:, u, t:t + 1],
                                   bias=cshift[:, u, t:t + 1]).then_inc(tile_norm_act, 1)

            tile_normed(0, 0)
            with act.Fori(0, B * 2 - 1) as i:
                for u in range(4):
                    tile_normed(4 * i + u + 1, (u + 1) % 4)
                    tile_turned(4 * i + u, u % 2)
            for u in range(4):
                if u < 3:
                    tile_normed(B * 8 - 3 + u, u + 1)
                tile_turned(B * 8 - 4 + u, u % 2)
            for t in range(NT4):
                act.wait_ge(y_turn, 2 * t + 2)
                act.activation(YT[:, t, :], SP_[t % 2][:, 0:D], ACT.Copy).then_inc(y_norm, 1)
            ln_sqrt(2)
            ln_sqrt(3)
            ln_evac(2)
            act.wait_ge(moe_g, MG_NEG)
            act.activation(G[:, 8, :, :], G[:, 7, :, :], ACT.Exp).then_inc(moe_g, 1)
            ln_sqrt(4)
            ln_sqrt(5)
            ln_evac(3, C_G2, C_B2)
            act.wait_ge(ln_out, 8)
            for c in range(DC):
                act.activation(latAll[:, c, :], XT[:, c, :], ACT.Copy).then_inc(lat_done, 1)
            with act.Fori(0, B) as b:
                act.wait_ge(lat_done, DC)
                act.activation(latT, latAll[:, :, bass.ds(b * S, S)], ACT.Copy).then_inc(lat_copy, 1)

                def keys_c(p):
                    e0 = (b * 8 + p) * NPC
                    for n in range(NKT):
                        w = C.tiles[n]
                        act.wait_ge(pjc_mm, e0 + n + 1)
                        act.activation(keyC[:, n * 512:n * 512 + w], PJ[n % 2][:, 0:w], ACT.Copy, scale=SCL)\
                            .then_inc(pjc_out, 1)
                    act.wait_ge(pjc_mm, e0 + NKT + 1)
                    act.activation(qC, PJ[NKT % 2][:, 0:S], ACT.Copy, scale=SCL).then_inc(pjc_out, 1)

                def values_c(p):
                    e0 = (b * 8 + p) * NPC + NKT + 1
                    for n in range(9):
                        w = 4 if n < 8 else 2
                        act.wait_ge(pjc_mm, e0 + n + 1)
                        act.activation(valC[:, 4 * n:4 * n + w, :].rearrange("p k d -> p (k d)"),
                                       PJ[(NKT + 1 + n) % 2][:, 0:w * P], ACT.Copy).then_inc(pjc_out, 1)

                keys_c(0)
                values_c(0)
                exps(C, scoreC, b * H, 0, 0)
                turned(C, b * H)
                with act.Fori(1, 8) as p:
                    keys_c(p)
                    exps(C, scoreC, b * H + 2 * p - 1, 2 * p - 1, 1)
                    turned(C, b * H + 2 * p - 1)
                    values_c(p)
                    exps(C, scoreC, b * H + 2 * p, 2 * p, 0)
                    turned(C, b * H + 2 * p)
                exps(C, scoreC, b * H + H - 1, H - 1, 1)
                turned(C, b * H + H - 1)
                post_act(act, b, 1)
            ln_sqrt(6)
            ln_evac(4)
            act.wait_ge(skv_mm, 1)
            act.activation(sK, PJ[0][:, :], ACT.Identity, bias=cols[:, C_SK:C_SK + 1]).then_inc(skv_out, 1)
            for t in range(NT4):
                act.wait_ge(skv_mm, 1 + NT4)
                act.activation(sV[:, t, :], PJ[1][:, t * 64:t * 64 + 64], ACT.Copy).then_inc(skv_out, 1)
            for t in range(NT4):
                for h in range(H):
                    act.wait_ge(s_nm, t + 1)
                    act.activation(sS[:, t, h, :], sS[:, t, h, :], ACT.Exp, bias=smx[:, t, h:h + 1],
                                   accum_out=sden[:, t, h:h + 1]).then_inc(s_ex, 1)
            for c in range(DC):
                act.wait_ge(s_ot, c + 1)
                act.activation(sOT[:, c, :], TP[c][:, :], ACT.Copy).then_inc(s_oc, 1)
            ln_sqrt(7)
            ln_evac(5)
            for n in range(2 * E8):
                act.wait_ge(f_h, n + 1)
                act.activation(hT[:, n // 2, n % 2, :], RB[n % 4][:, :], ACT.Gelu, bias=fb1[:, n:n + 1])\
                    .then_inc(f_ge, 1)

        @block.tensor
        def _(pe):
            def ln_pe(k, kx):
                pe.wait_ge(ln_norm, NT4 * (k + 1))
                if kx:
                    pe.wait_ge(ln_out, DC * kx)
                for c in range(DC):
                    for t in range(NT4):
                        mm = pe.transpose(TP[c][:, t * P:(t + 1) * P], XN[:, t, c * P:(c + 1) * P], ident[:, :])
                    mm.then_inc(ln_turn, 1)

            def scores(at, g, u, lhs, rhs):
                pe.wait_ge(at.score_out, g * at.ns + ONE)
                for t in range(QT):
                    for k, w in enumerate(at.tiles):
                        n = t * len(at.tiles) + k
                        if n >= 3:
                            pe.wait_ge(at.score_out, g * at.ns + n - 2 + ONE)
                        pe.matmul(SP_[n % 3][:, 0:w], lhs(t), rhs(k, w),
                                  start=True, stop=True).then_inc(at.scored, 1)

            def values(at, score, g, u, vals):
                def turn(n):
                    if n == 0:
                        pe.wait_ge(at.turned_act, g * at.na + ONE)
                        pe.wait_ge(at.turned_dve, g * at.nd + ONE)
                    if n >= at.ring:
                        pe.wait_ge(*at.copied(g, n - at.ring))
                    for cc in range(2):
                        for t in range(QT):
                            mm = pe.transpose(RB[n % at.ring][:, (cc * QT + t) * P:(cc * QT + t + 1) * P],
                                              score[:, u, t, (2 * n + cc) * P:(2 * n + cc + 1) * P], ident[:, :])
                    mm.then_inc(at.turned, 1)

                def weigh(n):
                    pe.wait_ge(*at.copied(g, n))
                    for cc in range(2):
                        k = 2 * n + cc
                        j = k % at.ct
                        mm = pe.matmul(OP[at.width * j:at.width * (j + 1), 0:S], vals(k),
                                       PT[:, n % 4, cc * S:(cc + 1) * S], start=k < at.ct,
                                       stop=k >= at.chunks - at.ct, skip_group_check=True)
                    mm.then_inc(at.weighed, 1)

                pe.wait_ge(at.exp_done, 2 * g + 2)
                pe.wait_ge(at.out_taken, g + ONE)
                for n in range(at.nt):
                    turn(n)
                    if n >= 2:
                        weigh(n - 2)
                weigh(at.nt - 2)
                weigh(at.nt - 1)

            pe.sem_inc(A.weighed, A.free_places)
            for s_ in (A.scored, C.scored, C.weighed):
                pe.sem_inc(s_, ONE)
            pe.sem_inc(tile_turn, 4)
            pe.wait_ge(consts, 3)
            pe.wait_ge(wqa_in, 16)
            ln_pe(0, 0)
            pe.wait_ge(ln_out, DC)
            wqa = RV[:, 0:512].rearrange("p (c n) -> p c n", c=DC)
            for m in range(DC):
                for c in range(DC):
                    mm = pe.matmul(PJ[m][:, :], wqa[:, c, m * P:(m + 1) * P], XT[:, c, :],
                                   start=(c == 0), stop=(c == DC - 1))
                mm.then_inc(qa_mm, 1)
            pe.wait_ge(wa_in, 48)
            pe.wait_ge(qa_out, 5 * DC)
            with pe.Fori(0, B) as b:
                pe.wait_ge(ctx_in, 64 * b + 64)
                pe.sem_inc(waited, 1)
                with pe.Fori(0, 4) as i:
                    for e in range(4):
                        pe.wait_ge(kp_r, b * NPK + i * 4 + e + 1)
                        for c in range(DC):
                            mm = pe.matmul(RB[e][:, :], WA[:, 0, c, (e % 2) * P:(e % 2 + 1) * P],
                                           ctxT[:, c, bass.ds(i * 1024 + (e // 2) * 512, 512)],
                                           start=(c == 0), stop=(c == DC - 1))
                        mm.then_inc(kp_mm, 1)
                for n in range(NPJ):
                    if n < 4:
                        pe.wait_ge(kp_r, b * NPK + NPK + n + 1)
                    pe.wait_ge(pja_out, b * NPJ + n + 1)
                    for kk in range(2):
                        for c in range(DC):
                            mm = pe.matmul(RB[n % 4][:, kk * D:(kk + 1) * D],
                                           ctxT[:, c, (2 * n + kk) * P:(2 * n + kk + 1) * P], WA[:, 1, c, :],
                                           start=(c == 0), stop=(c == DC - 1))
                    mm.then_inc(pja_mm, 1)
                pe.wait_ge(pja_out, b * NPJ + RING + NPJ)

                def score(h, u, t, n):
                    g = b * H + h
                    if n == 0 and t == 0:
                        pe.wait_ge(ks_in[u], (b * (H // 2) + (h - u) // 2 + 1) * QK_IN)
                    pe.wait_ge(A.score_out, g * A.ns + t * A.nt + n + 1)
                    pe.matmul(SP_[n % 2][:, :], qryS[:, u, t * P:(t + 1) * P],
                              keyS[:, u, n * 512:(n + 1) * 512], start=True, stop=True).then_inc(A.scored, 1)

                def turn(h, u, t, n):
                    y = QT * (b * H + h) + t
                    if n % 2 == 0:
                        pe.wait_ge(A.exp_done, y * 4 + n // 2 + 1)
                    if n >= 4:
                        pe.wait_ge(*A.copied(y, n - 4))
                    else:
                        pe.wait_ge(*A.copied(y, n - 4 + A.nt, -1))
                    for c in range(4):
                        mm = pe.transpose(RB[n % 4][:, c * P:(c + 1) * P],
                                          scoreA[:, u, t, (4 * n + c) * P:(4 * n + c + 1) * P], ident[:, :])
                    mm.then_inc(A.turned, 1)

                def weigh(h, u, t, n):
                    y = QT * (b * H + h) + t
                    if n == 0:
                        pe.wait_ge(A.out_taken, y + 1)
                        if t == 0:
                            pe.wait_ge(vh_zero, b + 1)
                            pe.wait_ge(vh_ready, b * H + h + 1)
                    pe.wait_ge(*A.copied(y, n))
                    for c in range(4):
                        mm = pe.matmul(OT[t][A.width * c:A.width * (c + 1), 0:P], VH[:, u, 4 * n + c, :],
                                       PT[:, n % 4, c * P:(c + 1) * P], start=n == 0, stop=n == A.nt - 1,
                                       skip_group_check=True)
                    mm.then_inc(A.weighed, 1)

                def head(h, u, first=False, last=False):
                    for t in range(QT):
                        for n in range(A.nt):
                            if not last:
                                score(h + 1, 1 - u, t, n)
                            turn(h, u, t, n)
                            if n >= 2:
                                weigh(h, u, t, n - 2)
                            elif t:
                                weigh(h, u, t - 1, n - 2 + A.nt)
                            elif not first:
                                weigh(h - 1, 1 - u, QT - 1, n - 2 + A.nt)

                for t in range(QT):
                    for n in range(A.nt):
                        score(0, 0, t, n)
                head(0, 0, first=True)
                head(1, 1)
                with pe.Fori(1, H // 2 - 1) as i:
                    for u in range(2):
                        head(2 * i + u, u)
                head(H - 2, 0)
                head(H - 1, 1, last=True)
                for n in (A.nt - 2, A.nt - 1):
                    weigh(H - 1, 1, QT - 1, n)
                post_pe(pe, b, 0)

            ln_pe(1, 1)
            pe.wait_ge(ln_out, 2 * DC)
            pe.wait_ge(gate_w_in, 48)
            for m in range(DC):
                for c in range(DC):
                    mm = pe.matmul(PJ[m][:, :], wgT[:, c, m * P:(m + 1) * P], XT[:, c, :],
                                   start=(c == 0), stop=(c == DC - 1))
                mm.then_inc(gate_mm, 1)
            pe.wait_ge(gate_act, DC)
            with pe.Fori(0, B * 4) as i:
                for u in range(2):
                    pe.wait_ge(tile_norm, (2 * i + u) * 2 + 2)
                    pe.wait_ge(tile_norm_act, (2 * i + u) * 2 + 2)
                    pe.wait_ge(tile_out, (2 * i + u) * 2 + 2)
                    for c in range(DC):
                        for t in range(4):
                            mm = pe.transpose(RB[2 * u + c][:, t * P:(t + 1) * P], cnorm[:, u, t, c * P:(c + 1) * P],
                                              ident[:, :])
                        mm.then_inc(tile_turn, 1)
            pe.wait_ge(tile_out, B * 8 * 2 + 4)
            pe.wait_ge(y_done, DC * B)
            for t in range(NT4):
                if t >= 2:
                    pe.wait_ge(y_norm, t - 1)
                for m in range(DC):
                    pe.transpose(SP_[t % 2][:, m * P:(m + 1) * P],
                                 Y[:, m, t // QT, (t % QT) * P:(t % QT + 1) * P], ident[:, :]).then_inc(y_turn, 1)
            ln_pe(3, 2)
            pe.wait_ge(ln_out, 3 * DC)
            pe.wait_ge(moe_w_in, 80)
            for t in range(NT4):
                for c in range(DC):
                    pe.matmul(OP[:, t * E8:(t + 1) * E8], XT[:, c, t * P:(t + 1) * P], gw[:, c, :],
                              start=(c == 0), stop=False)
                pe.matmul(OP[:, t * E8:(t + 1) * E8], ones[0:1, :], gbr, start=False, stop=True).then_inc(moe_lg, 1)
            for n in range(NT4 * 4):
                t, e2 = n // 4, n % 4
                if n >= 4:
                    pe.wait_ge(moe_acc, 2 * (n - 3))
                for c in range(DC):
                    pe.matmul(RB[n % 4][:, :], XT[:, c, t * P:(t + 1) * P], ew[:, c, e2 * 512:(e2 + 1) * 512],
                              start=(c == 0), stop=False)
                pe.matmul(RB[n % 4][:, :], ones[0:1, :], ebr[:, e2 * 512:(e2 + 1) * 512],
                          start=False, stop=True).then_inc(moe_mm, 1)
            pe.wait_ge(moe_acc, 2 * NT4 * 4)
            ln_pe(5, 3)
            with pe.Fori(0, B) as b:
                pe.wait_ge(xl_in, 128 * b + 128)
                pe.wait_ge(lat_copy, b + 1)

                def lhs(k, c):
                    return xlT[:, c, k * P:(k + 1) * P] if k < S2 // P else latT[:, c, (k - S2 // P) * P:(k - S2 // P + 1) * P]

                def project(p, n, mms):
                    pe.wait_ge(pjc_out, (b * 8 + p) * NPC + max(0, n - 1) + ONE)
                    for o, l, r, st, sp_ in mms:
                        mm = pe.matmul(PJ[n % 2][:, o[0]:o[1]], l, r, start=st, stop=sp_)
                    mm.then_inc(pjc_mm, 1)

                def keys_c(p):
                    pe.wait_ge(wkc_in, (b * 8 + p) * 16 + 16)
                    for n in range(NKT):
                        w = C.tiles[n]
                        project(p, n, [((0, w), wk[:, c, :], xlT[:, c, n * 512:n * 512 + w] if n < 8 else latT[:, c, :],
                                        c == 0, c == DC - 1) for c in range(DC)])
                    pe.wait_ge(wqc_in, (b * 8 + p) * 16 + 16)
                    project(p, NKT, [((0, S), wq[:, c, :], latT[:, c, :], c == 0, c == DC - 1) for c in range(DC)])

                def values_p(p):
                    pe.wait_ge(wvc_in, (b * 8 + p) * 16 + 16)
                    for n in range(9):
                        w = 4 if n < 8 else 2
                        project(p, NKT + 1 + n, [((kk * P, (kk + 1) * P), lhs(4 * n + kk, c), wv[:, c, :],
                                                  c == 0, c == DC - 1) for kk in range(w) for c in range(DC)])

                def scores_c(p, u):
                    pe.wait_ge(pjc_out, (b * 8 + p) * NPC + NKT + 1 + ONE)
                    pe.wait_ge(q_ready, b * H + 2 * p + u + 1)
                    scores(C, b * H + 2 * p + u, u, lambda t: QP[:, u, t * P:(t + 1) * P], lambda k, w: keyC[:, k * 512:k * 512 + w])

                def values_c(g, u, p):
                    pe.wait_ge(pjc_out, (b * 8 + p) * NPC + NPC + ONE)
                    values(C, scoreC, g, u, lambda k: valC[:, k, 64 * u:64 * u + 64])

                keys_c(0)
                scores_c(0, 0)
                values_p(0)
                scores_c(0, 1)
                values_c(b * H, 0, 0)
                with pe.Fori(1, 8) as p:
                    keys_c(p)
                    scores_c(p, 0)
                    values_c(b * H + 2 * p - 1, 1, p - 1)
                    values_p(p)
                    scores_c(p, 1)
                    values_c(b * H + 2 * p, 0, p)
                values_c(b * H + H - 1, 1, 7)
                post_pe(pe, b, 1)
            ln_pe(6, 4)
            pe.wait_ge(ln_out, 5 * DC)
            pe.wait_ge(sw_in, 7 * 16)
            for m in range(DC):
                for c in range(DC):
                    mm = pe.matmul(SP_[m][:, :], swq[:, c, m * P:(m + 1) * P], XT[:, c, :],
                                   start=(c == 0), stop=(c == DC - 1))
                mm.then_inc(sq_mm, 1)
            for c in range(DC):
                mm = pe.matmul(PJ[0][:, :], swk[:, c, :], XT[:, c, :], start=(c == 0), stop=(c == DC - 1))
            mm.then_inc(skv_mm, 1)
            for t in range(NT4):
                for c in range(DC):
                    pe.matmul(PJ[1][:, t * 64:t * 64 + 64], XT[:, c, t * P:(t + 1) * P], swv[:, c, :],
                              start=(c == 0), stop=False)
                pe.matmul(PJ[1][:, t * 64:t * 64 + 64], ones[0:1, :], sbv, start=False, stop=True).then_inc(skv_mm, 1)
            pe.wait_ge(sq_out, DC)
            pe.wait_ge(skv_out, 1 + NT4)
            for t in range(NT4):
                b = t // QT
                for h2 in range(H // 2):
                    n = t * 8 + h2
                    pe.wait_ge(s_q, 2 * h2 + 2)
                    if n >= 3:
                        pe.wait_ge(s_ev, n - 2)
                    for hh in range(2):
                        mm = pe.matmul(SP_[n % 3][:, hh * S:(hh + 1) * S], sQ[:, 2 * h2 + hh, t * P:(t + 1) * P],
                                       sK[:, b * S:(b + 1) * S], start=True, stop=True)
                    mm.then_inc(s_mm, 1)
            for n, (t, h) in enumerate((t, h) for t in range(NT4) for h in range(H)):
                nb = t % QT + 1
                pe.wait_ge(s_ex, n + 1)
                if n >= 2:
                    pe.wait_ge(s_tc, n - 1)
                for k in range(nb):
                    mm = pe.transpose(TP[n % 2][:, k * P:(k + 1) * P], sS[:, t, h, k * P:(k + 1) * P], ident[:, :])
                mm.then_inc(s_t, 1)
                if n >= 1:
                    self_weigh(pe, n - 1)
            self_weigh(pe, NT4 * H - 1)
            for c in range(DC):
                pe.wait_ge(s_on, NT4)
                pe.wait_ge(s_tc, NT4 * H)
                for t in range(NT4):
                    mm = pe.transpose(TP[c][:, t * P:(t + 1) * P], sO[:, t, c * P:(c + 1) * P], ident[:, :])
                mm.then_inc(s_ot, 1)
            pe.wait_ge(s_oc, DC)
            for t in range(NT4):
                for c in range(DC):
                    pe.matmul(RB[t][:, 0:D], sOT[:, c, t * P:(t + 1) * P], swo[:, c, :], start=(c == 0), stop=False)
                pe.matmul(RB[t][:, 0:D], ones[0:1, :], sbo, start=False, stop=True).then_inc(s_y, 1)
            ln_pe(7, 5)
            pe.wait_ge(ln_out, 6 * DC)
            pe.wait_ge(fw_in, 7 * 16)
            for t in range(NT4):
                for c in range(DC):
                    pe.matmul(OP[:, t * E8:(t + 1) * E8], XT[:, c, t * P:(t + 1) * P], fgw[:, c, :],
                              start=(c == 0), stop=False)
                pe.matmul(OP[:, t * E8:(t + 1) * E8], ones[0:1, :], fbg, start=False, stop=True).then_inc(f_lg, 1)
            for n in range(2 * E8):
                if n >= 4:
                    pe.wait_ge(f_ge, n - 3)
                for c in range(DC):
                    mm = pe.matmul(RB[n % 4][:, :], w1[:, c, n * P:(n + 1) * P], XT[:, c, :],
                                   start=(c == 0), stop=(c == DC - 1))
                mm.then_inc(f_h, 1)
            for n in range(NT4 * E8):
                t, e = n % NT4, n // NT4
                pe.wait_ge(f_ge, 2 * E8)
                if n >= 4:
                    pe.wait_ge(f_acc, n - 3)
                for c in range(DC):
                    pe.matmul(RB[n % 4][:, 0:D], hT[:, e, c, t * P:(t + 1) * P], w2[:, e, c, :],
                              start=(c == 0), stop=False)
                pe.matmul(RB[n % 4][:, 0:D], ones[0:1, :], b2r[:, e * D:(e + 1) * D],
                          start=False, stop=True).then_inc(f_y, 1)

        @block.vector
        def _(dve):
            def ln_dve(k, src):
                for t in range(NT4):
                    dve.bn_stats(stats[:, t, :], src[:, t, :]).then_inc(ln_stat, 1)
                for t in range(NT4):
                    dve.wait_ge(ln_stat, NT4 * k + t + 1)
                    dve.bn_aggr(mv[:, t, :], stats[:, t, :]).then_inc(ln_aggr, 1)
                dve.wait_ge(ln_aggr, NT4 * (k + 1))
                dve.wait_ge(ln_std, k + 1)
                dve.reciprocal(rstd[:, :], std[:, :]).then_inc(ln_rstd, 1)
                dve.wait_ge(ln_rstd, k + 1)
                for t in range(NT4):
                    dve.tensor_scalar(XN[:, t, :], src[:, t, :], mv[:, t, 0:1], rstd[:, t:t + 1],
                                      ALU.subtract, ALU.mult).then_inc(ln_norm, 1)

            def taken(at, score, g, u, mask=None):
                L = len(at.tiles)
                for t in range(QT):
                    for k, w in enumerate(at.tiles):
                        n = t * L + k
                        dve.wait_ge(at.scored, g * at.ns + n + 1 + ONE)
                        if mask is not None:
                            dve.sem_inc(waited, 1)
                        dst = score[:, u, t, k * 512:k * 512 + w]
                        if mask is not None:
                            dve.tensor_tensor_reduce(dst, SP_[n % 3][:, 0:w], mask[:, t, k * 512:k * 512 + w], 1.0,
                                                     NEG, ALU.add, ALU.max, mpart[:, u, t, k:k + 1])\
                                .then_inc(at.score_out, 1)
                        else:
                            dve.tensor_scalar(dst, SP_[n % 3][:, 0:w], 0.0, NEG, ALU.add, ALU.max,
                                              accum_out=mpart[:, u, t, k:k + 1]).then_inc(at.score_out, 1)
                    dve.wait_ge(at.score_out, g * at.ns + (t + 1) * L + ONE)
                    dve.tensor_reduce(nmax[:, u, t:t + 1], mpart[:, u, t, 0:L], AX.X, ALU.max, negate=True)\
                        .then_inc(at.max_ready, 1)

            def turned(at, g, h):
                for n in at.by_dve:
                    dve.wait_ge(at.turned, g * at.nt + n + 1)
                    dve.wait_ge(at.weighed, g * at.nt + (0 if n < 4 else n - 3) + ONE)
                    dve.tensor_copy(PT[:, n % 4, :], RB[n % at.ring][:, :]).then_inc(at.turned_dve, 1)
                dve.wait_ge(at.weighed, g * at.nt + at.nt + ONE)
                dve.tensor_copy(OA[:, bass.ds(h, 1), :].rearrange("p a k -> p (a k)"), OP[:, 0:S])\
                    .then_inc(at.out_taken, 1)

            dve.sem_inc(kp_r, 4)
            for at in (A, C):
                dve.sem_inc(at.score_out, at.free_scores)
                dve.sem_inc(at.turned_dve, at.free_dve)
                dve.sem_inc(at.out_taken, at.free_out)
            dve.wait_ge(x_in, 16)
            ln_dve(0, X)
            dve.wait_ge(cols_in, 48)
            for m in range(DC):
                def split(ins):
                    ins.then_inc(qa_out, 1)
                    split.n += 1
                    dve.wait_ge(qa_out, 5 * m + split.n)

                split.n = 0
                high, middle, low = [parts[:, 2 + m, g, :] for g in range(3)]
                dve.wait_ge(qa_mm, m + 1)
                split(dve.tensor_scalar(rest[:, m, :], PJ[m][:, :], cols[:, C_BQ + m:C_BQ + m + 1], 0.25,
                                        ALU.add, ALU.mult))
                split(dve.tensor_copy(high, rest[:, m, :]))
                split(dve.tensor_tensor(rest[:, m, :], rest[:, m, :], high, ALU.subtract))
                split(dve.tensor_copy(middle, rest[:, m, :]))
                split(dve.tensor_tensor(low, rest[:, m, :], middle, ALU.subtract))

            with dve.Fori(0, B) as b:
                dve.wait_ge(taps, b * H * TAP_OPS + ONE)
                dve.sem_inc(waited, 1)
                with dve.Fori(0, NPK // 4) as i:
                    for e in range(4):
                        dve.wait_ge(kp_h, b * NPK + i * 4 + e + 1)
                        dve.wait_ge(kp_l, b * NPK + i * 4 + e + 1)
                        dve.scalar_tensor_tensor(out=rest[:, e % 2, :], in0=RB[e][:, :],
                                                 scalar=cols[:, C_BK + e % 2:C_BK + e % 2 + 1],
                                                 in1=parts[:, e, 0, :], op0=ALU.add, op1=ALU.subtract)\
                            .then_inc(kp_r, 1)
                dve.wait_ge(mask_in, 32 * b + 32)
                dve.wait_ge(pja_out, b * NPJ + RING + NPJ)
                for t in range(QT):
                    dve.tensor_scalar(maskb[:, t, :], maskw[:, t, :], 0.0, NEG, ALU.is_equal, ALU.mult)\
                        .then_inc(mask_ready, 1)
                dve.wait_ge(mask_ready, 2 * b + 2)

                def score_taken(h, u, t, n):
                    g = b * H + h
                    dve.wait_ge(A.scored, g * A.ns + t * A.nt + n + 1 + ONE)
                    dve.sem_inc(waited, 1)
                    dve.tensor_tensor_reduce(scoreA[:, u, t, n * 512:(n + 1) * 512], SP_[n % 2][:, :],
                                             maskb[:, t, n * 512:(n + 1) * 512], 1.0, NEG, ALU.add, ALU.max,
                                             mpart[:, u, t, n:n + 1]).then_inc(A.score_out, 1)
                    if n == A.nt - 1:
                        dve.wait_ge(A.score_out, g * A.ns + (t + 1) * A.nt + A.free_scores)
                        dve.tensor_reduce(nmax[:, u, t:t + 1], mpart[:, u, t, 0:A.nt], AX.X, ALU.max, negate=True)\
                            .then_inc(A.max_ready, 1)

                def out_taken(h, t):
                    y = QT * (b * H + h) + t
                    dve.wait_ge(A.weighed, y * A.nt + A.nt + A.free_places)
                    dve.tensor_copy(OA[:, bass.ds(h, 1), t * P:(t + 1) * P].rearrange("p a k -> p (a k)"),
                                    OT[t][:, 0:P]).then_inc(A.out_taken, 1)

                def head(h, u, first=False, last=False):
                    for t in range(QT):
                        y = QT * (b * H + h) + t
                        for n in range(A.nt):
                            if not last:
                                score_taken(h + 1, 1 - u, t, n)
                            if n in A.by_dve:
                                dve.wait_ge(A.turned, y * A.nt + n + 1)
                                dve.wait_ge(A.weighed, y * A.nt + n + 1)
                                dve.tensor_copy(PT[:, n % 4, :], RB[n % 4][:, :]).then_inc(A.turned_dve, 1)
                            if n == 1 and t:
                                out_taken(h, t - 1)
                            elif n == 1 and not first:
                                out_taken(h - 1, QT - 1)

                for t in range(QT):
                    for n in range(A.nt):
                        score_taken(0, 0, t, n)
                head(0, 0, first=True)
                head(1, 1)
                with dve.Fori(1, H // 2 - 1) as i:
                    for u in range(2):
                        head(2 * i + u, u)
                head(H - 2, 0)
                head(H - 1, 1, last=True)
                out_taken(H - 1, QT - 1)
                post_dve(dve, b, 0)

            ln_dve(1, X)
            for m in range(DC):
                dve.wait_ge(gate_act, m + 1)
                dve.tensor_tensor(XG[:, m, :, :], XT[:, m, :].rearrange("p (b k) -> p b k", b=B),
                                  GT[:, m, :].rearrange("p (b k) -> p b k", b=B), ALU.mult).then_inc(gated, 1)
            dve.wait_ge(gated, DC)
            dve.wait_ge(cols_in, 48)
            count = [0]

            def scan(ins):
                count[0] += 1
                ins.then_inc(conv, 1)
                return count[0]

            def tile_reciprocal(e):
                dve.wait_ge(tile_sq, e + 1)
                dve.reciprocal(crstd[:, e % 4, :], cstd[:, e % 4, :]).then_inc(tile_rs, 1)
                dve.wait_ge(tile_rs, e + 1)
                dve.scalar_tensor_tensor(out=cshift[:, e % 4, :], in0=cmv[:, e % 4, :, 0], scalar=-1.0,
                                         in1=crstd[:, e % 4, :], op0=ALU.mult, op1=ALU.mult).then_inc(tile_shift, 1)

            def tile_stats(e):
                dve.wait_ge(tile_in[e % 4], (e // 4 + 1) * 16)
                if e >= 4:
                    dve.wait_ge(tile_norm, (e - 3) * 2)
                    dve.wait_ge(tile_norm_act, (e - 3) * 2)
                for t in range(4):
                    dve.bn_stats(cstats[:, e % 4, t, :], ctile[:, e % 4, t, :]).then_inc(tile_st, 1)
                for t in range(4):
                    dve.wait_ge(tile_st, e * 4 + t + 1)
                    dve.bn_aggr(cmv[:, e % 4, t, :], cstats[:, e % 4, t, :]).then_inc(tile_ag, 1)

            last = [0, 0]
            for m in range(DC):
                last[m] = scan(dve.tensor_scalar(Y[:, m, :, :], XG[:, m, :, :], cols[:, C_DP + m:C_DP + m + 1], None,
                                                 ALU.mult))
            for m in range(DC):
                dve.wait_ge(conv, last[m])
                last[m] = scan(dve.tensor_tensor(Y[:, m, :, :], Y[:, m, :, :], XG[:, m, :, :], ALU.add))
            dve.wait_ge(reversed_, TAU)
            k_terms = st_terms.rearrange("p m b a n -> p (m b a n)")[:, 0:512].rearrange("p (j h n) -> p j h n", h=2, n=NST)
            n_ = scan(dve.tensor_tensor(k_terms, kU[:, 0:TAU, :, :],
                                        kU[:, TAU:TAU + 1, :, :].rearrange("p j h n -> p (j h) n").unsqueeze(1)
                                        .broadcast_to([P, TAU, 2, NST]), ALU.mult))
            dve.wait_ge(conv, n_)
            n_ = scan(dve.tensor_reduce(K16, k_terms, AX.X, ALU.add))
            dve.wait_ge(conv, n_)

            def blocks(v, lo, hi, t0=0, t1=TAU):
                return v[:, lo * TAU:hi * TAU].rearrange("p (c j) -> p c j", j=TAU)[:, :, t0:t1]

            free = [0, 0]
            for i, (m, bb) in enumerate((m, bb) for m in range(DC) for bb in range(B)):
                dve.wait_ge(conv, max(1, free[i % 2]))
                n_ = scan(dve.tensor_tensor(
                    terms[i % 2], blocks(XG[:, m, bb, :], 0, NBK - 1).unsqueeze(2).broadcast_to([P, NBK - 1, NST, TAU]),
                    kW[:, :, m, :].rearrange("p j n -> p n j").unsqueeze(1).broadcast_to([P, NBK - 1, NST, TAU]), ALU.mult))
                dve.wait_ge(conv, n_)
                free[i % 2] = scan(dve.tensor_reduce(ST[:, m, :, bb, :], terms[i % 2], AX.X, ALU.add))
            state = [free[1]] * DC
            for c in range(1, NBK):
                tile_stats(c - 1)
                if c >= 2:
                    tile_reciprocal(c - 2)
                if c < NBK - 1:
                    for m in range(DC):
                        dve.wait_ge(conv, state[m])
                        state[m] = scan(dve.tensor_tensor(
                            st_terms[:, m, :, :, :], kP[:, m, :, :].rearrange("p n a -> p a n").unsqueeze(1)
                            .broadcast_to([P, B, NST, NST]),
                            ST[:, m, c - 1, :, :].unsqueeze(2).broadcast_to([P, B, NST, NST]), ALU.mult))
                    for m in range(DC):
                        dve.wait_ge(conv, state[m])
                        state[m] = scan(dve.tensor_reduce(st_sums[:, m, :, :], st_terms[:, m, :, :, :], AX.X, ALU.add))
                for k in ((0, 1) if c == 1 else (c,)):
                    for m in range(DC):
                        dve.wait_ge(conv, last[m])
                        yv = Y[:, m, :, :].rearrange("p b (c j) -> p b c j", j=TAU)[:, :, :, k:TAU]
                        xv = XG[:, m, :, :].rearrange("p b (c j) -> p b c j", j=TAU)[:, :, :, 0:TAU - k]
                        last[m] = scan(dve.scalar_tensor_tensor(out=yv, in0=xv, scalar=K16[:, k, m:m + 1], in1=yv,
                                                                op0=ALU.mult, op1=ALU.add))
                if c < NBK - 1:
                    for m in range(DC):
                        dve.wait_ge(conv, state[m])
                        state[m] = scan(dve.tensor_tensor(ST[:, m, c, :, :], ST[:, m, c, :, :], st_sums[:, m, :, :],
                                                          ALU.add))
            tile_stats(NBK - 1)
            tile_reciprocal(NBK - 2)
            tile_reciprocal(NBK - 1)
            dve.wait_ge(conv, count[0])
            free = [0, 0]
            for i, (m, bb) in enumerate((m, bb) for m in range(DC) for bb in range(B)):
                if i >= 2:
                    dve.wait_ge(conv, free[i % 2])
                n_ = scan(dve.tensor_tensor(
                    terms[i % 2], ST[:, m, :, bb, :].unsqueeze(2).broadcast_to([P, NBK - 1, TAU, NST]),
                    kU[:, TAU + 1:, m, :].unsqueeze(1).broadcast_to([P, NBK - 1, TAU, NST]), ALU.mult))
                dve.wait_ge(conv, n_)
                if i >= 2:
                    dve.wait_ge(y_done, i - 1)
                free[i % 2] = scan(dve.tensor_reduce(y_sums[:, i % 2, :, :], terms[i % 2], AX.X, ALU.add))
                dve.wait_ge(conv, free[i % 2])
                yv = blocks(Y[:, m, bb, :], 1, NBK)
                dve.tensor_tensor(yv, yv, y_sums[:, i % 2, :, :], ALU.add).then_inc(y_done, 1)
            dve.wait_ge(y_norm, NT4)
            dve.wait_ge(gate_w_in, 48)
            ln_dve(2, YT)
            for t in range(NT4):
                dve.wait_ge(ln_norm, NT4 * 2 + t + 1)
                dve.tensor_tensor(XN[:, t, :], XN[:, t, :], gamma_r, ALU.mult).then_inc(scan_done, 1)
                dve.wait_ge(scan_done, 3 * t + 1)
                dve.tensor_tensor(XN[:, t, :], XN[:, t, :], beta_r, ALU.add).then_inc(scan_done, 1)
                dve.wait_ge(scan_done, 3 * t + 2)
                dve.tensor_tensor(X[:, t, :], X[:, t, :], XN[:, t, :], ALU.add).then_inc(scan_done, 1)
            dve.wait_ge(scan_done, 3 * NT4)

            def gate_steps(Gt, iota, chain, logits, first, second):
                n = [0]

                def st(ins):
                    n[0] += 1
                    ins.then_inc(chain, 1)
                    dve.wait_ge(chain, n[0])

                def wide(v):
                    return v.broadcast_to([P, NT4, E8])

                def pick(src, hot, tmp, col):
                    mxv = Gt[:, col, :, 0:1]
                    st(dve.tensor_reduce(mxv, src, AX.X, ALU.max))
                    st(dve.tensor_tensor(tmp, src, wide(mxv), ALU.is_equal))
                    st(dve.tensor_tensor(tmp, tmp, iota.unsqueeze(1).broadcast_to([P, NT4, E8]), ALU.mult))
                    st(dve.tensor_reduce(Gt[:, col, :, 1:2], tmp, AX.X, ALU.min))
                    st(dve.tensor_tensor(hot, iota.unsqueeze(1).broadcast_to([P, NT4, E8]), wide(Gt[:, col, :, 1:2]),
                                         ALU.is_equal))
                    return mxv

                lg = Gt[:, 0, :, :]
                st(dve.tensor_copy(lg.rearrange("p t e -> p (t e)"), logits))
                m1 = pick(lg, Gt[:, 1, :, :], Gt[:, 2, :, :], 9)
                if not second:
                    return n[0]
                st(dve.tensor_scalar(Gt[:, 3, :, :], Gt[:, 1, :, :], NEG, None, ALU.mult))
                st(dve.tensor_tensor(Gt[:, 4, :, :], lg, Gt[:, 3, :, :], ALU.add))
                pick(Gt[:, 4, :, :], Gt[:, 5, :, :], Gt[:, 2, :, :], 10)
                st(dve.tensor_tensor(Gt[:, 6, :, :], Gt[:, 1, :, :], Gt[:, 5, :, :], ALU.add))
                st(dve.tensor_tensor(Gt[:, 7, :, :], lg, wide(m1), ALU.subtract))
                return n[0]

            ln_dve(3, X)
            dve.wait_ge(moe_lg, NT4)
            n_ = gate_steps(G, iot, moe_g, OP[:, 0:NT4 * E8], True, True)
            assert n_ == MG_NEG, n_
            dve.wait_ge(moe_g, n_ + 1)
            dve.tensor_tensor(G[:, 2, :, :], G[:, 8, :, :], G[:, 6, :, :], ALU.mult).then_inc(moe_g, 1)
            dve.wait_ge(moe_g, n_ + 2)
            dve.tensor_reduce(G[:, 11, :, 0:1], G[:, 2, :, :], AX.X, ALU.add).then_inc(moe_g, 1)
            dve.wait_ge(moe_g, n_ + 3)
            dve.reciprocal(G[:, 11, :, 1:2], G[:, 11, :, 0:1]).then_inc(moe_g, 1)
            dve.wait_ge(moe_g, n_ + 4)
            dve.tensor_tensor(G[:, 12, :, :], G[:, 2, :, :], G[:, 11, :, 1:2].broadcast_to([P, NT4, E8]), ALU.mult)\
                .then_inc(moe_g, 1)
            dve.wait_ge(moe_g, n_ + 5)
            for n in range(NT4 * 4):
                t, e2 = n // 4, n % 4
                dve.wait_ge(moe_mm, n + 1)
                for ee in range(2):
                    if n + ee:
                        dve.wait_ge(moe_acc, 2 * n + ee)
                    dve.scalar_tensor_tensor(out=X[:, t, :], in0=RB[n % 4][:, ee * D:(ee + 1) * D],
                                             scalar=G[:, 12, t, 2 * e2 + ee:2 * e2 + ee + 1], in1=X[:, t, :],
                                             op0=ALU.mult, op1=ALU.add).then_inc(moe_acc, 1)
            dve.wait_ge(moe_acc, 2 * NT4 * 4)
            ln_dve(4, X)
            dve.wait_ge(ln_norm, NT4 * 5)
            ln_dve(5, XN)
            dve.wait_ge(ln_turn, 4 * DC)
            with dve.Fori(0, B) as b:
                taken(C, scoreC, b * H, 0)
                taken(C, scoreC, b * H + 1, 1)
                turned(C, b * H, 0)
                with dve.Fori(1, 8) as p:
                    taken(C, scoreC, b * H + 2 * p, 0)
                    turned(C, b * H + 2 * p - 1, 2 * p - 1)
                    taken(C, scoreC, b * H + 2 * p + 1, 1)
                    turned(C, b * H + 2 * p, 2 * p)
                turned(C, b * H + H - 1, H - 1)
                post_dve(dve, b, 1)
            ln_dve(6, X)
            dve.wait_ge(sw_in, 7 * 16)
            for m in range(DC):
                dve.wait_ge(sq_mm, m + 1)
                dve.tensor_scalar(QTR[:, m, :], SP_[m][:, :], cols[:, C_SQ + m:C_SQ + m + 1], 0.25,
                                  ALU.add, ALU.mult).then_inc(sq_out, 1)
            for t in range(NT4):
                for h2 in range(H // 2):
                    n = t * 8 + h2
                    dve.wait_ge(s_mm, n + 1)
                    dve.tensor_tensor(sS[:, t, 2 * h2:2 * h2 + 2, :],
                                      SP_[n % 3][:, :].rearrange("p (a k) -> p a k", a=2),
                                      smask[:, t % QT, :].unsqueeze(1).broadcast_to([P, 2, S]), ALU.add)\
                        .then_inc(s_ev, 1)
                dve.wait_ge(s_ev, (t + 1) * 8)
                dve.tensor_reduce(smx[:, t, :], sS[:, t, :, :], AX.X, ALU.max, negate=True).then_inc(s_nm, 1)
            for n, (t, h) in enumerate((t, h) for t in range(NT4) for h in range(H)):
                nb = t % QT + 1
                dve.wait_ge(s_t, n + 1)
                if n >= 4:
                    dve.wait_ge(s_pv, n - 3)
                dve.tensor_copy(sPT[:, n % 4, 0:nb * P], TP[n % 2][:, 0:nb * P]).then_inc(s_tc, 1)
                if h == H - 1:
                    self_norm(dve, t)
            for t in range(NT4):
                dve.wait_ge(s_y, t + 1)
                dve.tensor_tensor(X[:, t, :], X[:, t, :], RB[t][:, 0:D], ALU.add).then_inc(s_x, 1)
            dve.wait_ge(s_x, NT4)
            ln_dve(7, X)
            dve.wait_ge(f_lg, NT4)
            gate_steps(G2, iot2, f_g, OP[:, 0:NT4 * E8], True, False)
            for n in range(NT4 * E8):
                t, e = n % NT4, n // NT4
                dve.wait_ge(f_y, n + 1)
                if n >= NT4:
                    dve.wait_ge(f_acc, n - NT4 + 1)
                dve.scalar_tensor_tensor(out=X[:, t, :], in0=RB[n % 4][:, 0:D], scalar=G2[:, 1, t, e:e + 1],
                                         in1=X[:, t, :], op0=ALU.mult, op1=ALU.add).then_inc(f_acc, 1)


def kernel(**inputs):
    import numpy as np
    import concourse.bacc as bacc
    from concourse import mybir as mb
    from concourse.bass_utils import run_bass_kernel_spmd as run

    v = {k: np.asarray(x) for k, x in inputs.items()}

    def rows(w):
        return np.ascontiguousarray(w.reshape(2, 128, -1).transpose(1, 0, 2))

    def col(x):
        return x.reshape(-1, 128).T

    f = np.float32
    p = np.arange(128)
    order = np.arange(256).reshape(4, 4, 16).transpose(1, 0, 2).reshape(-1)
    twice = np.concatenate([np.arange(64), np.arange(64)])
    selA = np.zeros((128, 8, 128), f)
    for j in range(8):
        for d in range(16):
            selA[d::32, j, 16 * j + d] = 1
    selC = np.zeros((128, 2, 128), f)
    for u in range(2):
        for d in range(64):
            selC[d::64, u, 64 * u + d] = 1
    h16 = np.arange(16)
    i, j = np.arange(256)[:, None], np.arange(256)[None, :]
    smask = np.where((i - 128 >= j) | (i < j), f(NEG), f(0)).astype(f).reshape(2, 128, 256).transpose(1, 0, 2)
    scan_a = v["L0_attn_A"].reshape(2, 128, 16, 16).transpose(1, 0, 2, 3)
    arrays = {
        "x": v["x"], "ctx": v["ctx_1024"], "ctxT": np.ascontiguousarray(v["ctx_1024"].transpose(0, 2, 1)),
        "mask": v["mask_BxSxS2_ik1"],
        "WqT": rows(v["L0_xattn_Wq"].T), "WkT": rows(v["L0_xattn_Wk"].T), "WvT": rows(v["L0_xattn_Wv"].T),
        "WoT": rows(v["L0_xattn_Wo"].T), "bo": v["L0_xattn_bo"][None, :],
        "cols": np.concatenate([col(v[n]) for n in (
            "L0_xattn_bq", "L0_xattn_bk", "L0_xattn_bv", "L0_attn_bg", "L0_attn_Dp", "L1_xattn_ln1_g",
            "L1_xattn_ln1_b", "L1_xattn_ln2_g", "L1_xattn_ln2_b")]
            + [col(v["L1_attn_bq"][order]), col(v["L1_attn_bk"][twice]), np.zeros((128, 1), f)], 1),
        "sel16": (p[:, None] // 16 == h16[None, :] % 8).astype(f),
        "sel64": (p[:, None] // 64 == np.arange(2)[None, :]).astype(f),
        "selA": selA, "hselA": (h16[:, None, None] == 8 * np.arange(2)[None, :, None] + p[None, None, :] // 16).astype(f),
        "selC": selC, "hselC": (h16[:, None, None] == 2 * np.arange(8)[None, :, None] + p[None, None, :] // 64).astype(f),
        "A": scan_a, "AA": np.stack([scan_a.transpose(0, 1, 3, 2), scan_a]),
        "BC": np.stack([rows(v["L0_attn_Bp"]), rows(v["L0_attn_Cp"])]),
        "WgT": rows(v["L0_attn_Wg"].T),
        "gamma": np.broadcast_to(v["L0_attn_gamma"], (128, 256)), "beta": np.broadcast_to(v["L0_attn_beta"], (128, 256)),
        "ew": v["L0_ffn_expert_w"].reshape(8, 2, 128, 256).transpose(2, 1, 0, 3).reshape(128, 2, 2048),
        "eb": v["L0_ffn_expert_b"].reshape(1, 2048), "gwT": rows(v["L0_ffn_gate_w"].T), "gb": v["L0_ffn_gate_b"][None, :],
        "iota": np.broadcast_to(np.arange(8, dtype=f) - 8, (128, 8)),
        "WqC": v["L1_xattn_Wq"].reshape(2, 128, 8, 128).transpose(2, 1, 0, 3),
        "WkC": v["L1_xattn_Wkv"][:, :1024].reshape(2, 128, 8, 128).transpose(2, 1, 0, 3),
        "WvC": v["L1_xattn_Wkv"][:, 1024:].reshape(2, 128, 8, 128).transpose(2, 1, 0, 3),
        "WoC": v["L1_xattn_Wo"].reshape(8, 128, 256).transpose(1, 0, 2),
        "sWq": rows(v["L1_attn_Wq"][:, order]), "sWk": rows(v["L1_attn_Wk"][:, twice]), "sWv": rows(v["L1_attn_Wv"]),
        "sWo": rows(v["L1_attn_Wo"]), "sbv": v["L1_attn_bv"][None, :], "sbo": v["L1_attn_bo"][None, :], "smask": smask,
        "fWg": rows(v["L1_ffn_Wg"]), "fbg": v["L1_ffn_bg"][None, :],
        "W1": v["L1_ffn_W1"].reshape(8, 2, 128, 256).transpose(2, 1, 0, 3).reshape(128, 2, 2048),
        "fb1": v["L1_ffn_b1"].reshape(16, 128).T,
        "W2": v["L1_ffn_W2"].reshape(8, 2, 128, 256).transpose(2, 0, 1, 3), "b2": v["L1_ffn_b2"].reshape(1, 2048),
    }
    arrays = {k: np.ascontiguousarray(x) for k, x in arrays.items()}
    nc = bacc.Bacc("TRN2", target_bir_lowering=False, num_devices=1)
    aps = {k: nc.dram_tensor(k + "_dram", x.shape, mb.dt.from_np(x.dtype), kind="ExternalInput").ap()
           for k, x in arrays.items()}
    res = nc.dram_tensor("result_dram", (2, 256, 256), mb.dt.float32, kind="ExternalOutput").ap()
    program(nc, aps, res)
    r = run(nc, [{k + "_dram": x for k, x in arrays.items()}], core_ids=[0])
    return r.results[0]["result_dram"]
```

```python
from contextlib import ExitStack

import concourse.bass as bass
from concourse import mybir
from concourse.alu_op_type import AluOpType as ALU

ACT = mybir.ActivationFunctionType
AX = mybir.AxisListType
F32 = mybir.dt.float32
BF16 = mybir.dt.bfloat16
I32 = mybir.dt.int32

P = 128
B = 2
S = 256
QT = S // P
NT4 = B * QT
D = 256
DC = D // P
S2 = 4096
H = 16
NEG = -3.0e38
EPS = 1e-5
E8 = 8
MOE_ADDS = NT4 * E8 + NT4
RING = 4
NPK = 16
NPJ = 16
QK_IN = 6 * 16
NKC = (S2 + S) // P
NKT = (NKC + 3) // 4
NPC = 1 + 2 * NKT
PAIRS = B * H // 2
NSB = NKC // 2
NSG = (NSB + 1) // 2
RUN = (NSB - 1) + 1
AT_PROJECTED = {3: (0,), 4: (1,), 5: (2,), 6: (3,), 7: (4,)}
AT_SCORED = {3: (5,), 6: (6,), 9: (7,), 12: (8,)}
SCL = 64 ** -0.25
ONE = 1
MG_NEG = 15
FG_HOT = 6
TAU = 16
NBK = S // TAU
K_READY = 2
TAP_OPS = 10
NST = 16


class Attention:

    def __init__(self, sem, name, keys, width, by_dve):
        self.width = width
        self.nt = keys // 512
        self.ns = QT * self.nt
        self.by_dve = by_dve
        self.by_act = [n for n in range(self.nt) if n not in by_dve]
        self.na = len(self.by_act)
        self.nd = len(by_dve)
        self.free_scores, self.free_places, self.free_out, self.free_act, self.free_dve = 2, 4, QT, self.na, self.nd
        self.scored = sem(name + "_scored")
        self.score_out = sem(name + "_score_out")
        self.max_ready = sem(name + "_max_ready")
        self.exp_done = sem(name + "_exp_done")
        self.turned = sem(name + "_turned")
        self.turned_act = sem(name + "_turned_act")
        self.turned_dve = sem(name + "_turned_dve")
        self.weighed = sem(name + "_weighed")
        self.out_taken = sem(name + "_out_taken")

    def copied(self, y, n, before=0):
        if n in self.by_dve:
            return self.turned_dve, y * self.nd + (self.by_dve.index(n) + 1 + before * self.nd + self.free_dve)
        return self.turned_act, y * self.na + (self.by_act.index(n) + 1 + before * self.na + self.free_act)


def program(nc, a, out):
    with ExitStack() as ctx:
        def sb(name, shape, dt=F32):
            return ctx.enter_context(nc.sbuf_tensor(name, shape, dt))

        def sem(name):
            return ctx.enter_context(nc.semaphore(name))

        RX = sb("RX", [P, 8192])
        RK = sb("RK", [P, 8192])
        RV = sb("RV", [P, 8192])
        RS = sb("RS", [P, 2 * 2 * 4352])
        PT = sb("PT", [P, 4, 512])
        OA = sb("OA", [P, H, S])
        X = sb("X", [P, NT4, D])
        QTR = RS[:, 16384:17408].rearrange("p (m k) -> p m k", m=DC)
        WA = sb("WA", [P, 3, DC, D])
        QR = sb("QR", [P, S + 2 * NST * NST + (2 * TAU + 1) * 2 * NST])
        ident = sb("ident", [P, P])
        ones = sb("ones", [P, P])
        sel16 = sb("sel16", [P, H])
        sel64 = sb("sel64", [P, 2])
        mpart = sb("mpart", [P, 2, QT, 9])
        nmax = sb("nmax", [P, 2, QT])
        den = sb("den", [P, QT, H])
        dpart = sb("dpart", [P, QT, H * 4])
        rden = sb("rden", [P, QT, H])
        cols = sb("cols", [P, 32])
        mv = sb("mv", [P, NT4, 2])
        std = sb("std", [P, NT4])
        rstd = sb("rstd", [P, NT4])
        stats = sb("stats", [P, NT4, 6])

        def bank(name):
            return ctx.enter_context(nc.psum_tensor(name, [P, 512], F32))

        SP_ = [bank(f"score_bank{i}") for i in range(3)]
        TP = [bank(f"turn_bank{i}") for i in range(2)]
        OP = bank("out_bank")
        PJ = [bank(f"proj_bank{i}") for i in range(2)]

        XN = OA[:, 0:4, :]
        XT = OA[:, 4:8, :].rearrange("p (c u) s -> p c (u s)", c=DC)
        ctxT = RX[:, :].rearrange("p (c k) -> p c k", c=DC)
        keyS = RK[0:6 * 16, 0:4096].bitcast(BF16).rearrange("p (u k) -> p u k", u=2)
        qryS = QR[0:6 * 16, 0:S].bitcast(BF16).rearrange("p (u k) -> p u k", u=2)
        QP = QR[:, 0:2 * S].rearrange("p (u k) -> p u k", u=2)
        parts = RK[:, 4096:7168].bitcast(BF16).rearrange("p (s g k) -> p s g k", s=4, g=3)
        rest = RK[:, 7168:8192].rearrange("p (s k) -> p s k", s=2)
        val = RV[:, :].rearrange("p (k d) -> p k d", d=D)
        maskb = RX[:, 0:4096].bitcast(BF16).rearrange("p (t k) -> p t k", t=QT)
        VH = RX[:, 4096:6144].rearrange("p (u k d) -> p u k d", u=2, d=32)
        selA = RX[:, 6144:7168].rearrange("p (j c) -> p j c", j=8)
        hselA = RX[0:H, 7168:7424].rearrange("p (m c) -> p m c", m=2)
        scoreA = RS[:, 0:16384].rearrange("p (u t k) -> p u t k", u=2, t=QT)
        maskw = RS[:, 8192:16384].bitcast(I32).rearrange("p (t k) -> p t k", t=QT)
        scoreC = RS[:, :].rearrange("p (u k q) -> p u k q", u=2, q=S)
        BOR = RX[0:1, 7424:7680]
        RB = [TP[0], TP[1], PJ[0], PJ[1]]
        OT = [OP, SP_[2]]
        recT = PT[0:H, 0, 0:S]
        ON = RS[:, 0:2048].rearrange("p (j k) -> p j k", j=8)
        OC = RS[:, 2048:4096].rearrange("p (j k) -> p j k", j=8)
        ctile = RX[:, 0:4096].rearrange("p (s t d) -> p s t d", s=4, t=4)
        cnorm = RX[:, 4096:6144].rearrange("p (s t d) -> p s t d", s=2, t=4)
        cturn = RX[:, 6144:8192].rearrange("p (s c k) -> p s c k", s=2, c=DC)
        cstats = RV[:, 7712:7808].rearrange("p (s t n) -> p s t n", s=4, t=4)
        cmv = RV[:, 7808:7840].rearrange("p (s t n) -> p s t n", s=4, t=4)
        cstd = RV[:, 7840:7856].rearrange("p (s t) -> p s t", s=4)
        crstd = RV[:, 7856:7872].rearrange("p (s t) -> p s t", s=4)
        cshift = RV[:, 7872:7888].rearrange("p (s t) -> p s t", s=4)
        xlT = RX[:, :].rearrange("p (c k) -> p c k", c=DC)
        keyC = RK[:, 0:4352]
        latT = RK[:, 4352:4864].rearrange("p (c k) -> p c k", c=DC)
        wq = RK[:, 4864:5120].rearrange("p (c n) -> p c n", c=DC)
        wk = RK[:, 5120:5376].rearrange("p (c n) -> p c n", c=DC)
        wv = RK[:, 5376:5632].rearrange("p (c n) -> p c n", c=DC)
        qC = RK[:, 5632:5888]
        latAll = RK[:, 5888:6912].rearrange("p (c k) -> p c k", c=DC)
        valC = RV[:, 0:4352].rearrange("p (k d) -> p k d", d=P)
        woC = [PT[:, :, :].rearrange("p a b -> p (a b)").rearrange("p (h n) -> p h n", n=D),
               RV[:, 4352:6400].rearrange("p (h n) -> p h n", n=D)]
        acc = RV[:, 6400:7424].rearrange("p (u k) -> p u k", u=2)
        run_max = RK[:, 6912:7424]
        half_max = RK[:, 7424:7680]
        diag = RK[:, 7680:7936]
        recip = RK[:, 7936:8192]

        key_parts = nc.dram_tensor("key_parts", (B, DC, 3, P, S2), BF16, kind="Internal").ap()
        xl_dram = nc.dram_tensor("context_normed", (B * 8, P, DC, 512), F32, kind="Internal").ap()
        qry_parts = nc.dram_tensor("query_parts", (DC, 3, P, B * S), BF16, kind="Internal").ap()

        block = ctx.enter_context(nc.Block())

        A = Attention(sem, "a", S2, 32, [3, 6])
        c_scored = sem("c_scored")
        c_kept = sem("c_kept")
        c_run = sem("c_run")
        c_turned = sem("c_turned")
        c_max = sem("c_max")
        c_diag = sem("c_diag")
        c_spread = sem("c_spread")
        c_sub = sem("c_sub")
        c_exp = sem("c_exp")
        c_acc = sem("c_acc")
        c_weighed = sem("c_weighed")
        c_sum = sem("c_sum")
        c_recip = sem("c_recip")
        c_out = sem("c_out")

        x_in, wqa_in, wa_in, cols_in = sem("x_in"), sem("wqa_in"), sem("wa_in"), sem("cols_in")
        scan_in = sem("scan_in")
        consts = sem("consts")
        ctx_in = [sem(f"ctx_in_{i}") for i in range(4)]
        mask_in, sela_in = sem("mask_in"), sem("sela_in")
        ln_stat, ln_aggr, ln_std, ln_rstd = sem("ln_stat"), sem("ln_aggr"), sem("ln_std"), sem("ln_rstd")
        ln_norm, ln_turn, ln_out = sem("ln_norm"), sem("ln_turn"), sem("ln_out")
        qa_mm, qa_out, qa_d = [sem("qa_" + n) for n in ("mm", "split", "dram")]
        q_ready = sem("q_ready")
        den_sum = sem("den_sum")
        ks_in = [sem(f"head_in_{u}") for u in range(2)]
        kp_mm, kp_h, kp_r, kp_m, kp_l = [sem("keys_" + n) for n in ("mm", "high", "rest", "mid", "low")]
        kp_d = [sem(f"keys_dram_{e}") for e in range(4)]
        pja_mm, pja_out = sem("pja_mm"), sem("pja_out")
        mask_ready = sem("mask_ready")
        vh_zero, vh_ready = sem("vh_zero"), sem("vh_ready")
        pa_rden, pa_rt, pa_rtc, pa_sum, pa_oc, pa_on, pa_y, pa_x = [sem("post_" + n) for n in (
            "recip", "recip_turned", "recip_in_sbuf", "summed", "sum_in_sbuf", "normed", "projected", "added")]
        taps = sem("taps")
        gate_w_in, gate_mm, gate_act, gated = sem("gate_w_in"), sem("gate_mm"), sem("gate_act"), sem("gated")
        conv, y_turn, y_norm, scan_done = sem("conv"), sem("y_turn"), sem("y_norm"), sem("scan_done")
        reversed_ = sem("scan_reversed")
        y_done = sem("y_done")
        pool_terms, states = sem("pool_terms"), sem("states")
        tap_diag, tap_mm = sem("tap_diagonal"), sem("tap_mm")
        moe_w_in, moe_lg, moe_g, moe_mm, moe_acc = (
            sem("moe_w_in"), sem("moe_logits"), sem("moe_gate"), sem("moe_mm"), sem("moe_acc"))
        moe_gt, moe_gtc, moe_b = sem("moe_gates_turned"), sem("moe_gates_out"), sem("moe_biases")
        f_gt, f_gtc, f_b = sem("ffn_gates_turned"), sem("ffn_gates_out"), sem("ffn_biases")
        lat_done = sem("lat_done")
        cw_in, cpost_in = sem("cw_in"), sem("cpost_in")
        tile_in = [sem(f"tile_in_{i}") for i in range(4)]
        tile_shift, tile_norm_act = sem("tile_shift"), sem("tile_norm_act")
        tile_kept = [sem(f"tile_stored_{i}") for i in range(2)]
        xl_in = sem("context_in")
        tile_norm, tile_turn, tile_out, tile_st = (
            sem("tile_norm"), sem("tile_turn"), sem("tile_out"), sem("tile_stat"))
        tile_ag, tile_sq, tile_rs = sem("tile_aggr"), sem("tile_std"), sem("tile_rstd")
        lat_copy = sem("lat_copy")
        wqc_in, wkc_in, wvc_in = sem("wqc_in"), sem("wkc_in"), sem("wvc_in")
        pjc_mm, pjc_out = sem("pjc_mm"), sem("pjc_out")
        sw_in, sq_mm, sq_out, skv_mm, skv_out = [sem("self_" + n) for n in ("w_in", "q_mm", "q_out", "kv_mm", "kv_out")]
        s_q, s_mm, s_ev, s_nm, s_ex, s_t, s_tc, s_pv, s_on, s_rd, s_ot, s_oc, s_y, s_x = [
            sem("self_" + n) for n in ("q", "scored", "score_out", "max", "exp", "turned", "turned_out", "weighed",
                                       "normed", "recip", "out_turned", "out_in_sbuf", "projected", "added")]
        fw_in, f_lg, f_g, f_h, f_ge, f_y, f_acc = [sem("ffn_" + n) for n in (
            "w_in", "logits", "gate", "hidden", "gelu", "mm", "acc")]
        s_qa = sem("self_q_act")
        stored = sem("stored")
        waited = sem("waited")

        C_BQ, C_BK, C_BV, C_BG, C_DP, C_G1, C_B1, C_G2, C_B2 = range(0, 18, 2)
        C_SQ, C_SK = 18, 20

        wgT = RV[:, 4096:4608].rearrange("p (c n) -> p c n", c=DC)
        gamma_r, beta_r = RV[:, 4608:4864], RV[:, 4864:5120]
        GT = RV[:, 5120:6144].rearrange("p (m k) -> p m k", m=DC)
        XG = RK[:, 0:1024].rearrange("p (m b k) -> p m b k", m=DC, b=B)
        Y = RK[:, 2048:3072].rearrange("p (m b k) -> p m b k", m=DC, b=B)
        YT = RV[:, 6144:7168].rearrange("p (t d) -> p t d", t=NT4)
        ew = RV[:, 0:4096].rearrange("p (c n) -> p c n", c=DC)
        ebr = RK[0:E8, 4096:4352]
        gateT = RK[0:E8, 4352:4864]
        gw = RV[:, 7168:7184].rearrange("p (c n) -> p c n", c=DC)
        gbr = RV[0:1, 7184:7192]
        iot = RV[:, 7192:7200]
        G = RV[:, 7200:7712].rearrange("p (n t e) -> p n t e", n=16, t=NT4)
        swq = RX[:, 0:512].rearrange("p (c n) -> p c n", c=DC)
        swk = RX[:, 512:768].rearrange("p (c n) -> p c n", c=DC)
        swv = RX[:, 768:896].rearrange("p (c n) -> p c n", c=DC)
        swo = RX[:, 896:1408].rearrange("p (c n) -> p c n", c=DC)
        sbv = RX[0:1, 1408:1472]
        sbo = RX[0:1, 1472:1728]
        smask = RX[:, 1728:2240].rearrange("p (t k) -> p t k", t=QT)
        sK = RX[:, 2240:2752]
        sV = RX[:, 2752:3008].rearrange("p (t d) -> p t d", t=NT4)
        sQ = RK[:, 0:8192].rearrange("p (h k) -> p h k", h=H)
        sS = RS[:, 0:16384].rearrange("p (t h k) -> p t h k", t=NT4, h=H)
        sPT = PT[:, :, :]
        sO = RV[:, 1024:2048].rearrange("p (t d) -> p t d", t=NT4)
        sOT = RV[:, 2048:3072].rearrange("p (c k) -> p c k", c=DC)
        smx = RV[:, 3072:3136].rearrange("p (t h) -> p t h", t=NT4)
        sden = RV[:, 3136:3200].rearrange("p (t h) -> p t h", t=NT4)
        srd = RV[:, 3200:3264].rearrange("p (t h) -> p t h", t=NT4)
        w1 = RV[:, 4096:8192].rearrange("p (c n) -> p c n", c=DC)
        w2 = RX[:, 4096:8192].rearrange("p (e c n) -> p e c n", e=E8, c=DC)
        b2r = RX[0:E8, 3584:3840]
        gateT2 = RV[0:E8, 0:512]
        fgw = RX[:, 3008:3024].rearrange("p (c n) -> p c n", c=DC)
        fbg = RX[0:1, 3024:3032]
        fb1 = RX[:, 3040:3056]
        iot2 = RX[:, 3056:3064]
        G2 = RX[:, 3072:3584].rearrange("p (n t e) -> p n t e", n=16, t=NT4)
        hT = RK[:, 0:8192].rearrange("p (e c k) -> p e c k", e=E8, c=DC)

        kA = QR[:, S:S + 512].rearrange("p (h a c) -> p h a c", h=2, a=NST)
        kU = QR[:, S + 512:].rearrange("p (j h n) -> p j h n", h=2, n=NST)
        kP = RS[:, 16384:17408].rearrange("p (s n m) -> p s n m", s=4, n=NST)
        kT = rest.rearrange("p s k -> p (s k)")
        kTv = kT[:, 0:512].rearrange("p (h a c) -> p h a c", h=2, a=NST)
        kTs = kT.rearrange("p (n m k) -> p n m k", n=4, m=NST)
        kW = RS[:, 10784:11296].rearrange("p (j h n) -> p j h n", h=2, n=NST)
        K16 = RS[:, 11296:11328].rearrange("p (j h) -> p j h", h=2)
        terms = [RS[:, i:i + (NBK - 1) * TAU * NST].rearrange("p (c a n) -> p c a n", c=NBK - 1, a=TAU)
                 for i in (0, 4096, 12288)]
        ST = RS[:, 8192:9152].rearrange("p (m c b n) -> p m c b n", m=DC, c=NBK - 1, b=B)
        st_terms = RS[:, 9216:10240].rearrange("p (m b a n) -> p m b a n", m=DC, b=B, a=NST)
        tap_ring = [RK[:, k:k + P] for k in (*range(1024, 2048, P), *range(3072, 4096, P))]
        YP = [SP_[2], OP]
        st_sums = RS[:, 10240:10304].rearrange("p (m b a) -> p m b a", m=DC, b=B)
        y_sums = RS[:, 10304:10784].rearrange("p (i c j) -> p i c j", i=2, c=NBK - 1)

        def blocks(v, lo, hi):
            return v[:, lo * TAU:hi * TAU].rearrange("p (c j) -> p c j", j=TAU)

        def in_terms(eng, t_, m, bb):
            return eng.tensor_tensor(
                t_, blocks(XG[:, m, bb, :], 0, NBK - 1).unsqueeze(2).broadcast_to([P, NBK - 1, NST, TAU]),
                kW[:, :, m, :].rearrange("p j n -> p n j").unsqueeze(1).broadcast_to([P, NBK - 1, NST, TAU]), ALU.mult)

        def out_terms(eng, t_, m, bb):
            return eng.tensor_tensor(
                t_, ST[:, m, :, bb, :].unsqueeze(2).broadcast_to([P, NBK - 1, TAU, NST]),
                kU[:, TAU + 1:, m, :].unsqueeze(1).broadcast_to([P, NBK - 1, TAU, NST]), ALU.mult)

        def ctx_views(b):
            return a["ctxT"][bass.ds(b, 1), :, :].rearrange("b (c p) k -> p (b c) k", p=P)

        def post_pe(pe, b):
            pe.wait_ge(A.out_taken, (b * H + H) * QT + A.free_out)
            pe.wait_ge(sela_in, 48 * b + 48)
            pe.wait_ge(pa_rden, b + 1)
            for t in range(QT):
                mm = pe.transpose(TP[0][0:H, t * P:(t + 1) * P], rden[:, t, :], ident[:, :])
            mm.then_inc(pa_rt, 1)
            pe.wait_ge(pa_rtc, b + 1)
            for j in range(DC):
                pe.matmul(PJ[j][:, 0:S], hselA[:, j, :], recT, start=True, stop=True)
                for u in range(8):
                    mm = pe.matmul(SP_[j][:, 0:S], selA[:, u, :], OA[:, 8 * j + u, :], start=(u == 0), stop=(u == 7))
                mm.then_inc(pa_sum, 1)
            pe.wait_ge(pa_on, b * 4 + 4)
            for t in range(QT):
                for j in range(DC):
                    pe.matmul(TP[t][:, 0:D], ON[:, j, t * P:(t + 1) * P], WA[:, 2, j, :], start=(j == 0), stop=False)
                pe.matmul(TP[t][:, 0:D], ones[0:1, :], BOR, start=False, stop=True).then_inc(pa_y, 1)
            pe.wait_ge(pa_x, QT * b + QT)

        def post_act(act, b):
            act.wait_ge(pa_rt, b + 1)
            act.activation(recT, TP[0][0:H, 0:S], ACT.Copy).then_inc(pa_rtc, 1)
            for j in range(DC):
                act.wait_ge(pa_sum, b * 2 + j + 1)
                act.activation(OC[:, j, :], SP_[j][:, 0:S], ACT.Copy).then_inc(pa_oc, 1)

        def post_dve(dve, b):
            dve.wait_ge(A.exp_done, (b * H + H) * QT * 4)
            dve.tensor_reduce(den[:, :, :], dpart[:, :, :].rearrange("p t (h q) -> p t h q", q=4), AX.X, ALU.add)\
                .then_inc(den_sum, 1)
            dve.wait_ge(den_sum, b + 1)
            dve.reciprocal(rden[:, :, :], den[:, :, :]).then_inc(pa_rden, 1)
            for j in range(DC):
                dve.wait_ge(pa_oc, b * 2 + j + 1)
                dve.tensor_tensor(ON[:, j, :], OC[:, j, :], PJ[j][:, 0:S], ALU.mult).then_inc(pa_on, 1)
                dve.wait_ge(pa_on, b * 4 + 2 * j + 1)
                dve.tensor_scalar(ON[:, j, :], ON[:, j, :], cols[:, C_BV + j:C_BV + j + 1], None, ALU.add)\
                    .then_inc(pa_on, 1)
            added(dve, b, b, TP)

        def added(dve, b, k, banks):
            for t in range(QT):
                dve.wait_ge(pa_y, QT * k + t + 1)
                x = X[:, bass.ds(b * QT + t, 1), :].rearrange("p a d -> p (a d)")
                dve.tensor_tensor(x, x, banks[t][:, 0:D], ALU.add).then_inc(pa_x, 1)
            dve.wait_ge(pa_x, QT * k + QT)

        def self_weigh(pe, n):
            t, h2 = divmod(n, H // 2)
            nb = t % QT + 1
            pe.wait_ge(s_tc, n + 1)
            if h2 == 0 and t >= 2:
                pe.wait_ge(s_on, t - 1)
            for hh in range(2):
                h = 2 * h2 + hh
                for k in range(nb):
                    mm = pe.matmul([OP, PJ[0]][t % 2][:, h * 16:h * 16 + 16],
                                   sPT[:, n % 4, (hh * nb + k) * P:(hh * nb + k + 1) * P],
                                   sV[:, t // QT * QT + k, (h // 4) * 16:(h // 4) * 16 + 16],
                                   start=(k == 0), stop=(k == nb - 1))
            mm.then_inc(s_pv, 1)

        def self_norm(dve, t):
            dve.wait_ge(s_pv, (t + 1) * H // 2)
            dve.reciprocal(srd[:, t, :], sden[:, t, :]).then_inc(s_rd, 1)
            dve.wait_ge(s_rd, t + 1)
            dve.tensor_tensor(sO[:, t, :].rearrange("p (h d) -> p h d", h=H),
                              [OP, PJ[0]][t % 2][:, 0:D].rearrange("p (h d) -> p h d", h=H),
                              srd[:, t, :].unsqueeze(2).broadcast_to([P, H, 16]), ALU.mult).then_inc(s_on, 1)

        @block.sync
        def _(sp):
            def load(dst, name, s_):
                return sp.dma_start(dst, a[name]).then_inc(s_, 16)

            sp.dma_start(X[:, :, :], a["x"].rearrange("b (t p) d -> p (b t) d", p=P)).then_inc(x_in, 16)
            for e in range(4):
                sp.sem_inc(kp_d[e], 16)
            load(RV[:, 0:512].rearrange("p (c n) -> p c n", c=DC), "WqT", wqa_in)
            load(WA[:, 0, :, :], "WkT", wa_in)
            load(WA[:, 1, :, :], "WvT", wa_in)
            load(WA[:, 2, :, :], "WoT", wa_in)
            load(cols[:, 0:22], "cols", cols_in)
            load(sel16[:, :], "sel16", cols_in)
            load(sel64[:, :], "sel64", cols_in)
            load(kP[:, 0:2, :, :], "A", scan_in)
            for b in range(B):
                sp.wait_ge(A.out_taken, b * H * QT + A.free_out)
                for k in range(4):
                    if b and k == 2:
                        sp.wait_ge(pa_x, QT * b)
                    sp.dma_start(ctxT[:, :, 1024 * k:1024 * k + 1024],
                                 ctx_views(b)[:, :, 1024 * k:1024 * k + 1024]).then_inc(ctx_in[k], 16)
                if b == 0:
                    for m in range(DC):
                        sp.wait_ge(qa_out, (m + 1) * 5)
                        sp.dma_start(qry_parts[m].rearrange("g p k -> p g k"), parts[:, 2 + m, :, :]).then_inc(qa_d, 16)
                    sp.wait_ge(qa_d, 32)
                sp.wait_ge(taps, b * H * TAP_OPS + ONE)
                sp.dma_start(kA, a["AA"][bass.ds(b, 1), :, :, :, :].rearrange("b p h n m -> p (b h) n m"))\
                    .then_inc(scan_in, 16)
                sp.dma_start(kU[:, bass.ds(b * TAU, 1), :, :], a["BC"][bass.ds(b, 1), :, :, :]
                             .rearrange("b p h n -> p b h n")).then_inc(scan_in, 16)
                with sp.Fori(0, NPK // 4) as i:
                    for e in range(4):
                        sp.wait_ge(kp_l, b * NPK + i * 4 + e + 1 + 2)
                        sp.dma_start(key_parts[bass.ds(b, 1), e % 2, :, :, bass.ds(i * 1024 + (e // 2) * 512, 512)]
                                     .rearrange("b g p k -> p (b g) k"), parts[:, e, :, :]).then_inc(kp_d[e], 16)
                for t in range(QT):
                    sp.dma_start(maskw[:, t, :], a["mask"][bass.ds(b, 1), t * P:(t + 1) * P, :]
                                 .rearrange("b p k -> p (b k)")).then_inc(mask_in, 16)
                for e in range(4):
                    sp.wait_ge(kp_d[e], 64 * b + 64 + 16)

                def head_in(h, u):
                    row = (h % 8) * 16
                    for n, (lo, hi) in enumerate(((0, 3), (0, 2), (0, 1))):
                        p0, p1 = (0, 48, 80)[n], (48, 80, 96)[n]
                        sp.dma_start(keyS[p0:p1, u, :],
                                     key_parts[bass.ds(b, 1), bass.ds(h // 8, 1), lo:hi, bass.ds(row, 16), :]
                                     .rearrange("a m g p k -> (a m g) p k")).then_inc(ks_in[u], 16)
                        sp.dma_start(qryS[p0:p1, u, :],
                                     qry_parts[bass.ds(h // 8, 1), n:n + 1, bass.ds(row, 16), bass.ds(b * S, S)]
                                     .rearrange("m g p k -> (m g) p k").broadcast_to([hi, 16, S])).then_inc(ks_in[u], 16)

                head_in(0, 0)
                head_in(1, 1)
                sp.wait_ge(pja_out, b * NPJ + RING + NPJ)
                sp.dma_start(selA, a["selA"]).then_inc(sela_in, 16)
                sp.dma_start(hselA, a["hselA"]).then_inc(sela_in, 16)
                sp.dma_start(BOR, a["bo"]).then_inc(sela_in, 16)
                with sp.Fori(1, H // 2) as p:
                    for u in range(2):
                        sp.wait_ge(A.scored, (b * H + 2 * p + u - 1) * A.ns + ONE)
                        head_in(2 * p + u, u)
                sp.wait_ge(pa_x, QT * b + QT)
                sp.sem_inc(waited, 1)

            load(wgT, "WgT", gate_w_in)
            load(gamma_r, "gamma", gate_w_in)
            load(beta_r, "beta", gate_w_in)
            load(ew, "ew", moe_w_in)
            load(ebr, "eb", moe_w_in)
            load(gw, "gwT", moe_w_in)
            load(gbr, "gb", moe_w_in)
            load(iot, "iota", moe_w_in)
            ctx_t = a["ctx"].rearrange("b (t p) d -> (b t) p d", p=P)

            def tile_load(i, u):
                sp.dma_start(ctile[:, u, :, :], ctx_t[bass.ds(i * 4, 4), :, :].rearrange("t p d -> p t d"))\
                    .then_inc(tile_in[u], 16)

            def tile_store(i, u):
                sp.wait_ge(tile_out, i * 2 + DC + 4)
                sp.dma_start(xl_dram[bass.ds(i, 1), :, :, :].rearrange("a p c k -> p (a c) k"), cturn[:, u, :, :])\
                    .then_inc(tile_kept[u], 16)

            for u in range(2):
                sp.sem_inc(tile_kept[u], 16)
            for u in range(4):
                tile_load(u, u)
            with sp.Fori(0, B * 2 - 1) as i:
                for u in range(4):
                    sp.wait_ge(tile_norm, (4 * i + u) * 2 + 2)
                    sp.wait_ge(tile_norm_act, (4 * i + u) * 2 + 2)
                    tile_load(4 * i + u + 4, u)
                    tile_store(4 * i + u, u % 2)
            for u in range(4):
                tile_store(B * 8 - 4 + u, u % 2)
            for u in range(2):
                sp.wait_ge(tile_kept[u], 16 * (B * 4 + 1))

            def pair_w(w, dst, name, p):
                sp.dma_start(dst, a[name][bass.ds(p, 1), :, :, :].rearrange("a p c n -> p (a c) n")).then_inc(w, 16)

            def context_in(b):
                for k in range(8):
                    sp.dma_start(xlT[:, :, 512 * k:512 * k + 512], xl_dram[b * 8 + k]).then_inc(xl_in, 16)

            context_in(0)
            pair_w(wkc_in, wk, "WkC", 0)
            pair_w(wqc_in, wq, "WqC", 0)
            pair_w(wvc_in, wv, "WvC", 0)
            sp.wait_ge(moe_acc, MOE_ADDS)
            for i in range(2):
                sp.dma_start(woC[i], a["WoC"][:, 8 * i:8 * i + 8, :]).then_inc(cpost_in, 16)
            for b in range(B):
                with sp.Fori(0 if b else 1, 8) as p:
                    sp.wait_ge(pjc_out, (b * 8 + p) * NPC + ONE)
                    pair_w(wqc_in, wq, "WqC", p)
                    pair_w(wkc_in, wk, "WkC", p)
                    pair_w(wvc_in, wv, "WvC", p)
                if b + 1 < B:
                    sp.wait_ge(pjc_out, (b + 1) * 8 * NPC + ONE)
                    context_in(b + 1)
            sp.wait_ge(pa_x, QT * (2 * B))
            load(swq, "sWq", sw_in)
            load(swk, "sWk", sw_in)
            load(swv, "sWv", sw_in)
            load(swo, "sWo", sw_in)
            load(sbv, "sbv", sw_in)
            load(sbo, "sbo", sw_in)
            load(smask, "smask", sw_in)
            load(w1, "W1", fw_in)
            load(w2, "W2", fw_in)
            load(b2r, "b2", fw_in)
            load(fgw, "fWg", fw_in)
            load(fbg, "fbg", fw_in)
            load(fb1, "fb1", fw_in)
            load(iot2, "iota", fw_in)
            sp.wait_ge(f_acc, MOE_ADDS)
            sp.dma_start(out.rearrange("b (t p) d -> p (b t) d", p=P), X[:, :, :]).then_inc(stored, 16)
            sp.wait_ge(stored, 16)

        @block.gpsimd
        def _(pool):
            pool.sem_inc(kp_l, 2)
            pool.sem_inc(taps, ONE)
            pool.memset(ident[:, :], 0.0).then_inc(consts, 1)
            pool.memset(ones[:, :], 1.0).then_inc(consts, 1)
            pool.wait_ge(consts, 2)
            pool.affine_select(out=ident[:, :], in_=ident[:, :], compare_op=ALU.not_equal, fill=1.0, base=0,
                               pattern=[[-1, P]], channel_multiplier=1).then_inc(consts, 1)
            def values_a(h, u):
                pool.tensor_copy(VH[:, u, :, 0:16], val[:, :, bass.ds(h * 16, 16)]).then_inc(vh_ready, 1)

            with pool.Fori(0, B) as b:
                with pool.Fori(0, NPK // 4) as i:
                    for e in range(4):
                        pool.wait_ge(kp_m, b * NPK + i * 4 + e + 1)
                        pool.sem_inc(waited, 1)
                        pool.tensor_tensor(parts[:, e, 2, :], rest[:, e % 2, :], parts[:, e, 1, :], ALU.subtract)\
                            .then_inc(kp_l, 1)
                pool.wait_ge(pja_out, b * NPJ + RING + NPJ)
                pool.sem_inc(waited, 1)
                pool.memset(VH[:, :, :, 16:32], 0.0).then_inc(vh_zero, 1)
                values_a(0, 0)

                def tap(n, ins_of):
                    pool.wait_ge(taps, n + ONE)
                    pool.sem_inc(waited, 1)
                    ins_of().then_inc(taps, 1)

                def fold(n, t, out_):
                    w = NST // 2
                    while w:
                        lo, hi = t[..., 0:w], t[..., w:2 * w]
                        dst = lo if w > 1 else out_.unsqueeze(len(lo.shape) - 1)
                        tap(n, lambda: pool.tensor_tensor(dst, lo, hi, ALU.add))
                        n = n + 1
                        w //= 2

                def weights(h, s_, d_, r_):
                    n = (b * H + h) * TAP_OPS
                    src = kU[:, bass.ds(b * TAU + h, 1), :, :].rearrange("p j h n -> p (j h) n")
                    dst = kU[:, bass.ds(b * TAU + h + 1, 1), :, :].rearrange("p j h n -> p (j h) n")
                    tap(n, lambda: pool.tensor_tensor(kTv, kA, src.unsqueeze(2).broadcast_to([P, 2, NST, NST]), ALU.mult))
                    fold(n + 1, kTv, dst)
                    power = kP[:, bass.ds(s_, 1), :, :].rearrange("p s n m -> p (s n) m")
                    square = kP[:, bass.ds(d_, 1), 4 * r_:4 * r_ + 4, :].rearrange("p s n m -> p (s n) m")
                    tap(n + 5, lambda: pool.tensor_tensor(
                        kTs, power[:, 4 * r_:4 * r_ + 4, :].unsqueeze(2).broadcast_to([P, 4, NST, NST]),
                        power.rearrange("p k m -> p m k").unsqueeze(1).broadcast_to([P, 4, NST, NST]), ALU.mult))
                    fold(n + 6, kTs, square)

                def step(h, u, s_, d_, r_):
                    g = b * H + h
                    pool.wait_ge(A.weighed, g * QT * A.nt + A.free_places)
                    pool.sem_inc(waited, 1)
                    values_a(h + 1, 1 - u)
                    weights(h, s_, d_, r_)

                pool.wait_ge(scan_in, 32 * b + 48)
                pool.sem_inc(waited, 1)
                pool.wait_ge(kp_l, b * NPK + NPK + 2)
                pool.sem_inc(waited, 1)
                with pool.Fori(0, 2) as i:
                    for r_ in range(4):
                        step(4 * i + r_, r_ % 2, i, i + 2, r_)
                for r_ in range(7):
                    step(8 + r_, r_ % 2, 2 + r_ // 4, r_ // 4, r_ % 4)
                weights(15, 3, 1, 3)

            pool.wait_ge(pa_x, QT * B)
            pool.wait_ge(taps, B * H * TAP_OPS + ONE)
            for j in range(TAU):
                pool.tensor_copy(kW[:, j, :, :], kU[:, TAU - 1 - j, :, :]).then_inc(reversed_, 1)

            pool.wait_ge(reversed_, TAU)
            pool.wait_ge(gated, DC)
            for m in range(DC):
                in_terms(pool, terms[1 + m], m, 1).then_inc(pool_terms, 1)
            with pool.Fori(0, B * 2) as i:
                for u in range(4):
                    for t in range(2):
                        pool.wait_ge(tile_rs, 4 * i + u + 1)
                        pool.wait_ge(tile_turn, (4 * i + u) * 2 + 1)
                        pool.sem_inc(waited, 1)
                        pool.tensor_scalar(cnorm[:, u % 2, t, :], ctile[:, u, t, :], cmv[:, u, t, 0:1],
                                           crstd[:, u, t:t + 1], ALU.subtract, ALU.mult).then_inc(tile_norm, 1)
            pool.wait_ge(states, 1)
            for m in range(DC):
                out_terms(pool, terms[1 + m], m, 1).then_inc(pool_terms, 1)
            pool.wait_ge(cols_in, 48)
            def queries_c(p, event=0):
                pool.wait_ge(pjc_out, p * NPC + event + 1 + ONE)
                for u in range(2):
                    pool.tensor_tensor(QP[:, u, :], qC, sel64[:, u:u + 1].broadcast_to([P, S]), ALU.mult)\
                        .then_inc(q_ready, 1)

            def bank_c(u, n):
                return scoreC[:, u, 2 * n:2 * n + 2, :].rearrange("p k q -> p (k q)")

            def sums_c(g, u):
                pool.wait_ge(c_sum, g + 1)
                pool.sem_inc(waited, 1)
                for n in range(1, NSB):
                    pool.wait_ge(c_exp, g * NSG + n // 2 + 1)
                    if n > 1:
                        pool.wait_ge(c_acc, g * (NSB - 1) + n - 1)
                    pool.tensor_tensor(acc[:, u, :], bank_c(u, 0) if n == 1 else acc[:, u, :], bank_c(u, n), ALU.add)\
                        .then_inc(c_acc, 1)

            queries_c(0, NKT - 1)
            sums_c(0, 0)
            with pool.Fori(1, PAIRS) as p:
                queries_c(p)
                sums_c(2 * p - 1, 1)
                sums_c(2 * p, 0)
            sums_c(B * H - 1, 1)

            pool.wait_ge(sq_out, DC)
            for h in range(0, H, 2):
                s_, g = h % 4, h // 4
                pool.tensor_tensor(sQ[:, h, :], QTR[:, s_ // 2, :],
                                   sel16[:, 4 * (s_ % 2) + g:4 * (s_ % 2) + g + 1].broadcast_to([P, B * S]),
                                   ALU.mult).then_inc(s_q, 1)

        @block.scalar
        def _(act):
            def ln_sqrt(k):
                act.wait_ge(ln_aggr, NT4 * (k + 1))
                if k:
                    act.wait_ge(ln_rstd, k)
                act.activation(std[:, :], mv[:, :, 1], ACT.Sqrt, bias=EPS).then_inc(ln_std, 1)

            def ln_evac(k, gain=None, shift=None):
                for c in range(DC):
                    act.wait_ge(ln_turn, DC * k + c + 1)
                    kw = {} if gain is None else dict(scale=cols[:, gain + c:gain + c + 1],
                                                      bias=cols[:, shift + c:shift + c + 1])
                    act.activation(XT[:, c, :], TP[c][:, :], ACT.Identity if kw else ACT.Copy, **kw).then_inc(ln_out, 1)

            act.sem_inc(pja_out, RING)
            act.sem_inc(A.turned_act, A.free_act)
            act.sem_inc(c_kept, ONE)
            act.sem_inc(pjc_out, ONE)
            act.sem_inc(tile_out, 4)
            act.wait_ge(cols_in, 48)
            ln_sqrt(0)
            ln_evac(0)
            act.wait_ge(qa_d, 32)
            with act.Fori(0, B) as b:
                with act.Fori(0, NPK // 4) as i:
                    def high(e):
                        act.wait_ge(kp_mm, b * NPK + i * 4 + e + 1)
                        act.wait_ge(kp_d[e], (b * 4 + i + 1) * 16)
                        act.activation(parts[:, e, 0, :], RB[e][:, :], ACT.Identity,
                                       bias=cols[:, C_BK + e % 2:C_BK + e % 2 + 1]).then_inc(kp_h, 1)

                    def middle(e):
                        act.wait_ge(kp_r, b * NPK + i * 4 + e + 1 + 4)
                        act.activation(parts[:, e, 1, :], rest[:, e % 2, :], ACT.Copy).then_inc(kp_m, 1)

                    high(0)
                    high(1)
                    middle(0)
                    high(2)
                    middle(1)
                    high(3)
                    middle(2)
                    middle(3)
                for n in range(NPJ):
                    act.wait_ge(pja_mm, b * NPJ + n + 1)
                    act.activation(val[:, 2 * n:2 * n + 2, :].rearrange("p k d -> p (k d)"), RB[n % 4][:, :],
                                   ACT.Copy).then_inc(pja_out, 1)

                def exp_quarter(h, u, t, q):
                    g = b * H + h
                    act.wait_ge(A.max_ready, QT * g + t + 1)
                    act.activation(scoreA[:, u, t, q * 1024:(q + 1) * 1024], scoreA[:, u, t, q * 1024:(q + 1) * 1024],
                                   ACT.Exp, bias=nmax[:, u, t:t + 1],
                                   accum_out=dpart[:, t, bass.ds(h * 4 + q, 1)]).then_inc(A.exp_done, 1)

                def unit(h, u, t, last=False):
                    y = QT * (b * H + h) + t
                    for n in range(A.nt):
                        if n in A.by_act:
                            act.wait_ge(A.turned, y * A.nt + n + 1)
                            act.wait_ge(A.weighed, y * A.nt + n + 1)
                            act.activation(PT[:, n % 4, :], RB[n % 4][:, :], ACT.Copy).then_inc(A.turned_act, 1)
                        if n % 2 == 0 and not last:
                            if t + 1 < QT:
                                exp_quarter(h, u, t + 1, n // 2)
                            else:
                                exp_quarter(h + 1, 1 - u, 0, n // 2)

                for q in range(4):
                    exp_quarter(0, 0, 0, q)
                with act.Fori(0, H - 2, 2) as i:
                    for u in range(2):
                        for t in range(QT):
                            unit(i + u, u, t)
                for h in range(H - 2, H):
                    for t in range(QT):
                        unit(h, h % 2, t, last=(h == H - 1 and t == QT - 1))
                post_act(act, b)

            ln_sqrt(1)
            ln_evac(1)
            for m in range(DC):
                act.wait_ge(gate_mm, m + 1)
                act.activation(GT[:, m, :], PJ[m][:, :], ACT.Sigmoid, bias=cols[:, C_BG + m:C_BG + m + 1])\
                    .then_inc(gate_act, 1)
            act.wait_ge(conv, K_READY)
            for j in range(DC * (TAU + 1)):
                m, k = divmod(j, TAU + 1)
                if j >= len(tap_ring):
                    act.wait_ge(tap_mm, j - len(tap_ring) + 1)
                act.activation(tap_ring[j % len(tap_ring)], ident[:, :], ACT.Copy,
                               scale=cols[:, C_DP + m:C_DP + m + 1] if k == 0 else K16[:, k - 1, m:m + 1])\
                    .then_inc(tap_diag, 1)

            def tile_turned(e, u):
                for c in range(DC):
                    act.wait_ge(tile_turn, e * 2 + c + 1 + 4)
                    act.wait_ge(tile_kept[u], e // 2 * 16 + 16)
                    act.activation(cturn[:, u, c, :], RB[2 * u + c][:, :], ACT.Identity,
                                   scale=cols[:, C_G1 + c:C_G1 + c + 1],
                                   bias=cols[:, C_B1 + c:C_B1 + c + 1]).then_inc(tile_out, 1)

            def tile_normed(e, u, first=False):
                act.wait_ge(tile_ag, (e + 1) * 4)
                act.activation(cstd[:, u, :], cmv[:, u, :, 1], ACT.Sqrt, bias=EPS).then_inc(tile_sq, 1)
                for t in range(2, 4):
                    act.wait_ge(tile_shift, e + 1)
                    act.wait_ge(tile_turn, e * 2 + 1)
                    act.activation(cnorm[:, u % 2, t, :], ctile[:, u, t, :], ACT.Identity, scale=crstd[:, u, t:t + 1],
                                   bias=cshift[:, u, t:t + 1]).then_inc(tile_norm_act, 1)

            tile_normed(0, 0)
            with act.Fori(0, B * 2 - 1) as i:
                for u in range(4):
                    tile_normed(4 * i + u + 1, (u + 1) % 4)
                    tile_turned(4 * i + u, u % 2)
            for u in range(4):
                if u < 3:
                    tile_normed(B * 8 - 3 + u, u + 1)
                tile_turned(B * 8 - 4 + u, u % 2)
            for t in range(NT4):
                act.wait_ge(y_turn, 2 * t + 2)
                act.activation(YT[:, t, :], SP_[t % 2][:, 0:D], ACT.Copy).then_inc(y_norm, 1)
            ln_sqrt(2)
            ln_sqrt(3)
            ln_evac(2)
            act.wait_ge(moe_g, MG_NEG)
            act.activation(G[:, 8, :, :], G[:, 7, :, :], ACT.Exp).then_inc(moe_g, 1)
            act.wait_ge(moe_gt, 1)
            act.activation(gateT, SP_[0][0:E8, :], ACT.Copy).then_inc(moe_gtc, 1)
            def latents(b):
                act.activation(latT, latAll[:, :, b * S:(b + 1) * S], ACT.Copy).then_inc(lat_copy, 1)

            def on_diagonal(g):
                act.wait_ge(c_max, g + 1)
                for t in range(QT):
                    act.activation(diag[:, t * P:(t + 1) * P], ident[:, :], ACT.Copy, scale=nmax[:, 0, t:t + 1])\
                        .then_inc(c_diag, 1)

            def exps_c(g, u, groups):
                for k in groups:
                    act.wait_ge(c_sub, g * NSG + k + 1 + ONE)
                    e = scoreC[:, u, 4 * k:min(4 * k + 4, NKC), :]
                    act.activation(e, e, ACT.Exp).then_inc(c_exp, 1)

            def projected(p, e0, n, dst, src, **kw):
                act.wait_ge(pjc_mm, p * NPC + e0 + n + 1)
                act.activation(dst, PJ[(e0 + n) % 2][:, 0:src], ACT.Copy, **kw).then_inc(pjc_out, 1)

            def keys_c(p, g=None):
                projected(p, 0, 0, qC, S, scale=SCL)
                for n in range(NKT):
                    if g is not None and n == 1:
                        on_diagonal(g)
                    w = min(512, S2 + S - n * 512)
                    projected(p, 1, n, keyC[:, n * 512:n * 512 + w], w, scale=SCL)
                    if g is not None:
                        exps_c(g, 1, AT_PROJECTED.get(n, ()))

            def values_c(p, g):
                for n in range(NKT):
                    if n == 2:
                        on_diagonal(g)
                    w = min(4, NKC - 4 * n)
                    projected(p, 1 + NKT, n, valC[:, 4 * n:4 * n + w, :].rearrange("p k d -> p (k d)"), w * P)
                    exps_c(g, 0, AT_PROJECTED.get(n, ()))

            def kept(g, u, before=True):
                for n in range(NSB):
                    act.wait_ge(c_scored, g * NSB + n + 1)
                    act.activation(scoreC[:, u, 2 * n:2 * n + 2, :].rearrange("p k q -> p (k q)"), SP_[n % 3][:, :],
                                   ACT.Copy).then_inc(c_kept, 1)
                    if before:
                        exps_c(g - 1, 1 - u, AT_SCORED.get(n, ()))

            def pair(p):
                keys_c(p, 2 * p - 1)
                kept(2 * p, 0)
                values_c(p, 2 * p)
                kept(2 * p + 1, 1)

            ln_sqrt(4)
            for n in range(S2 // 512):
                if n == 2:
                    ln_sqrt(5)
                projected(0, 0, n, keyC[:, n * 512:n * 512 + 512], 512, scale=SCL)
            ln_evac(3, C_G2, C_B2)
            act.wait_ge(ln_out, 8)
            for c in range(DC):
                act.activation(latAll[:, c, :], XT[:, c, :], ACT.Copy).then_inc(lat_done, 1)
            act.wait_ge(lat_done, DC)
            latents(0)
            projected(0, NKT - 1, 0, qC, S, scale=SCL)
            projected(0, NKT, 0, keyC[:, S2:S2 + S], S, scale=SCL)
            kept(0, 0, before=False)
            values_c(0, 0)
            kept(1, 1)
            for b in range(B):
                if b:
                    latents(b)
                    pair(8 * b)
                with act.Fori(8 * b + 1, 8 * b + 8) as p:
                    pair(p)
            on_diagonal(B * H - 1)
            exps_c(B * H - 1, 1, range(NSG))
            ln_sqrt(6)
            ln_evac(4)
            act.wait_ge(skv_mm, 1)
            act.activation(sK, PJ[0][:, :], ACT.Identity, bias=cols[:, C_SK:C_SK + 1]).then_inc(skv_out, 1)
            for t in range(NT4):
                act.wait_ge(skv_mm, 1 + NT4)
                act.activation(sV[:, t, :], PJ[1][:, t * 64:t * 64 + 64], ACT.Copy).then_inc(skv_out, 1)
            act.wait_ge(sq_out, DC)
            for h in range(1, H, 2):
                s_, g = h % 4, h // 4
                act.activation(sQ[:, h, :], QTR[:, s_ // 2, :], ACT.Copy,
                               scale=sel16[:, 4 * (s_ % 2) + g:4 * (s_ % 2) + g + 1]).then_inc(s_qa, 1)
            for t in range(NT4):
                for h in range(H):
                    act.wait_ge(s_nm, t + 1)
                    seen = (t % QT + 1) * P
                    act.activation(sS[:, t, h, 0:seen], sS[:, t, h, 0:seen], ACT.Exp, bias=smx[:, t, h:h + 1],
                                   accum_out=sden[:, t, h:h + 1]).then_inc(s_ex, 1)
            for c in range(DC):
                act.wait_ge(s_ot, c + 1)
                act.activation(sOT[:, c, :], TP[c][:, :], ACT.Copy).then_inc(s_oc, 1)
            ln_sqrt(7)
            ln_evac(5)
            for n in range(2 * E8):
                act.wait_ge(f_h, n + 1)
                act.activation(hT[:, n // 2, n % 2, :], RB[n % 4][:, :], ACT.Gelu, bias=fb1[:, n:n + 1])\
                    .then_inc(f_ge, 1)
            act.wait_ge(f_gt, 1)
            act.activation(gateT2, SP_[0][0:E8, :], ACT.Copy).then_inc(f_gtc, 1)

        @block.tensor
        def _(pe):
            def ln_pe(k, kx):
                pe.wait_ge(ln_norm, NT4 * (k + 1))
                if kx:
                    pe.wait_ge(ln_out, DC * kx)
                for c in range(DC):
                    for t in range(NT4):
                        mm = pe.transpose(TP[c][:, t * P:(t + 1) * P], XN[:, t, c * P:(c + 1) * P], ident[:, :])
                    mm.then_inc(ln_turn, 1)

            def turn_gates(Gt, row, ready, count, done):
                pe.wait_ge(ready, count)
                for t in range(NT4):
                    mm = pe.transpose(SP_[0][0:E8, t * P:(t + 1) * P], Gt[:, row, t, :], ident[:, :])
                mm.then_inc(done, 1)

            def biases(gates, b_, ready, done):
                pe.wait_ge(ready, 1)
                for t in range(NT4):
                    pe.matmul(SP_[1 + t // 2][:, (t % 2) * D:(t % 2 + 1) * D], gates[:, t * P:(t + 1) * P], b_,
                              start=True, stop=True).then_inc(done, 1)

            pe.sem_inc(A.weighed, A.free_places)
            pe.sem_inc(A.scored, ONE)
            pe.sem_inc(c_sum, 2)
            pe.sem_inc(tile_turn, 4)
            pe.wait_ge(consts, 3)
            pe.wait_ge(wqa_in, 16)
            ln_pe(0, 0)
            pe.wait_ge(ln_out, DC)
            wqa = RV[:, 0:512].rearrange("p (c n) -> p c n", c=DC)
            for m in range(DC):
                for c in range(DC):
                    mm = pe.matmul(PJ[m][:, :], wqa[:, c, m * P:(m + 1) * P], XT[:, c, :],
                                   start=(c == 0), stop=(c == DC - 1))
                mm.then_inc(qa_mm, 1)
            pe.wait_ge(wa_in, 48)
            pe.wait_ge(qa_out, 5 * DC)
            with pe.Fori(0, B) as b:
                for i in range(4):
                    pe.wait_ge(ctx_in[i], 16 * b + 16)
                    pe.sem_inc(waited, 1)
                    for e in range(4):
                        pe.wait_ge(kp_r, b * NPK + i * 4 + e + 1)
                        for c in range(DC):
                            mm = pe.matmul(RB[e][:, :], WA[:, 0, c, (e % 2) * P:(e % 2 + 1) * P],
                                           ctxT[:, c, i * 1024 + (e // 2) * 512:i * 1024 + (e // 2) * 512 + 512],
                                           start=(c == 0), stop=(c == DC - 1))
                        mm.then_inc(kp_mm, 1)
                for n in range(NPJ):
                    if n < 4:
                        pe.wait_ge(kp_r, b * NPK + NPK + n + 1)
                    pe.wait_ge(pja_out, b * NPJ + n + 1)
                    for kk in range(2):
                        for c in range(DC):
                            mm = pe.matmul(RB[n % 4][:, kk * D:(kk + 1) * D],
                                           ctxT[:, c, (2 * n + kk) * P:(2 * n + kk + 1) * P], WA[:, 1, c, :],
                                           start=(c == 0), stop=(c == DC - 1))
                    mm.then_inc(pja_mm, 1)
                pe.wait_ge(pja_out, b * NPJ + RING + NPJ)

                def score(h, u, t, n):
                    g = b * H + h
                    if n == 0 and t == 0:
                        pe.wait_ge(ks_in[u], (b * (H // 2) + (h - u) // 2 + 1) * QK_IN)
                    pe.wait_ge(A.score_out, g * A.ns + t * A.nt + n + 1)
                    pe.matmul(SP_[n % 2][:, :], qryS[:, u, t * P:(t + 1) * P],
                              keyS[:, u, n * 512:(n + 1) * 512], start=True, stop=True).then_inc(A.scored, 1)

                def turn(h, u, t, n):
                    y = QT * (b * H + h) + t
                    if n % 2 == 0:
                        pe.wait_ge(A.exp_done, y * 4 + n // 2 + 1)
                    if n >= 4:
                        pe.wait_ge(*A.copied(y, n - 4))
                    else:
                        pe.wait_ge(*A.copied(y, n - 4 + A.nt, -1))
                    for c in range(4):
                        mm = pe.transpose(RB[n % 4][:, c * P:(c + 1) * P],
                                          scoreA[:, u, t, (4 * n + c) * P:(4 * n + c + 1) * P], ident[:, :])
                    mm.then_inc(A.turned, 1)

                def weigh(h, u, t, n):
                    y = QT * (b * H + h) + t
                    if n == 0:
                        pe.wait_ge(A.out_taken, y + 1)
                        if t == 0:
                            pe.wait_ge(vh_zero, b + 1)
                            pe.wait_ge(vh_ready, b * H + h + 1)
                    pe.wait_ge(*A.copied(y, n))
                    for c in range(4):
                        mm = pe.matmul(OT[t][A.width * c:A.width * (c + 1), 0:P], VH[:, u, 4 * n + c, :],
                                       PT[:, n % 4, c * P:(c + 1) * P], start=n == 0, stop=n == A.nt - 1,
                                       skip_group_check=True)
                    mm.then_inc(A.weighed, 1)

                def head(h, u, first=False, last=False):
                    for t in range(QT):
                        for n in range(A.nt):
                            if not last:
                                score(h + 1, 1 - u, t, n)
                            turn(h, u, t, n)
                            if n >= 2:
                                weigh(h, u, t, n - 2)
                            elif t:
                                weigh(h, u, t - 1, n - 2 + A.nt)
                            elif not first:
                                weigh(h - 1, 1 - u, QT - 1, n - 2 + A.nt)

                for t in range(QT):
                    for n in range(A.nt):
                        score(0, 0, t, n)
                head(0, 0, first=True)
                head(1, 1)
                with pe.Fori(1, H // 2 - 1) as i:
                    for u in range(2):
                        head(2 * i + u, u)
                head(H - 2, 0)
                head(H - 1, 1, last=True)
                for n in (A.nt - 2, A.nt - 1):
                    weigh(H - 1, 1, QT - 1, n)
                post_pe(pe, b)

            ln_pe(1, 1)
            pe.wait_ge(ln_out, 2 * DC)
            pe.wait_ge(gate_w_in, 48)
            for m in range(DC):
                for c in range(DC):
                    mm = pe.matmul(PJ[m][:, :], wgT[:, c, m * P:(m + 1) * P], XT[:, c, :],
                                   start=(c == 0), stop=(c == DC - 1))
                mm.then_inc(gate_mm, 1)
            pe.wait_ge(gated, DC)
            for m in range(DC):
                pe.matmul(YP[m][:, :], ident[:, :], XG[:, m, :, :], start=True, stop=False, skip_group_check=True)
                for i in range(TAU + 1):
                    j = m * (TAU + 1) + i
                    k = max(0, i - 1)
                    pe.wait_ge(tap_diag, j + 1)
                    yv = YP[m][:, :].rearrange("p (b c j) -> p b c j", b=B, j=TAU)[:, :, :, k:TAU]
                    xv = XG[:, m, :, :].rearrange("p b (c j) -> p b c j", j=TAU)[:, :, :, 0:TAU - k]
                    pe.matmul(yv, tap_ring[j % len(tap_ring)], xv, start=False, stop=(i == TAU), skip_group_check=True)\
                        .then_inc(tap_mm, 1)
            pe.wait_ge(gate_act, DC)
            with pe.Fori(0, B * 4) as i:
                for u in range(2):
                    pe.wait_ge(tile_norm, (2 * i + u) * 2 + 2)
                    pe.wait_ge(tile_norm_act, (2 * i + u) * 2 + 2)
                    pe.wait_ge(tile_out, (2 * i + u) * 2 + 2)
                    for c in range(DC):
                        for t in range(4):
                            mm = pe.transpose(RB[2 * u + c][:, t * P:(t + 1) * P], cnorm[:, u, t, c * P:(c + 1) * P],
                                              ident[:, :])
                        mm.then_inc(tile_turn, 1)
            pe.wait_ge(tile_out, B * 8 * 2 + 4)
            pe.wait_ge(y_done, DC * B + DC)
            for t in range(NT4):
                if t >= 2:
                    pe.wait_ge(y_norm, t - 1)
                for m in range(DC):
                    pe.transpose(SP_[t % 2][:, m * P:(m + 1) * P],
                                 Y[:, m, t // QT, (t % QT) * P:(t % QT + 1) * P], ident[:, :]).then_inc(y_turn, 1)
            ln_pe(3, 2)
            pe.wait_ge(ln_out, 3 * DC)
            pe.wait_ge(moe_w_in, 80)
            for t in range(NT4):
                for c in range(DC):
                    pe.matmul(OP[:, t * E8:(t + 1) * E8], XT[:, c, t * P:(t + 1) * P], gw[:, c, :],
                              start=(c == 0), stop=False)
                pe.matmul(OP[:, t * E8:(t + 1) * E8], ones[0:1, :], gbr, start=False, stop=True).then_inc(moe_lg, 1)
            for n in range(NT4 * 4):
                t, e2 = n // 4, n % 4
                if n >= 4:
                    pe.wait_ge(moe_acc, 2 * (n - 3))
                for c in range(DC):
                    mm = pe.matmul(RB[n % 4][:, :], XT[:, c, t * P:(t + 1) * P], ew[:, c, e2 * 512:(e2 + 1) * 512],
                                   start=(c == 0), stop=(c == DC - 1))
                mm.then_inc(moe_mm, 1)
                if n == 8:
                    turn_gates(G, 12, moe_g, MG_NEG + 5, moe_gt)
            biases(gateT, ebr, moe_gtc, moe_b)
            def lhs(k, c):
                return xlT[:, c, k * P:(k + 1) * P] if k < S2 // P else latT[:, c, (k - S2 // P) * P:(k - S2 // P + 1) * P]

            def project(p, n, mms):
                pe.wait_ge(pjc_out, p * NPC + max(0, n - 1) + ONE)
                for o, l, r, st, sp_ in mms:
                    mm = pe.matmul(PJ[n % 2][:, o[0]:o[1]], l, r, start=st, stop=sp_)
                mm.then_inc(pjc_mm, 1)

            def turn_max(g):
                pe.wait_ge(c_run, g * RUN + RUN + ONE)
                pe.wait_ge(c_sub, g * NSG + ONE)
                for t in range(QT):
                    mm = pe.transpose(TP[0][:, t * P:(t + 1) * P], half_max[:, t * P:(t + 1) * P], ident[:, :])
                mm.then_inc(c_turned, 1)

            def spread_max(g):
                pe.wait_ge(c_diag, g * QT + QT)
                pe.matmul(TP[0][:, S:2 * S], ones[:, :], diag, start=True, stop=True).then_inc(c_spread, 1)

            def keys_c(p, g=None):
                pe.wait_ge(wqc_in, p * 16 + 16)
                project(p, 0, [((0, S), wq[:, c, :], latT[:, c, :], c == 0, c == DC - 1) for c in range(DC)])
                pe.wait_ge(wkc_in, p * 16 + 16)
                for n in range(NKT):
                    w = min(512, S2 + S - n * 512)
                    project(p, 1 + n, [((0, w), wk[:, c, :], xlT[:, c, n * 512:n * 512 + w] if n < 8 else latT[:, c, :],
                                        c == 0, c == DC - 1) for c in range(DC)])
                    if g is not None and n == 1:
                        spread_max(g)

            def values_p(p, g):
                pe.wait_ge(wvc_in, p * 16 + 16)
                for n in range(NKT):
                    w = min(4, NKC - 4 * n)
                    project(p, 1 + NKT + n, [((kk * P, (kk + 1) * P), lhs(4 * n + kk, c), wv[:, c, :],
                                              c == 0, c == DC - 1) for kk in range(w) for c in range(DC)])
                    if n == 2:
                        spread_max(g)

            def scores_c(p, u):
                g = 2 * p + u
                pe.wait_ge(q_ready, g + 1)
                pe.wait_ge(c_kept, g * NSB + ONE)
                for n in range(NSB):
                    if u == 0 and n % 2 == 0:
                        pe.wait_ge(pjc_out, p * NPC + 2 + n // 2 + ONE)
                    if n >= 3:
                        pe.wait_ge(c_kept, g * NSB + n - 2 + ONE)
                    for k in range(2):
                        mm = pe.matmul(SP_[n % 3][:, k * S:(k + 1) * S], keyC[:, (2 * n + k) * P:(2 * n + k + 1) * P],
                                       QP[:, u, :], start=True, stop=True)
                    mm.then_inc(c_scored, 1)

            def weigh_c(g, u, p):
                pe.wait_ge(pjc_out, p * NPC + NPC + ONE)
                pe.wait_ge(c_out, g + ONE)
                for k in range(NKC):
                    if k % 4 == 0:
                        pe.wait_ge(c_exp, g * NSG + k // 4 + 1)
                    j = k % 2
                    mm = pe.matmul(OP[64 * j:64 * j + 64, 0:S], valC[:, k, 64 * u:64 * u + 64], scoreC[:, u, k, :],
                                   start=k < 2, stop=k >= NKC - 2, skip_group_check=True)
                mm.then_inc(c_weighed, 1)

            def sum_c(g, u):
                pe.wait_ge(c_acc, (g + 1) * (NSB - 1))
                for k in range(2):
                    mm = pe.matmul(TP[1][:, 0:S], ones[:, :], acc[:, u, k * S:(k + 1) * S],
                                   start=(k == 0), stop=(k == 1))
                mm.then_inc(c_sum, 1)

            def project_out(b, heads):
                pe.wait_ge(c_out, b * H + heads[-1] + 1 + ONE)
                pe.wait_ge(cpost_in, 32)
                pe.wait_ge(c_kept, min((b + 1) * H + 1, B * H) * NSB + ONE)
                for t in range(QT):
                    for h in heads:
                        mm = pe.matmul(SP_[t][:, 0:D], OA[:, h, t * P:(t + 1) * P], woC[h // 8][:, h % 8, :],
                                       start=(h == 0), stop=(h == H - 1))
                    if heads[-1] == H - 1:
                        mm.then_inc(pa_y, 1)

            def pair(p, after=None):
                keys_c(p, 2 * p - 1)
                scores_c(p, 0)
                weigh_c(2 * p - 1, 1, p - 1)
                sum_c(2 * p - 1, 1)
                turn_max(2 * p)
                if after is not None:
                    project_out(after, range(H))
                    pe.wait_ge(pa_x, QT * (after + B) + QT)
                values_p(p, 2 * p)
                scores_c(p, 1)
                weigh_c(2 * p, 0, p)
                sum_c(2 * p, 0)
                turn_max(2 * p + 1)

            pe.wait_ge(moe_acc, MOE_ADDS)
            pe.wait_ge(xl_in, 128)
            pe.wait_ge(wkc_in, 16)
            for n in range(S2 // 512):
                project(0, n, [((0, 512), wk[:, c, :], xlT[:, c, n * 512:n * 512 + 512], c == 0, c == DC - 1)
                               for c in range(DC)])
            ln_pe(5, 3)
            pe.wait_ge(lat_copy, 1)
            pe.wait_ge(wqc_in, 16)
            for n, w in ((NKT - 1, wq), (NKT, wk)):
                project(0, n, [((0, S), w[:, c, :], latT[:, c, :], c == 0, c == DC - 1) for c in range(DC)])
            scores_c(0, 0)
            turn_max(0)
            values_p(0, 0)
            scores_c(0, 1)
            weigh_c(0, 0, 0)
            sum_c(0, 0)
            turn_max(1)
            for b in range(B):
                if b:
                    pe.wait_ge(xl_in, 128 * b + 128)
                    pe.wait_ge(lat_copy, b + 1)
                    pair(8 * b, after=b - 1)
                with pe.Fori(8 * b + 1, 8 * b + 8) as p:
                    pair(p)
            spread_max(B * H - 1)
            weigh_c(B * H - 1, 1, PAIRS - 1)
            project_out(B - 1, range(H - 1))
            sum_c(B * H - 1, 1)
            project_out(B - 1, range(H - 1, H))
            pe.wait_ge(pa_x, QT * 2 * B)
            ln_pe(6, 4)
            pe.wait_ge(ln_out, 5 * DC)
            pe.wait_ge(sw_in, 7 * 16)
            for m in range(DC):
                for c in range(DC):
                    mm = pe.matmul(SP_[m][:, :], swq[:, c, m * P:(m + 1) * P], XT[:, c, :],
                                   start=(c == 0), stop=(c == DC - 1))
                mm.then_inc(sq_mm, 1)
            for c in range(DC):
                mm = pe.matmul(PJ[0][:, :], swk[:, c, :], XT[:, c, :], start=(c == 0), stop=(c == DC - 1))
            mm.then_inc(skv_mm, 1)
            for t in range(NT4):
                for c in range(DC):
                    pe.matmul(PJ[1][:, t * 64:t * 64 + 64], XT[:, c, t * P:(t + 1) * P], swv[:, c, :],
                              start=(c == 0), stop=False)
                pe.matmul(PJ[1][:, t * 64:t * 64 + 64], ones[0:1, :], sbv, start=False, stop=True).then_inc(skv_mm, 1)
            pe.wait_ge(sq_out, DC)
            pe.wait_ge(skv_out, 1 + NT4)

            def self_scores(n):
                t, h2 = divmod(n, H // 2)
                nb = t % QT + 1
                if t == 0:
                    pe.wait_ge(s_q, h2 + 1)
                    pe.wait_ge(s_qa, h2 + 1)
                if n >= 3:
                    pe.wait_ge(s_ev, n - 2)
                for hh in range(2):
                    mm = pe.matmul(SP_[n % 3][:, hh * S:hh * S + nb * P], sQ[:, 2 * h2 + hh, t * P:(t + 1) * P],
                                   sK[:, t // QT * S:t // QT * S + nb * P], start=True, stop=True)
                mm.then_inc(s_mm, 1)

            steps = NT4 * H // 2
            for n in range(H):
                self_scores(n)
            for n in range(steps):
                t, h2 = divmod(n, H // 2)
                nb = t % QT + 1
                if n + H < steps:
                    self_scores(n + H)
                pe.wait_ge(s_ex, 2 * n + 2)
                if n >= 2:
                    pe.wait_ge(s_tc, n - 1)
                for hh in range(2):
                    for k in range(nb):
                        mm = pe.transpose(TP[n % 2][:, (hh * nb + k) * P:(hh * nb + k + 1) * P],
                                          sS[:, t, 2 * h2 + hh, k * P:(k + 1) * P], ident[:, :])
                mm.then_inc(s_t, 1)
                if n >= 1:
                    self_weigh(pe, n - 1)
            self_weigh(pe, steps - 1)
            for c in range(DC):
                pe.wait_ge(s_on, NT4)
                pe.wait_ge(s_tc, steps)
                for t in range(NT4):
                    mm = pe.transpose(TP[c][:, t * P:(t + 1) * P], sO[:, t, c * P:(c + 1) * P], ident[:, :])
                mm.then_inc(s_ot, 1)
            pe.wait_ge(s_oc, DC)
            for t in range(NT4):
                for c in range(DC):
                    pe.matmul(RB[t][:, 0:D], sOT[:, c, t * P:(t + 1) * P], swo[:, c, :], start=(c == 0), stop=False)
                pe.matmul(RB[t][:, 0:D], ones[0:1, :], sbo, start=False, stop=True).then_inc(s_y, 1)
            ln_pe(7, 5)
            pe.wait_ge(ln_out, 6 * DC)
            pe.wait_ge(fw_in, 7 * 16)
            for t in range(NT4):
                for c in range(DC):
                    pe.matmul(OP[:, t * E8:(t + 1) * E8], XT[:, c, t * P:(t + 1) * P], fgw[:, c, :],
                              start=(c == 0), stop=False)
                pe.matmul(OP[:, t * E8:(t + 1) * E8], ones[0:1, :], fbg, start=False, stop=True).then_inc(f_lg, 1)
            for n in range(2 * E8):
                if n >= 4:
                    pe.wait_ge(f_ge, n - 3)
                for c in range(DC):
                    mm = pe.matmul(RB[n % 4][:, :], w1[:, c, n * P:(n + 1) * P], XT[:, c, :],
                                   start=(c == 0), stop=(c == DC - 1))
                mm.then_inc(f_h, 1)
            turn_gates(G2, 1, f_g, FG_HOT, f_gt)
            for n in range(NT4 * E8):
                t, e = n % NT4, n // NT4
                pe.wait_ge(f_ge, 2 * E8)
                if n >= 4:
                    pe.wait_ge(f_acc, n - 3)
                for c in range(DC):
                    mm = pe.matmul(RB[n % 4][:, 0:D], hT[:, e, c, t * P:(t + 1) * P], w2[:, e, c, :],
                                   start=(c == 0), stop=(c == DC - 1))
                mm.then_inc(f_y, 1)
                if n == NT4:
                    biases(gateT2, b2r, f_gtc, f_b)

        @block.vector
        def _(dve):
            def ln_dve(k, src):
                for t in range(NT4):
                    dve.bn_stats(stats[:, t, :], src[:, t, :]).then_inc(ln_stat, 1)
                for t in range(NT4):
                    dve.wait_ge(ln_stat, NT4 * k + t + 1)
                    dve.bn_aggr(mv[:, t, :], stats[:, t, :]).then_inc(ln_aggr, 1)
                dve.wait_ge(ln_aggr, NT4 * (k + 1))
                dve.wait_ge(ln_std, k + 1)
                dve.reciprocal(rstd[:, :], std[:, :]).then_inc(ln_rstd, 1)
                dve.wait_ge(ln_rstd, k + 1)
                for t in range(NT4):
                    dve.tensor_scalar(XN[:, t, :], src[:, t, :], mv[:, t, 0:1], rstd[:, t:t + 1],
                                      ALU.subtract, ALU.mult).then_inc(ln_norm, 1)

            dve.sem_inc(kp_r, 4)
            dve.sem_inc(A.score_out, A.free_scores)
            dve.sem_inc(A.turned_dve, A.free_dve)
            dve.sem_inc(A.out_taken, A.free_out)
            for s_ in (c_run, c_sub, c_out):
                dve.sem_inc(s_, ONE)
            dve.wait_ge(x_in, 16)
            ln_dve(0, X)
            dve.wait_ge(cols_in, 48)
            for m in range(DC):
                def split(ins):
                    ins.then_inc(qa_out, 1)
                    split.n += 1
                    dve.wait_ge(qa_out, 5 * m + split.n)

                split.n = 0
                high, middle, low = [parts[:, 2 + m, g, :] for g in range(3)]
                dve.wait_ge(qa_mm, m + 1)
                split(dve.tensor_scalar(rest[:, m, :], PJ[m][:, :], cols[:, C_BQ + m:C_BQ + m + 1], 0.25,
                                        ALU.add, ALU.mult))
                split(dve.tensor_copy(high, rest[:, m, :]))
                split(dve.tensor_tensor(rest[:, m, :], rest[:, m, :], high, ALU.subtract))
                split(dve.tensor_copy(middle, rest[:, m, :]))
                split(dve.tensor_tensor(low, rest[:, m, :], middle, ALU.subtract))

            with dve.Fori(0, B) as b:
                dve.wait_ge(taps, b * H * TAP_OPS + ONE)
                dve.sem_inc(waited, 1)
                with dve.Fori(0, NPK // 4) as i:
                    for e in range(4):
                        dve.wait_ge(kp_h, b * NPK + i * 4 + e + 1)
                        dve.wait_ge(kp_l, b * NPK + i * 4 + e + 1)
                        dve.scalar_tensor_tensor(out=rest[:, e % 2, :], in0=RB[e][:, :],
                                                 scalar=cols[:, C_BK + e % 2:C_BK + e % 2 + 1],
                                                 in1=parts[:, e, 0, :], op0=ALU.add, op1=ALU.subtract)\
                            .then_inc(kp_r, 1)
                dve.wait_ge(mask_in, 32 * b + 32)
                dve.wait_ge(pja_out, b * NPJ + RING + NPJ)
                for t in range(QT):
                    dve.tensor_scalar(maskb[:, t, :], maskw[:, t, :], 0.0, NEG, ALU.is_equal, ALU.mult)\
                        .then_inc(mask_ready, 1)
                dve.wait_ge(mask_ready, 2 * b + 2)

                def score_taken(h, u, t, n):
                    g = b * H + h
                    dve.wait_ge(A.scored, g * A.ns + t * A.nt + n + 1 + ONE)
                    dve.sem_inc(waited, 1)
                    dve.tensor_tensor_reduce(scoreA[:, u, t, n * 512:(n + 1) * 512], SP_[n % 2][:, :],
                                             maskb[:, t, n * 512:(n + 1) * 512], 1.0, NEG, ALU.add, ALU.max,
                                             mpart[:, u, t, n:n + 1]).then_inc(A.score_out, 1)
                    if n == A.nt - 1:
                        dve.wait_ge(A.score_out, g * A.ns + (t + 1) * A.nt + A.free_scores)
                        dve.tensor_reduce(nmax[:, u, t:t + 1], mpart[:, u, t, 0:A.nt], AX.X, ALU.max, negate=True)\
                            .then_inc(A.max_ready, 1)

                def out_taken(h, t):
                    y = QT * (b * H + h) + t
                    dve.wait_ge(A.weighed, y * A.nt + A.nt + A.free_places)
                    dve.tensor_copy(OA[:, bass.ds(h, 1), t * P:(t + 1) * P].rearrange("p a k -> p (a k)"),
                                    OT[t][:, 0:P]).then_inc(A.out_taken, 1)

                def head(h, u, first=False, last=False):
                    for t in range(QT):
                        y = QT * (b * H + h) + t
                        for n in range(A.nt):
                            if not last:
                                score_taken(h + 1, 1 - u, t, n)
                            if n in A.by_dve:
                                dve.wait_ge(A.turned, y * A.nt + n + 1)
                                dve.wait_ge(A.weighed, y * A.nt + n + 1)
                                dve.tensor_copy(PT[:, n % 4, :], RB[n % 4][:, :]).then_inc(A.turned_dve, 1)
                            if n == 1 and t:
                                out_taken(h, t - 1)
                            elif n == 1 and not first:
                                out_taken(h - 1, QT - 1)

                for t in range(QT):
                    for n in range(A.nt):
                        score_taken(0, 0, t, n)
                head(0, 0, first=True)
                head(1, 1)
                with dve.Fori(1, H // 2 - 1) as i:
                    for u in range(2):
                        head(2 * i + u, u)
                head(H - 2, 0)
                head(H - 1, 1, last=True)
                out_taken(H - 1, QT - 1)
                post_dve(dve, b)

            ln_dve(1, X)
            for m in range(DC):
                dve.wait_ge(gate_act, m + 1)
                dve.tensor_tensor(XG[:, m, :, :], XT[:, m, :].rearrange("p (b k) -> p b k", b=B),
                                  GT[:, m, :].rearrange("p (b k) -> p b k", b=B), ALU.mult).then_inc(gated, 1)
            dve.wait_ge(gated, DC)
            dve.wait_ge(cols_in, 48)
            count = [0]

            def scan(ins):
                count[0] += 1
                ins.then_inc(conv, 1)
                return count[0]

            def tile_reciprocal(e):
                dve.wait_ge(tile_sq, e + 1)
                dve.reciprocal(crstd[:, e % 4, :], cstd[:, e % 4, :]).then_inc(tile_rs, 1)
                dve.wait_ge(tile_rs, e + 1)
                dve.scalar_tensor_tensor(out=cshift[:, e % 4, :], in0=cmv[:, e % 4, :, 0], scalar=-1.0,
                                         in1=crstd[:, e % 4, :], op0=ALU.mult, op1=ALU.mult).then_inc(tile_shift, 1)

            def tile_stats(e):
                dve.wait_ge(tile_in[e % 4], (e // 4 + 1) * 16)
                if e >= 4:
                    dve.wait_ge(tile_norm, (e - 3) * 2)
                    dve.wait_ge(tile_norm_act, (e - 3) * 2)
                for t in range(4):
                    dve.bn_stats(cstats[:, e % 4, t, :], ctile[:, e % 4, t, :]).then_inc(tile_st, 1)
                for t in range(4):
                    dve.wait_ge(tile_st, e * 4 + t + 1)
                    dve.bn_aggr(cmv[:, e % 4, t, :], cstats[:, e % 4, t, :]).then_inc(tile_ag, 1)

            dve.wait_ge(reversed_, TAU)
            k_terms = st_terms.rearrange("p m b a n -> p (m b a n)")[:, 0:512].rearrange("p (j h n) -> p j h n", h=2, n=NST)
            n_ = scan(dve.tensor_tensor(k_terms, kU[:, 0:TAU, :, :],
                                        kU[:, TAU:TAU + 1, :, :].rearrange("p j h n -> p (j h) n").unsqueeze(1)
                                        .broadcast_to([P, TAU, 2, NST]), ALU.mult))
            dve.wait_ge(conv, n_)
            n_ = scan(dve.tensor_reduce(K16, k_terms, AX.X, ALU.add))
            assert n_ == K_READY

            for m in range(DC):
                if m:
                    dve.wait_ge(conv, n_)
                n_ = scan(in_terms(dve, terms[0], m, 0))
                dve.wait_ge(conv, n_)
                n_ = scan(dve.tensor_reduce(ST[:, m, :, 0, :], terms[0], AX.X, ALU.add))
            for m in range(DC):
                dve.wait_ge(pool_terms, m + 1)
                n_ = scan(dve.tensor_reduce(ST[:, m, :, 1, :], terms[1 + m], AX.X, ALU.add))
            state = [n_] * DC
            for c in range(1, NBK):
                tile_stats(c - 1)
                if c >= 2:
                    tile_reciprocal(c - 2)
                if c < NBK - 1:
                    for m in range(DC):
                        dve.wait_ge(conv, state[m])
                        state[m] = scan(dve.tensor_tensor(
                            st_terms[:, m, :, :, :], kP[:, m, :, :].rearrange("p n a -> p a n").unsqueeze(1)
                            .broadcast_to([P, B, NST, NST]),
                            ST[:, m, c - 1, :, :].unsqueeze(2).broadcast_to([P, B, NST, NST]), ALU.mult))
                    for m in range(DC):
                        dve.wait_ge(conv, state[m])
                        state[m] = scan(dve.tensor_reduce(st_sums[:, m, :, :], st_terms[:, m, :, :, :], AX.X, ALU.add))
                    for m in range(DC):
                        dve.wait_ge(conv, state[m])
                        state[m] = scan(dve.tensor_tensor(ST[:, m, c, :, :], ST[:, m, c, :, :], st_sums[:, m, :, :],
                                                          ALU.add))
            tile_stats(NBK - 1)
            tile_reciprocal(NBK - 2)
            tile_reciprocal(NBK - 1)
            dve.wait_ge(conv, count[0])
            dve.sem_inc(states, 1)
            dve.wait_ge(tap_mm, DC * (TAU + 1))
            for m in range(DC):
                dve.tensor_copy(Y[:, m, :, 0:TAU], YP[m][:, :].rearrange("p (b k) -> p b k", b=B)[:, :, 0:TAU])\
                    .then_inc(y_done, 1)
            for i, (bb, m) in enumerate((bb, m) for bb in range(B) for m in range(DC)):
                if bb == 0:
                    if i:
                        dve.wait_ge(conv, n_)
                    n_ = scan(out_terms(dve, terms[0], m, 0))
                    dve.wait_ge(conv, n_)
                else:
                    dve.wait_ge(pool_terms, DC + m + 1)
                if i >= 2:
                    dve.wait_ge(y_done, DC + i - 1)
                n_ = scan(dve.tensor_reduce(y_sums[:, i % 2, :, :], terms[0 if bb == 0 else 1 + m], AX.X, ALU.add))
                dve.wait_ge(conv, n_)
                dve.tensor_tensor(blocks(Y[:, m, bb, :], 1, NBK), blocks(YP[m][:, bb * S:(bb + 1) * S], 1, NBK),
                                  y_sums[:, i % 2, :, :], ALU.add).then_inc(y_done, 1)
            dve.wait_ge(y_norm, NT4)
            dve.wait_ge(gate_w_in, 48)
            ln_dve(2, YT)
            for t in range(NT4):
                dve.wait_ge(ln_norm, NT4 * 2 + t + 1)
                dve.tensor_tensor(XN[:, t, :], XN[:, t, :], gamma_r, ALU.mult).then_inc(scan_done, 1)
                dve.wait_ge(scan_done, 3 * t + 1)
                dve.tensor_tensor(XN[:, t, :], XN[:, t, :], beta_r, ALU.add).then_inc(scan_done, 1)
                dve.wait_ge(scan_done, 3 * t + 2)
                dve.tensor_tensor(X[:, t, :], X[:, t, :], XN[:, t, :], ALU.add).then_inc(scan_done, 1)
            dve.wait_ge(scan_done, 3 * NT4)

            def gate_steps(Gt, iota, chain, logits, second):
                n = [0]

                def st(ins):
                    n[0] += 1
                    ins.then_inc(chain, 1)
                    dve.wait_ge(chain, n[0])

                def wide(v):
                    return v.broadcast_to([P, NT4, E8])

                def pick(src, hot, tmp, col):
                    mxv = Gt[:, col, :, 0:1]
                    st(dve.tensor_reduce(mxv, src, AX.X, ALU.max))
                    st(dve.tensor_tensor(tmp, src, wide(mxv), ALU.is_equal))
                    st(dve.tensor_tensor(tmp, tmp, iota.unsqueeze(1).broadcast_to([P, NT4, E8]), ALU.mult))
                    st(dve.tensor_reduce(Gt[:, col, :, 1:2], tmp, AX.X, ALU.min))
                    st(dve.tensor_tensor(hot, iota.unsqueeze(1).broadcast_to([P, NT4, E8]), wide(Gt[:, col, :, 1:2]),
                                         ALU.is_equal))
                    return mxv

                lg = Gt[:, 0, :, :]
                st(dve.tensor_copy(lg.rearrange("p t e -> p (t e)"), logits))
                m1 = pick(lg, Gt[:, 1, :, :], Gt[:, 2, :, :], 9)
                if not second:
                    return n[0]
                st(dve.tensor_scalar(Gt[:, 3, :, :], Gt[:, 1, :, :], NEG, None, ALU.mult))
                st(dve.tensor_tensor(Gt[:, 4, :, :], lg, Gt[:, 3, :, :], ALU.add))
                pick(Gt[:, 4, :, :], Gt[:, 5, :, :], Gt[:, 2, :, :], 10)
                st(dve.tensor_tensor(Gt[:, 6, :, :], Gt[:, 1, :, :], Gt[:, 5, :, :], ALU.add))
                st(dve.tensor_tensor(Gt[:, 7, :, :], lg, wide(m1), ALU.subtract))
                return n[0]

            def add_biases(added_, ready):
                dve.wait_ge(added_, NT4 * E8)
                for t in range(NT4):
                    dve.wait_ge(ready, t // 2 * 2 + 2)
                    dve.tensor_tensor(X[:, t, :], X[:, t, :], SP_[1 + t // 2][:, (t % 2) * D:(t % 2 + 1) * D], ALU.add)\
                        .then_inc(added_, 1)

            ln_dve(3, X)
            dve.wait_ge(moe_lg, NT4)
            n_ = gate_steps(G, iot, moe_g, OP[:, 0:NT4 * E8], True)
            assert n_ == MG_NEG, n_
            dve.wait_ge(moe_g, n_ + 1)
            dve.tensor_tensor(G[:, 2, :, :], G[:, 8, :, :], G[:, 6, :, :], ALU.mult).then_inc(moe_g, 1)
            dve.wait_ge(moe_g, n_ + 2)
            dve.tensor_reduce(G[:, 11, :, 0:1], G[:, 2, :, :], AX.X, ALU.add).then_inc(moe_g, 1)
            dve.wait_ge(moe_g, n_ + 3)
            dve.reciprocal(G[:, 11, :, 1:2], G[:, 11, :, 0:1]).then_inc(moe_g, 1)
            dve.wait_ge(moe_g, n_ + 4)
            dve.tensor_tensor(G[:, 12, :, :], G[:, 2, :, :], G[:, 11, :, 1:2].broadcast_to([P, NT4, E8]), ALU.mult)\
                .then_inc(moe_g, 1)
            dve.wait_ge(moe_g, n_ + 5)
            for n in range(NT4 * 4):
                t, e2 = n // 4, n % 4
                dve.wait_ge(moe_mm, n + 1)
                for ee in range(2):
                    if n + ee:
                        dve.wait_ge(moe_acc, 2 * n + ee)
                    dve.scalar_tensor_tensor(out=X[:, t, :], in0=RB[n % 4][:, ee * D:(ee + 1) * D],
                                             scalar=G[:, 12, t, 2 * e2 + ee:2 * e2 + ee + 1], in1=X[:, t, :],
                                             op0=ALU.mult, op1=ALU.add).then_inc(moe_acc, 1)
            add_biases(moe_acc, moe_b)
            dve.wait_ge(moe_acc, MOE_ADDS)
            ln_dve(4, X)
            dve.wait_ge(ln_norm, NT4 * 5)
            ln_dve(5, XN)
            dve.wait_ge(ln_turn, 4 * DC)
            def bank_c(u, n):
                return scoreC[:, u, 2 * n:2 * n + 2, :].rearrange("p k q -> p (k q)")

            def maxima(g, u):
                for n in range(1, NSB):
                    dve.wait_ge(c_kept, g * NSB + n + 1 + ONE)
                    dve.wait_ge(c_run, g * RUN + n - 1 + ONE)
                    dve.tensor_tensor(run_max, bank_c(u, 0) if n == 1 else run_max, bank_c(u, n), ALU.max)\
                        .then_inc(c_run, 1)
                dve.wait_ge(c_run, g * RUN + NSB - 1 + ONE)
                dve.tensor_tensor(half_max, run_max[:, 0:S], run_max[:, S:2 * S], ALU.max).then_inc(c_run, 1)

            def less_maximum(g, u):
                dve.wait_ge(c_turned, g + 1)
                dve.tensor_reduce(nmax[:, 0, :], TP[0][:, 0:S].rearrange("p (t k) -> p t k", t=QT), AX.X, ALU.max,
                                  negate=True).then_inc(c_max, 1)
                for k in range(NSG):
                    dve.wait_ge(c_spread, g + 1)
                    x = scoreC[:, u, 4 * k:min(4 * k + 4, NKC), :]
                    dve.tensor_tensor(x, x, TP[0][:, S:2 * S].unsqueeze(1).broadcast_to(list(x.shape)), ALU.add)\
                        .then_inc(c_sub, 1)

            def out_c(g, h):
                dve.wait_ge(c_sum, g + 1 + 2)
                dve.reciprocal(recip, TP[1][:, 0:S]).then_inc(c_recip, 1)
                dve.wait_ge(c_recip, g + 1)
                dve.wait_ge(c_weighed, g + 1)
                dve.tensor_tensor(OA[:, bass.ds(h, 1), :].rearrange("p a k -> p (a k)"), OP[:, 0:S], recip, ALU.mult)\
                    .then_inc(c_out, 1)

            def head_c(g, u, h, after=None):
                maxima(g, u)
                out_c(g - 1, h)
                if after is not None:
                    added(dve, after, after + B, SP_)
                less_maximum(g, u)

            maxima(0, 0)
            less_maximum(0, 0)
            head_c(1, 1, 0)
            for b in range(B):
                if b:
                    head_c(b * H, 0, H - 1, after=b - 1)
                    head_c(b * H + 1, 1, 0)
                with dve.Fori(1, 8) as p:
                    for u in range(2):
                        head_c(b * H + 2 * p + u, u, 2 * p + u - 1)
            out_c(B * H - 1, H - 1)
            added(dve, B - 1, 2 * B - 1, SP_)
            ln_dve(6, X)
            dve.wait_ge(sw_in, 7 * 16)
            for m in range(DC):
                dve.wait_ge(sq_mm, m + 1)
                dve.tensor_scalar(QTR[:, m, :], SP_[m][:, :], cols[:, C_SQ + m:C_SQ + m + 1], 0.25,
                                  ALU.add, ALU.mult).then_inc(sq_out, 1)
            def self_taken(n):
                t, h2 = divmod(n, H // 2)
                seen = (t % QT + 1) * P
                dve.wait_ge(s_mm, n + 1)
                dve.tensor_tensor(sS[:, t, 2 * h2:2 * h2 + 2, 0:seen],
                                  SP_[n % 3][:, :].rearrange("p (a k) -> p a k", a=2)[:, :, 0:seen],
                                  smask[:, t % QT, 0:seen].unsqueeze(1).broadcast_to([P, 2, seen]), ALU.add)\
                    .then_inc(s_ev, 1)
                if h2 == H // 2 - 1:
                    dve.wait_ge(s_ev, n + 1)
                    dve.tensor_reduce(smx[:, t, :], sS[:, t, :, 0:seen], AX.X, ALU.max, negate=True).then_inc(s_nm, 1)

            steps = NT4 * H // 2
            for n in range(H):
                self_taken(n)
            for n in range(steps):
                t, h2 = divmod(n, H // 2)
                nb = t % QT + 1
                if n + H < steps:
                    self_taken(n + H)
                dve.wait_ge(s_t, n + 1)
                if n >= 4:
                    dve.wait_ge(s_pv, n - 3)
                dve.tensor_copy(sPT[:, n % 4, 0:2 * nb * P], TP[n % 2][:, 0:2 * nb * P]).then_inc(s_tc, 1)
                if h2 == H // 2 - 1:
                    self_norm(dve, t)
            for t in range(NT4):
                dve.wait_ge(s_y, t + 1)
                dve.tensor_tensor(X[:, t, :], X[:, t, :], RB[t][:, 0:D], ALU.add).then_inc(s_x, 1)
            dve.wait_ge(s_x, NT4)
            ln_dve(7, X)
            dve.wait_ge(f_lg, NT4)
            n_ = gate_steps(G2, iot2, f_g, OP[:, 0:NT4 * E8], False)
            assert n_ == FG_HOT, n_
            for n in range(NT4 * E8):
                t, e = n % NT4, n // NT4
                dve.wait_ge(f_y, n + 1)
                if n >= NT4:
                    dve.wait_ge(f_acc, n - NT4 + 1)
                dve.scalar_tensor_tensor(out=X[:, t, :], in0=RB[n % 4][:, 0:D], scalar=G2[:, 1, t, e:e + 1],
                                         in1=X[:, t, :], op0=ALU.mult, op1=ALU.add).then_inc(f_acc, 1)
            add_biases(f_acc, f_b)


def kernel(**inputs):
    import numpy as np
    import concourse.bacc as bacc
    from concourse import mybir as mb
    from concourse.bass_utils import run_bass_kernel_spmd as run

    v = {k: np.asarray(x) for k, x in inputs.items()}

    def rows(w):
        return np.ascontiguousarray(w.reshape(2, 128, -1).transpose(1, 0, 2))

    def col(x):
        return x.reshape(-1, 128).T

    f = np.float32
    p = np.arange(128)
    order = np.arange(256).reshape(4, 4, 16).transpose(1, 0, 2).reshape(-1)
    twice = np.concatenate([np.arange(64), np.arange(64)])
    selA = np.zeros((128, 8, 128), f)
    for j in range(8):
        for d in range(16):
            selA[d::32, j, 16 * j + d] = 1
    h16 = np.arange(16)
    i, j = np.arange(256)[:, None], np.arange(256)[None, :]
    smask = np.where((i - 128 >= j) | (i < j), f(NEG), f(0)).astype(f).reshape(2, 128, 256).transpose(1, 0, 2)
    scan_a = v["L0_attn_A"].reshape(2, 128, 16, 16).transpose(1, 0, 2, 3)
    arrays = {
        "x": v["x"], "ctx": v["ctx_1024"], "ctxT": np.ascontiguousarray(v["ctx_1024"].transpose(0, 2, 1)),
        "mask": v["mask_BxSxS2_ik1"],
        "WqT": rows(v["L0_xattn_Wq"].T), "WkT": rows(v["L0_xattn_Wk"].T), "WvT": rows(v["L0_xattn_Wv"].T),
        "WoT": rows(v["L0_xattn_Wo"].T), "bo": v["L0_xattn_bo"][None, :],
        "cols": np.concatenate([col(v[n]) for n in (
            "L0_xattn_bq", "L0_xattn_bk", "L0_xattn_bv", "L0_attn_bg", "L0_attn_Dp", "L1_xattn_ln1_g",
            "L1_xattn_ln1_b", "L1_xattn_ln2_g", "L1_xattn_ln2_b")]
            + [col(v["L1_attn_bq"][order]), col(v["L1_attn_bk"][twice]), np.zeros((128, 1), f)], 1),
        "sel16": (p[:, None] // 16 == h16[None, :] % 8).astype(f),
        "sel64": (p[:, None] // 64 == np.arange(2)[None, :]).astype(f),
        "selA": selA, "hselA": (h16[:, None, None] == 8 * np.arange(2)[None, :, None] + p[None, None, :] // 16).astype(f),
        "A": scan_a, "AA": np.stack([scan_a.transpose(0, 1, 3, 2), scan_a]),
        "BC": np.stack([rows(v["L0_attn_Bp"]), rows(v["L0_attn_Cp"])]),
        "WgT": rows(v["L0_attn_Wg"].T),
        "gamma": np.broadcast_to(v["L0_attn_gamma"], (128, 256)), "beta": np.broadcast_to(v["L0_attn_beta"], (128, 256)),
        "ew": v["L0_ffn_expert_w"].reshape(8, 2, 128, 256).transpose(2, 1, 0, 3).reshape(128, 2, 2048),
        "eb": v["L0_ffn_expert_b"], "gwT": rows(v["L0_ffn_gate_w"].T), "gb": v["L0_ffn_gate_b"][None, :],
        "iota": np.broadcast_to(np.arange(8, dtype=f) - 8, (128, 8)),
        "WqC": v["L1_xattn_Wq"].reshape(2, 128, 8, 128).transpose(2, 1, 0, 3),
        "WkC": v["L1_xattn_Wkv"][:, :1024].reshape(2, 128, 8, 128).transpose(2, 1, 0, 3),
        "WvC": v["L1_xattn_Wkv"][:, 1024:].reshape(2, 128, 8, 128).transpose(2, 1, 0, 3),
        "WoC": np.concatenate([v["L1_xattn_Wo"].reshape(16, 64, 256).transpose(1, 0, 2)] * 2),
        "sWq": rows(v["L1_attn_Wq"][:, order]), "sWk": rows(v["L1_attn_Wk"][:, twice]), "sWv": rows(v["L1_attn_Wv"]),
        "sWo": rows(v["L1_attn_Wo"]), "sbv": v["L1_attn_bv"][None, :], "sbo": v["L1_attn_bo"][None, :], "smask": smask,
        "fWg": rows(v["L1_ffn_Wg"]), "fbg": v["L1_ffn_bg"][None, :],
        "W1": v["L1_ffn_W1"].reshape(8, 2, 128, 256).transpose(2, 1, 0, 3).reshape(128, 2, 2048),
        "fb1": v["L1_ffn_b1"].reshape(16, 128).T,
        "W2": v["L1_ffn_W2"].reshape(8, 2, 128, 256).transpose(2, 0, 1, 3), "b2": v["L1_ffn_b2"],
    }
    arrays = {k: np.ascontiguousarray(x) for k, x in arrays.items()}
    nc = bacc.Bacc("TRN2", target_bir_lowering=False, num_devices=1)
    aps = {k: nc.dram_tensor(k + "_dram", x.shape, mb.dt.from_np(x.dtype), kind="ExternalInput").ap()
           for k, x in arrays.items()}
    res = nc.dram_tensor("result_dram", (2, 256, 256), mb.dt.float32, kind="ExternalOutput").ap()
    program(nc, aps, res)
    r = run(nc, [{k + "_dram": x for k, x in arrays.items()}], core_ids=[0])
    return r.results[0]["result_dram"]
```
